# Optimizing a Trainium2 kernel written in Bass

```python
import numpy as np
import jax
import jax.numpy as jnp

def _softmax(x, axis=-1):
    return jax.nn.softmax(x, axis=axis)
def _gelu(x):
    return jax.nn.gelu(x, approximate=True)
def _silu(x):
    return jax.nn.silu(x)
def _sigmoid(x):
    return jax.nn.sigmoid(x)
def _layernorm(x, axis=-1, eps=1e-5):
    m = jnp.mean(x, axis=axis, keepdims=True)
    v = jnp.var(x, axis=axis, keepdims=True)
    return (x - m) / jnp.sqrt(v + eps)
def _scatter_add(tgt, idx, src, axis=0):
    return tgt.at[idx].add(src)
def _segment_sum(src, seg, n):
    return jax.ops.segment_sum(src, seg, n)

kernel_name = 'mk_conv_attn_hybrid_d4_conv_nhwc128_ade1cf'

def setup_inputs(seed: int = 0):
    np.random.seed(seed)
    _w = jnp.asarray
    def _rec_inputs():
        import jax
        import jax.numpy as jnp
        _gk = jax.random.key(seed)
        x = -0.000929 + 1 * jax.random.normal(jax.random.fold_in(_gk, 1), (2, 64, 64, 128), jnp.float32)
        return x
    x = _rec_inputs()
    def _L0_conv_setup():
        import jax, jax.numpy as jnp
        import numpy as np
        D_MODEL = 128
        D_STATE = 16
        D_INNER = 256
        DT_RANK = 8
        K = 4
        B, H, W = (2, 64, 64)

        def silu(x):
            return x * jax.nn.sigmoid(x)

        def selective_scan(xs, dts, As, Bs, Cs, Ds, dt_bias):
            delta = jax.nn.softplus(dts + dt_bias[None, :, :, None])
            d_l = jnp.moveaxis(delta, -1, 0)
            x_l = jnp.moveaxis(xs, -1, 0)
            B_l = jnp.moveaxis(Bs, -1, 0)
            C_l = jnp.moveaxis(Cs, -1, 0)

            def step(h, inp):
                d_t, x_t, B_t, C_t = inp
                dA = jnp.exp(d_t[..., None] * As)
                h = dA * h + (d_t * x_t)[..., None] * B_t[:, :, None, :]
                y = jnp.einsum('bkdn,bkn->bkd', h, C_t)
                return (h, y)
            h0 = jnp.zeros((xs.shape[0], K, As.shape[1], As.shape[2]), xs.dtype)
            _, ys = jax.lax.scan(step, h0, (d_l, x_l, B_l, C_l))
            ys = jnp.moveaxis(ys, 0, -1)
            return ys + Ds[None, :, :, None] * xs
        key = jax.random.key(seed)
        ks = jax.random.split(key, 8)
        f = lambda k, s, scale=0.02: jax.random.normal(k, s, dtype=jnp.float32) * scale
        A = jnp.tile(jnp.arange(1, D_STATE + 1, dtype=jnp.float32)[None, :], (K * D_INNER, 1))
        return {'x': jax.random.normal(ks[0], (B, H, W, D_MODEL), dtype=jnp.float32), 'w_in': f(ks[1], (2 * D_INNER, D_MODEL)), 'conv_w': f(ks[2], (D_INNER, 1, 3, 3)), 'conv_b': jnp.zeros((D_INNER,), jnp.float32), 'x_proj_w': f(ks[3], (K, DT_RANK + 2 * D_STATE, D_INNER)), 'dt_w': f(ks[4], (K, D_INNER, DT_RANK)), 'dt_b': f(ks[5], (K, D_INNER), 0.1), 'A_logs': jnp.log(A), 'Ds': jnp.ones((K * D_INNER,), jnp.float32), 'ln_w': jnp.ones((D_INNER,), jnp.float32), 'ln_b': jnp.zeros((D_INNER,), jnp.float32), 'w_out': f(ks[6], (D_MODEL, D_INNER))}
    _L0_conv_all = _L0_conv_setup()
    _L0_conv_in = {k: v for k, v in _L0_conv_all.items() if k in ('w_in', 'conv_w', 'conv_b', 'x_proj_w', 'dt_w', 'dt_b', 'A_logs', 'Ds', 'ln_w', 'ln_b', 'w_out', )}
    del _L0_conv_all

    def _L1_conv_setup():
        import jax, jax.numpy as jnp
        import numpy as np
        from jax import lax
        H = 128

        def _ema_scan(x):
            xt = jnp.moveaxis(x, 1, 0)

            def step(s, xi):
                s = s * 0.9 + xi * 0.1
                return (s, s)
            _, ys = lax.scan(step, jnp.zeros_like(xt[0]), xt)
            return jnp.moveaxis(ys, 0, 1)
        key = jax.random.key(seed)
        k1, k2, k3, k4, k5 = jax.random.split(key, 5)
        B, T, N = (4, 96, 512)
        x = jax.random.normal(k1, (B, T, N, H), dtype=jnp.float32)
        s = 1.0 / np.sqrt(H)
        W_exp = jax.random.uniform(k2, (2 * H, H), jnp.float32, -s, s)
        b_exp = jax.random.uniform(k3, (2 * H,), jnp.float32, -s, s)
        W_con = jax.random.uniform(k4, (H, H), jnp.float32, -s, s)
        b_con = jax.random.uniform(k5, (H,), jnp.float32, -s, s)
        return {'spatial_temporal_representation': x, 'W_exp': W_exp, 'b_exp': b_exp, 'W_con': W_con, 'b_con': b_con}
    _L1_conv_all = _L1_conv_setup()
    _L1_conv_in = {k: v for k, v in _L1_conv_all.items() if k in ('W_exp', 'b_exp', 'W_con', 'b_con', )}
    del _L1_conv_all

    def _L2_attn_setup():
        import jax, jax.numpy as jnp
        import numpy as np
        B, L, C, H = (8, 16384, 128, 4)
        EPS = 1e-05
        key = jax.random.key(seed)
        k1, k2, k3, k4 = jax.random.split(key, 4)
        return {'x': jax.random.normal(k1, (B, L, C), dtype=jnp.float32), 'W_qkv': jax.random.normal(k2, (3 * C, C), dtype=jnp.float32) * C ** (-0.5), 'W_out': jax.random.normal(k3, (C, C), dtype=jnp.float32) * C ** (-0.5), 'b_out': jax.random.normal(k4, (C,), dtype=jnp.float32) * 0.01, 'gn_w': jnp.ones((C,), dtype=jnp.float32), 'gn_b': jnp.zeros((C,), dtype=jnp.float32)}
    _L2_attn_all = _L2_attn_setup()
    _L2_attn_in = {k: v for k, v in _L2_attn_all.items() if k in ('W_qkv', 'W_out', 'b_out', 'gn_w', 'gn_b', )}
    del _L2_attn_all

    def _L2_ffn_setup():
        import jax, jax.numpy as jnp
        import numpy as np
        PADDED_SL = 8192
        TEMPERATURE = 1.0
        SIGMA_POW = 0.25

        def _stu_conv(phi, u, n):
            b, sl, d = u.shape
            sgn = jnp.where(jnp.arange(sl) % 2 == 0, 1.0, -1.0).astype(u.dtype)
            sgn3 = sgn[None, :, None]
            Vf = jnp.fft.rfft(phi, n=n, axis=0)
            Uf_p = jnp.fft.rfft(u, n=n, axis=1)
            Uf_m = jnp.fft.rfft(u * sgn3, n=n, axis=1)
            U_plus = jnp.fft.irfft(Vf[None, :, :, None] * Uf_p[:, :, None, :], n=n, axis=1)[:, :sl]
            U_minus = jnp.fft.irfft(Vf[None, :, :, None] * Uf_m[:, :, None, :], n=n, axis=1)[:, :sl]
            U_minus = U_minus * sgn[None, :, None, None]
            return (U_plus, U_minus)

        def _compute_spectral(u, sigma, phi, Mpp, Mpm):
            U_plus, U_minus = _stu_conv(phi, u, PADDED_SL)
            s = sigma ** SIGMA_POW
            out = jnp.einsum('btkd,k,kde->bte', U_plus, s, Mpp)
            out = out + jnp.einsum('btkd,k,kde->bte', U_minus, s, Mpm)
            return out

        def _compute_ar_u(Mu, u):
            sl = u.shape[1]
            out = jnp.zeros(u.shape[:2] + (Mu.shape[-1],), dtype=u.dtype)
            for i in range(Mu.shape[0]):
                ui = jnp.pad(u, ((0, 0), (i, 0), (0, 0)))[:, :sl]
                out = out + jnp.einsum('btd,de->bte', ui, Mu[i])
            return out

        def _stu(u, sigma, phi, Mu, Mpp, Mpm):
            return _compute_spectral(u, sigma, phi, Mpp, Mpm) + _compute_ar_u(Mu, u)
        key = jax.random.key(seed)
        ks = jax.random.split(key, 8)
        b, sl, d, K, k_u = (2, 4096, 128, 16, 3)
        x = jax.random.normal(ks[0], (b, sl, d), dtype=jnp.float32)
        sigma = jax.random.uniform(ks[1], (K,), dtype=jnp.float32, minval=0.001, maxval=1.0)
        phi = jax.random.normal(ks[2], (sl, K), dtype=jnp.float32) / np.sqrt(sl)
        M_u = jax.random.normal(ks[3], (4, k_u, d, d), dtype=jnp.float32) * 0.02
        M_phi_plus = jax.random.normal(ks[4], (4, K, d, d), dtype=jnp.float32) * 0.02
        M_phi_minus = jax.random.normal(ks[5], (4, K, d, d), dtype=jnp.float32) * 0.02
        log_weights = jnp.ones((4,), dtype=jnp.float32)
        u01 = jax.random.uniform(ks[6], (4,), dtype=jnp.float32, minval=1e-06, maxval=1.0 - 1e-06)
        gumbel = -jnp.log(-jnp.log(u01))
        return {'x': x, 'sigma': sigma, 'phi': phi, 'M_u': M_u, 'M_phi_plus': M_phi_plus, 'M_phi_minus': M_phi_minus, 'log_weights': log_weights, 'gumbel': gumbel}
    _L2_ffn_all = _L2_ffn_setup()
    _L2_ffn_in = {k: v for k, v in _L2_ffn_all.items() if k in ('sigma', 'phi', 'M_u', 'M_phi_plus', 'M_phi_minus', 'log_weights', 'gumbel', )}
    del _L2_ffn_all

    def _L3_attn_setup():
        import jax, jax.numpy as jnp
        import numpy as np
        B, S, H, A = (8, 1024, 128, 16)
        key = jax.random.key(seed)
        ks = jax.random.split(key, 5)
        scale = 1.0 / np.sqrt(2 * H)
        return {'x': jax.random.normal(ks[0], (B, S, H), dtype=jnp.float32), 'W1': jax.random.normal(ks[1], (2 * H, A), dtype=jnp.float32) * scale, 'b1': jax.random.normal(ks[2], (A,), dtype=jnp.float32) * scale, 'w2': jax.random.normal(ks[3], (A, 1), dtype=jnp.float32) * (1.0 / np.sqrt(A)), 'b2': jax.random.normal(ks[4], (1,), dtype=jnp.float32) * (1.0 / np.sqrt(A))}
    _L3_attn_all = _L3_attn_setup()
    _L3_attn_in = {k: v for k, v in _L3_attn_all.items() if k in ('W1', 'b1', 'w2', 'b2', )}
    del _L3_attn_all

    def _L3_ffn_setup():
        import jax, jax.numpy as jnp
        import numpy as np
        B, N, D, C, E, K = (8, 8192, 128, 128, 8, 2)
        key = jax.random.key(seed)
        k0, k1, k2 = jax.random.split(key, 3)
        x = jax.random.normal(k0, (B, N, D), dtype=jnp.float32)
        router_w = jax.random.normal(k1, (D, E), dtype=jnp.float32) * 0.05
        router_b = jnp.zeros((E,), dtype=jnp.float32)
        expert_w = jax.random.normal(k2, (E, D, C), dtype=jnp.float32) * (1.0 / np.sqrt(D))
        expert_b = jnp.zeros((E, C), dtype=jnp.float32)
        return {'x': x, 'router_w': router_w, 'router_b': router_b, 'expert_w': expert_w, 'expert_b': expert_b}
    _L3_ffn_all = _L3_ffn_setup()
    _L3_ffn_in = {k: v for k, v in _L3_ffn_all.items() if k in ('router_w', 'router_b', 'expert_w', 'expert_b', )}
    del _L3_ffn_all

    return {
        "x": x,
        "L0_conv_w_in": _L0_conv_in["w_in"],
        "L0_conv_conv_w": _L0_conv_in["conv_w"],
        "L0_conv_conv_b": _L0_conv_in["conv_b"],
        "L0_conv_x_proj_w": _L0_conv_in["x_proj_w"],
        "L0_conv_dt_w": _L0_conv_in["dt_w"],
        "L0_conv_dt_b": _L0_conv_in["dt_b"],
        "L0_conv_A_logs": _L0_conv_in["A_logs"],
        "L0_conv_Ds": _L0_conv_in["Ds"],
        "L0_conv_ln_w": _L0_conv_in["ln_w"],
        "L0_conv_ln_b": _L0_conv_in["ln_b"],
        "L0_conv_w_out": _L0_conv_in["w_out"],
        "L1_conv_W_exp": _L1_conv_in["W_exp"],
        "L1_conv_b_exp": _L1_conv_in["b_exp"],
        "L1_conv_W_con": _L1_conv_in["W_con"],
        "L1_conv_b_con": _L1_conv_in["b_con"],
        "L2_attn_W_qkv": _L2_attn_in["W_qkv"],
        "L2_attn_W_out": _L2_attn_in["W_out"],
        "L2_attn_b_out": _L2_attn_in["b_out"],
        "L2_attn_gn_w": _L2_attn_in["gn_w"],
        "L2_attn_gn_b": _L2_attn_in["gn_b"],
        "L2_ffn_sigma": _L2_ffn_in["sigma"],
        "L2_ffn_phi": _L2_ffn_in["phi"],
        "L2_ffn_M_u": _L2_ffn_in["M_u"],
        "L2_ffn_M_phi_plus": _L2_ffn_in["M_phi_plus"],
        "L2_ffn_M_phi_minus": _L2_ffn_in["M_phi_minus"],
        "L2_ffn_log_weights": _L2_ffn_in["log_weights"],
        "L2_ffn_gumbel": _L2_ffn_in["gumbel"],
        "L3_attn_W1": _L3_attn_in["W1"],
        "L3_attn_b1": _L3_attn_in["b1"],
        "L3_attn_w2": _L3_attn_in["w2"],
        "L3_attn_b2": _L3_attn_in["b2"],
        "L3_ffn_router_w": _L3_ffn_in["router_w"],
        "L3_ffn_router_b": _L3_ffn_in["router_b"],
        "L3_ffn_expert_w": _L3_ffn_in["expert_w"],
        "L3_ffn_expert_b": _L3_ffn_in["expert_b"],
    }

def reference(x, L0_conv_w_in, L0_conv_conv_w, L0_conv_conv_b, L0_conv_x_proj_w, L0_conv_dt_w, L0_conv_dt_b, L0_conv_A_logs, L0_conv_Ds, L0_conv_ln_w, L0_conv_ln_b, L0_conv_w_out, L1_conv_W_exp, L1_conv_b_exp, L1_conv_W_con, L1_conv_b_con, L2_attn_W_qkv, L2_attn_W_out, L2_attn_b_out, L2_attn_gn_w, L2_attn_gn_b, L2_ffn_sigma, L2_ffn_phi, L2_ffn_M_u, L2_ffn_M_phi_plus, L2_ffn_M_phi_minus, L2_ffn_log_weights, L2_ffn_gumbel, L3_attn_W1, L3_attn_b1, L3_attn_w2, L3_attn_b2, L3_ffn_router_w, L3_ffn_router_b, L3_ffn_expert_w, L3_ffn_expert_b):
    import jax
    import jax.numpy as jnp
    def _L0_conv_ref(x, w_in, conv_w, conv_b, x_proj_w, dt_w, dt_b, A_logs, Ds, ln_w, ln_b, w_out):
        import jax, jax.numpy as jnp
        import numpy as np
        D_MODEL = 128
        D_STATE = 16
        D_INNER = 256
        DT_RANK = 8
        K = 4
        B, H, W = (2, 64, 64)

        def silu(x):
            return x * jax.nn.sigmoid(x)

        def selective_scan(xs, dts, As, Bs, Cs, Ds, dt_bias):
            delta = jax.nn.softplus(dts + dt_bias[None, :, :, None])
            d_l = jnp.moveaxis(delta, -1, 0)
            x_l = jnp.moveaxis(xs, -1, 0)
            B_l = jnp.moveaxis(Bs, -1, 0)
            C_l = jnp.moveaxis(Cs, -1, 0)

            def step(h, inp):
                d_t, x_t, B_t, C_t = inp
                dA = jnp.exp(d_t[..., None] * As)
                h = dA * h + (d_t * x_t)[..., None] * B_t[:, :, None, :]
                y = jnp.einsum('bkdn,bkn->bkd', h, C_t)
                return (h, y)
            h0 = jnp.zeros((xs.shape[0], K, As.shape[1], As.shape[2]), xs.dtype)
            _, ys = jax.lax.scan(step, h0, (d_l, x_l, B_l, C_l))
            ys = jnp.moveaxis(ys, 0, -1)
            return ys + Ds[None, :, :, None] * xs
        xz = x @ w_in.T
        xi, z = jnp.split(xz, 2, axis=-1)
        z = silu(z)
        xc = jnp.transpose(xi, (0, 3, 1, 2))
        xc = jax.lax.conv_general_dilated(xc, conv_w, (1, 1), 'SAME', feature_group_count=D_INNER, dimension_numbers=('NCHW', 'OIHW', 'NCHW')) + conv_b[None, :, None, None]
        xc = silu(xc)
        b, d, h, w = xc.shape
        L = h * w
        x_flat = xc.reshape(b, d, L)
        x_t = jnp.transpose(xc, (0, 1, 3, 2)).reshape(b, d, L)
        x_hwwh = jnp.stack([x_flat, x_t], axis=1)
        xs = jnp.concatenate([x_hwwh, jnp.flip(x_hwwh, axis=-1)], axis=1)
        x_dbl = jnp.einsum('bkdl,kcd->bkcl', xs, x_proj_w)
        dts, Bs, Cs = jnp.split(x_dbl, [DT_RANK, DT_RANK + D_STATE], axis=2)
        dts = jnp.einsum('bkrl,kdr->bkdl', dts, dt_w)
        As = -jnp.exp(A_logs).reshape(K, d, D_STATE)
        out_y = selective_scan(xs, dts, As, Bs, Cs, Ds.reshape(K, d), dt_b)
        inv_y = jnp.flip(out_y[:, 2:4], axis=-1)
        wh_y = jnp.transpose(out_y[:, 1].reshape(b, d, w, h), (0, 1, 3, 2)).reshape(b, d, L)
        invwh_y = jnp.transpose(inv_y[:, 1].reshape(b, d, w, h), (0, 1, 3, 2)).reshape(b, d, L)
        y = out_y[:, 0] + inv_y[:, 0] + wh_y + invwh_y
        y = jnp.transpose(y, (0, 2, 1))
        mu = y.mean(-1, keepdims=True)
        var = ((y - mu) ** 2).mean(-1, keepdims=True)
        y = (y - mu) / jnp.sqrt(var + 1e-05) * ln_w + ln_b
        y = y.reshape(b, h, w, d) * z
        return y @ w_out.T

    def _L1_conv_ref(spatial_temporal_representation, W_exp, b_exp, W_con, b_con):
        import jax, jax.numpy as jnp
        import numpy as np
        from jax import lax
        H = 128

        def _ema_scan(x):
            xt = jnp.moveaxis(x, 1, 0)

            def step(s, xi):
                s = s * 0.9 + xi * 0.1
                return (s, s)
            _, ys = lax.scan(step, jnp.zeros_like(xt[0]), xt)
            return jnp.moveaxis(ys, 0, 1)
        x = spatial_temporal_representation
        expanded = jnp.einsum('btnh,oh->btno', x, W_exp) + b_exp
        state_primary, state_gating = jnp.split(expanded, 2, axis=-1)
        gated_activation = jax.nn.sigmoid(_ema_scan(state_gating))
        out = jnp.einsum('btnh,oh->btno', state_primary * gated_activation, W_con) + b_con
        return out

    def _L2_attn_ref(x, W_qkv, W_out, b_out, gn_w, gn_b):
        import jax, jax.numpy as jnp
        import numpy as np
        B, L, C, H = (8, 16384, 128, 4)
        EPS = 1e-05
        b, l, c = x.shape
        h = H
        d = c // h
        scale = d ** (-0.5)
        xc = jnp.swapaxes(x, 1, 2)
        qkv = jnp.einsum('oc,bcl->bol', W_qkv, xc)
        q, k, v = jnp.split(qkv, 3, axis=1)
        q = q.reshape(b, h, d, l)
        k = k.reshape(b, h, d, l)
        v = v.reshape(b, h, d, l)
        q = jax.nn.softmax(q, axis=2) * scale
        k = jax.nn.softmax(k, axis=3)
        context = jnp.einsum('bhcj,bhdj->bhcd', k, v)
        out = jnp.einsum('bhcd,bhdi->bhci', context, q)
        out = out.reshape(b, h * d, l)
        out = jnp.einsum('oc,bcl->bol', W_out, out) + b_out[None, :, None]
        mean = jnp.mean(out, axis=(1, 2), keepdims=True)
        var = jnp.var(out, axis=(1, 2), keepdims=True)
        out = (out - mean) * jax.lax.rsqrt(var + EPS)
        out = out * gn_w[None, :, None] + gn_b[None, :, None]
        return jnp.swapaxes(out, 1, 2)

    def _L2_ffn_ref(x, sigma, phi, M_u, M_phi_plus, M_phi_minus, log_weights, gumbel):
        import jax, jax.numpy as jnp
        import numpy as np
        PADDED_SL = 8192
        TEMPERATURE = 1.0
        SIGMA_POW = 0.25

        def _stu_conv(phi, u, n):
            b, sl, d = u.shape
            sgn = jnp.where(jnp.arange(sl) % 2 == 0, 1.0, -1.0).astype(u.dtype)
            sgn3 = sgn[None, :, None]
            Vf = jnp.fft.rfft(phi, n=n, axis=0)
            Uf_p = jnp.fft.rfft(u, n=n, axis=1)
            Uf_m = jnp.fft.rfft(u * sgn3, n=n, axis=1)
            U_plus = jnp.fft.irfft(Vf[None, :, :, None] * Uf_p[:, :, None, :], n=n, axis=1)[:, :sl]
            U_minus = jnp.fft.irfft(Vf[None, :, :, None] * Uf_m[:, :, None, :], n=n, axis=1)[:, :sl]
            U_minus = U_minus * sgn[None, :, None, None]
            return (U_plus, U_minus)

        def _compute_spectral(u, sigma, phi, Mpp, Mpm):
            U_plus, U_minus = _stu_conv(phi, u, PADDED_SL)
            s = sigma ** SIGMA_POW
            out = jnp.einsum('btkd,k,kde->bte', U_plus, s, Mpp)
            out = out + jnp.einsum('btkd,k,kde->bte', U_minus, s, Mpm)
            return out

        def _compute_ar_u(Mu, u):
            sl = u.shape[1]
            out = jnp.zeros(u.shape[:2] + (Mu.shape[-1],), dtype=u.dtype)
            for i in range(Mu.shape[0]):
                ui = jnp.pad(u, ((0, 0), (i, 0), (0, 0)))[:, :sl]
                out = out + jnp.einsum('btd,de->bte', ui, Mu[i])
            return out

        def _stu(u, sigma, phi, Mu, Mpp, Mpm):
            return _compute_spectral(u, sigma, phi, Mpp, Mpm) + _compute_ar_u(Mu, u)
        T = x.shape[1]
        outs = []
        for i, frac in enumerate((1, 2, 4, 8)):
            xi = x[:, :T // frac]
            si = _stu(xi, sigma, phi, M_u[i], M_phi_plus[i], M_phi_minus[i])
            si = jnp.pad(si, ((0, 0), (0, T - si.shape[1]), (0, 0)))
            outs.append(si)
        y_soft = jax.nn.softmax((log_weights + gumbel) / TEMPERATURE)
        y_hard = jax.nn.one_hot(jnp.argmax(y_soft), 4, dtype=y_soft.dtype)
        weights = y_hard - jax.lax.stop_gradient(y_soft) + y_soft
        stacked = jnp.stack(outs, axis=-1)
        return jnp.sum(stacked * weights, axis=-1)

    def _L3_attn_ref(x, W1, b1, w2, b2):
        import jax, jax.numpy as jnp
        import numpy as np
        B, S, H, A = (8, 1024, 128, 16)
        h = x.shape[-1]
        f = jnp.einsum('bih,ha->bia', x, W1[:h])
        g = jnp.einsum('bjh,ha->bja', x, W1[h:])
        t = jnp.tanh(f[:, :, None, :] + g[:, None, :, :] + b1)
        scores = jnp.einsum('bija,a->bij', t, w2[:, 0]) + b2[0]
        n_seq = x.shape[1]
        flag = jnp.tril(jnp.ones((n_seq, n_seq), dtype=x.dtype), -1)[None, :, :]
        e = jnp.exp(scores) * flag
        denom = jnp.sum(e, axis=-1, keepdims=True) + 1e-10
        w = e / denom
        return jnp.einsum('bij,bjh->bih', w, x)

    def _L3_ffn_ref(x, router_w, router_b, expert_w, expert_b):
        import jax, jax.numpy as jnp
        import numpy as np
        B, N, D, C, E, K = (8, 8192, 128, 128, 8, 2)
        router_probs = jax.nn.softmax(x @ router_w + router_b, axis=-1)
        top_p, top_i = jax.lax.top_k(router_probs, K)
        top_p = top_p / jnp.sum(top_p, axis=-1, keepdims=True)
        expert_out = jnp.einsum('bnd,edc->bnec', x, expert_w) + expert_b
        gathered = jnp.take_along_axis(expert_out, top_i[..., None], axis=2)
        return jnp.einsum('bnk,bnkc->bnc', top_p, gathered)

    def _gn(v, G=32, eps=1e-5):
        B_, H_, W_, C_ = v.shape
        g = v.reshape(B_, H_, W_, G, C_ // G)
        m = jnp.mean(g, axis=(1, 2, 4), keepdims=True)
        s = jnp.var(g, axis=(1, 2, 4), keepdims=True)
        return ((g - m) / jnp.sqrt(s + eps)).reshape(v.shape)

    def _ln_c(v, eps=1e-6):
        m = jnp.mean(v, axis=-1, keepdims=True)
        s = jnp.var(v, axis=-1, keepdims=True)
        return (v - m) / jnp.sqrt(s + eps)

    def _ln_t(v, eps=1e-5):
        m = jnp.mean(v, axis=-1, keepdims=True)
        s = jnp.var(v, axis=-1, keepdims=True)
        return (v - m) / jnp.sqrt(s + eps)

    def _to_tokens(v):
        B_, H_, W_, C_ = v.shape
        return v.reshape(B_, H_ * W_, C_)
    def _from_tokens(t, like):
        return t.reshape(like.shape)

    x = x + _L0_conv_ref(_gn(x), L0_conv_w_in, L0_conv_conv_w, L0_conv_conv_b, L0_conv_x_proj_w, L0_conv_dt_w, L0_conv_dt_b, L0_conv_A_logs, L0_conv_Ds, L0_conv_ln_w, L0_conv_ln_b, L0_conv_w_out)
    x = x + _L1_conv_ref(_gn(x), L1_conv_W_exp, L1_conv_b_exp, L1_conv_W_con, L1_conv_b_con)
    t = _to_tokens(x)
    t = t + _L2_attn_ref(_ln_t(t), L2_attn_W_qkv, L2_attn_W_out, L2_attn_b_out, L2_attn_gn_w, L2_attn_gn_b)
    t = t + _L2_ffn_ref(_ln_t(t), L2_ffn_sigma, L2_ffn_phi, L2_ffn_M_u, L2_ffn_M_phi_plus, L2_ffn_M_phi_minus, L2_ffn_log_weights, L2_ffn_gumbel)
    t = t + _L3_attn_ref(_ln_t(t), L3_attn_W1, L3_attn_b1, L3_attn_w2, L3_attn_b2)
    t = t + _L3_ffn_ref(_ln_t(t), L3_ffn_router_w, L3_ffn_router_b, L3_ffn_expert_w, L3_ffn_expert_b)
    x = _from_tokens(t, x)
    return x


_drawn_inputs = setup_inputs


def setup_inputs(seed=0):
    import zlib

    import numpy as np

    out = dict(_drawn_inputs(seed))
    spreads = {'L0_conv_conv_b': (0.0, 0.1),
     'L0_conv_Ds': (1.0, 0.6),
     'L0_conv_ln_w': (1.0, 0.2),
     'L0_conv_ln_b': (0.0, 0.369),
     'L2_attn_gn_w': (1.0, 0.2),
     'L2_attn_gn_b': (0.0, 0.1),
     'L2_ffn_log_weights': (1.0, 0.2),
     'L3_ffn_router_b': (0.0, 0.1),
     'L3_ffn_expert_b': (0.0, 0.1)}
    factors = {'L0_conv_x_proj_w': 64.0,
     'L0_conv_dt_w': 64.0,
     'L0_conv_dt_b': 64.0,
     'L0_conv_A_logs': 64.0,
     'L3_attn_b1': 22.814}
    for name, (base, spread) in spreads.items():
        noise = np.random.default_rng([zlib.crc32(name.encode()), seed]).standard_normal(out[name].shape)
        drawn = base * np.exp(spread * noise) if base else spread * noise
        out[name] = jnp.asarray(drawn.astype(out[name].dtype))
    for name, factor in factors.items():
        out[name] = (out[name] * factor).astype(out[name].dtype)
    return out
```

```python
from contextlib import ExitStack

import concourse.bass as bass
from concourse import mybir

F32 = mybir.dt.float32
BF16 = mybir.dt.bfloat16
ACT = mybir.ActivationFunctionType
ALU = mybir.AluOpType
AX_X = mybir.AxisListType.X

P = 128
B = 2
HH = WW = 64
L = HH * WW
N = B * L
CH = 512
NC = N // CH
CB = L // CH
ROWS = CH // WW
PAD = WW + 2
FREE = 2
KD = 4
NS = 16
LN_SET = "natural_log_exp_and_others"


def halves(ap, n):
    a = [list(x) for x in ap.ap]
    return bass.AP(tensor=ap.tensor, offset=ap.offset, ap=[a[0], [0, n]] + a[1:])


def inside(ap, n):
    return bass.AP(tensor=ap.tensor, offset=ap.offset, ap=[list(x) for x in ap.ap] + [[0, n]])


class Place:

    def __init__(self, nc, ctx):
        self.nc, self.ctx, self.sems = nc, ctx, []
        ctx.callback(self.clear)

    def sb(self, name, shape, dt=F32):
        return self.ctx.enter_context(self.nc.sbuf_tensor(name, shape, dt))

    def ps(self, name, shape, dt=F32):
        return self.ctx.enter_context(self.nc.psum_tensor(name, shape, dt))

    def sem(self, name):
        self.sems.append(self.nc.alloc_semaphore(name))
        return self.sems[-1]

    def clear(self):
        if self.sems:
            with self.nc.Block() as block:
                @block.gpsimd
                def _(pool):
                    for s in self.sems:
                        pool.sem_clear(s)
            for s in self.sems:
                self.nc.release_semaphore(s)


class Steps:

    def __init__(self, eng, sem, base=0):
        self.eng, self.sem, self.base, self.n = eng, sem, base, 0

    def __call__(self, ins):
        self.n += 1
        ins.then_inc(self.sem, 1)
        self.eng.wait_ge(self.sem, self.base + self.n)


def load_residual(nc, xt, x_cm, name):
    with ExitStack() as ctx:
        p = Place(nc, ctx)
        x_loaded = p.sem(name + "_x_loaded")
        with nc.Block() as block:
            @block.sync
            def _(sp):
                for q in range(4):
                    w = N // 4
                    sp.dma_start(xt[:, q * w:(q + 1) * w], x_cm[:, q * w:(q + 1) * w]).then_inc(x_loaded, 16)
                sp.wait_ge(x_loaded, 64)


def group_stats(nc, xt, cm, gscale, gshift, name):
    with ExitStack() as ctx:
        p = Place(nc, ctx)
        stats = p.sb(name + "_stats", [P, NC, 6])
        mv = p.sb(name + "_mv", [P, B, 2])
        ex = p.sb(name + "_ex", [P, B, 2])
        g = p.sb(name + "_g", [P, B, 2])
        var = p.sb(name + "_var", [P, B])
        std = p.sb(name + "_std", [P, B])
        pg = p.ps(name + "_pg", [P, CH])
        stats_ready = p.sem(name + "_stats_ready")
        step = p.sem(name + "_step")
        moments_ready = p.sem(name + "_moments_ready")
        group_ready = p.sem(name + "_group_ready")
        var_ready = p.sem(name + "_var_ready")
        std_ready = p.sem(name + "_std_ready")
        with nc.Block() as block:
            @block.vector
            def _(dve):
                with dve.Fori(0, NC) as i:
                    dve.bn_stats(stats[:, bass.ds(i, 1), :].rearrange("p a s -> p (a s)"),
                                 xt[:, bass.ds(i * CH, CH)]).then_inc(stats_ready, 1)
                dve.wait_ge(stats_ready, NC)
                link = Steps(dve, step)
                for b in range(B):
                    link(dve.bn_aggr(mv[:, b, :], stats[:, b * CB:(b + 1) * CB, :].rearrange("p a s -> p (a s)")))
                link(dve.tensor_tensor(ex[:, :, 1], mv[:, :, 0], mv[:, :, 0], ALU.mult))
                link(dve.tensor_copy(ex[:, :, 0], mv[:, :, 0]))
                dve.tensor_tensor(ex[:, :, 1], ex[:, :, 1], mv[:, :, 1], ALU.add).then_inc(moments_ready, 1)
                dve.wait_ge(group_ready, 1)
                link(dve.tensor_copy(g[:, :, :].rearrange("p b s -> p (b s)"), pg[:, 0:2 * B]))
                link(dve.tensor_tensor(var[:, :], g[:, :, 0], g[:, :, 0], ALU.mult))
                dve.tensor_tensor(var[:, :], g[:, :, 1], var[:, :], ALU.subtract).then_inc(var_ready, 1)
                dve.wait_ge(std_ready, 1)
                link(dve.reciprocal(gscale[:, :], std[:, :]))
                link(dve.scalar_tensor_tensor(gshift[:, :], g[:, :, 0], -1.0, gscale[:, :], ALU.mult, ALU.mult))

            @block.tensor
            def _(pe):
                pe.wait_ge(moments_ready, 1)
                pe.matmul(pg[:, 0:2 * B], cm("gmat"), ex[:, :, :].rearrange("p b s -> p (b s)"),
                          start=True, stop=True).then_inc(group_ready, 1)

            @block.scalar
            def _(act):
                act.wait_ge(var_ready, 1)
                act.activation(std[:, :], var[:, :], ACT.Sqrt, bias=cm("eps")).then_inc(std_ready, 1)


def conv_branch(nc, xt, cm, wa, gscale, gshift, xc):
    with ExitStack() as ctx:
        p = Place(nc, ctx)
        pad = p.sb("xi_pad", [P, B, PAD, PAD])
        diag = p.sb("conv_diag", [P, 2, 9, P])
        psx = [p.ps(f"psx{s}", [P, CH]) for s in range(2)]
        psc = [p.ps(f"psc{s}", [P, CH]) for s in range(2)]
        pad_zeroed = p.sem("pad_zeroed")
        diag_ready = p.sem("diag_ready")
        xn_ready = p.sem("xn_ready")
        xi_ready = p.sem("xi_ready")
        xi_padded = p.sem("xi_padded")
        conv_ready = p.sem("conv_ready")
        xc_ready = p.sem("xc_ready")
        with nc.Block() as block:
            @block.gpsimd
            def _(pool):
                pool.memset(pad[:, :, :, :], 0.0).then_inc(pad_zeroed, 1)

            @block.vector
            def _(dve):
                for b in range(B):
                    with dve.Fori(0, CB) as c:
                        x = xt[:, bass.ds(c * CH + b * L, CH)]
                        dve.tensor_scalar(x, x, gscale[:, b:b + 1], gshift[:, b:b + 1],
                                          ALU.mult, ALU.add).then_inc(xn_ready, 1)
                for half in range(2):
                    for tap in range(9):
                        dve.tensor_scalar(diag[:, half, tap, :], cm("ident"), wa("conv_w", 9 * half + tap), None,
                                          ALU.mult).then_inc(diag_ready, 1)
                dve.wait_ge(pad_zeroed, 1)
                for half in range(2):
                    for b in range(B):
                        if half == 1:
                            dve.wait_ge(conv_ready, (b + 1) * CB)
                        with dve.Fori(0, CB // 2) as i:
                            for s in range(2):
                                c = 2 * i + s
                                dve.wait_ge(xi_ready, c + (half * NC + b * CB + 1))
                                dve.tensor_copy(pad[:, b, bass.ds(c * ROWS + 1, ROWS), 1:1 + WW],
                                                psx[s][:, :].rearrange("p (h w) -> p h w", w=WW)).then_inc(xi_padded, 1)

            @block.tensor
            def _(pe):
                pe.sem_inc(xi_padded, FREE)
                pe.sem_inc(xc_ready, FREE)
                for half in range(2):
                    with pe.Fori(0, NC // 2) as i:
                        for s in range(2):
                            t = 2 * i + s
                            if half == 0:
                                pe.wait_ge(xn_ready, t + 1)
                            pe.wait_ge(xi_padded, t + (half * NC + 1))
                            pe.matmul(psx[s][:, :], wa("win", half * P, P), xt[:, bass.ds(t * CH, CH)],
                                      start=True, stop=True).then_inc(xi_ready, 1)
                    pe.wait_ge(diag_ready, 18)
                    for b in range(B):
                        pe.wait_ge(xi_padded, FREE + half * NC + (b + 1) * CB)
                        with pe.Fori(0, CB // 2) as i:
                            for s in range(2):
                                c = 2 * i + s
                                pe.wait_ge(xc_ready, c + (half * NC + b * CB + 1))
                                for tap in range(9):
                                    dy, dx = divmod(tap, 3)
                                    mm = pe.matmul(psc[s][:, :], diag[:, half, tap, :],
                                                   pad[:, b, bass.ds(c * ROWS + dy, ROWS), dx:dx + WW],
                                                   start=(tap == 0), stop=(tap == 8))
                                mm.then_inc(conv_ready, 1)

            @block.scalar
            def _(act):
                act.preload_act_table(ACT.Silu)
                for half in range(2):
                    with act.Fori(0, NC // 2) as i:
                        for s in range(2):
                            t = 2 * i + s
                            act.wait_ge(conv_ready, t + (half * NC + 1))
                            act.activation(xc[:, half].rearrange("p b h w -> p (b h w)")[:, bass.ds(t * CH, CH)],
                                           psc[s][:, :], ACT.Silu, bias=wa("conv_b", half)).then_inc(xc_ready, 1)


def selective_scan(nc, cm, wa, sel, xproj, dtw, xc, y):
    with ExitStack() as ctx:
        p = Place(nc, ctx)
        neg_a = p.sb("neg_a", [P, KD, 2, NS])
        d_sum = p.sb("d_sum", [P, 2])
        split = p.sb("bc_split", [96, CH], BF16)
        mid = p.sb("bc_mid", [96, CH], BF16)
        rest = p.sb("bc_rest", [96, CH])
        dts = p.sb("dts", [P, CH])
        e = p.sb("e", [P, 2, CH])
        ln = p.sb("ln", [P, 2, CH])
        r = p.sb("r", [P, 2, CH])
        delta = p.sb("delta", [P, 2, CH])
        u = p.sb("u", [P, 2, CH])
        c_sb = [p.sb(f"c_sb{s}", [P, CH]) for s in range(2)]
        da = [p.sb(f"da{s}", [P, 2, CH]) for s in range(2)]
        dbx = [p.sb(f"dbx{s}", [P, 2, CH]) for s in range(2)]
        h = [p.sb(f"h{s}", [P, 2, CH]) for s in range(2)]
        state = p.sb("state", [P, 2, NS])
        ps_xd = p.ps("ps_xd", [P, CH])
        ps_dt = p.ps("ps_dt", [P, 2, CH])
        ps_b = [p.ps(f"ps_b{s}", [P, CH]) for s in range(2)]
        ps_c = p.ps("ps_c", [P, CH])
        ps_y = p.ps("ps_y", [P, 2, CH])
        a_clamped = p.sem("a_clamped")
        d_ready = p.sem("d_ready")
        a_exp = p.sem("a_exp")
        a_ready = p.sem("a_ready")
        y_started = p.sem("y_started")
        xd_ready = p.sem("xd_ready")
        hi_ready = p.sem("hi_ready")
        dts_ready = p.sem("dts_ready")
        rest_ready = p.sem("rest_ready")
        mid_ready = p.sem("mid_ready")
        split_ready = p.sem("split_ready")
        dt_ready = p.sem("dt_ready")
        xm_ready = p.sem("xm_ready")
        e_ready = p.sem("e_ready")
        ln_ready = p.sem("ln_ready")
        soft_step = p.sem("soft_step")
        delta_ready = p.sem("delta_ready")
        u_ready = p.sem("u_ready")
        b_ready = p.sem("b_ready")
        c_ready = p.sem("c_ready")
        c_copied = p.sem("c_copied")
        da_ready = p.sem("da_ready")
        dbx_ready = p.sem("dbx_ready")
        scanned = p.sem("scanned")
        state_reset = p.sem("state_reset")
        state_saved = p.sem("state_saved")
        hc_ready = p.sem("hc_ready")
        y_summed = p.sem("y_summed")
        y_added = p.sem("y_added")
        SOFT = 5

        def piece(t_x, k, b, c, half=None):
            some = bass.ds(c * ROWS, ROWS)
            if half is not None:
                v = t_x[:, half, bass.ds(b, 1), some, :] if k % 2 == 0 else t_x[:, half, bass.ds(b, 1), :, some]
                return v.rearrange("p o h w -> p (o h) w" if k % 2 == 0 else "p o h w -> p (o w) h")
            v = t_x[:, :, bass.ds(b, 1), some, :] if k % 2 == 0 else t_x[:, :, bass.ds(b, 1), :, some]
            return v.rearrange("p f o h w -> p f (o h) w" if k % 2 == 0 else "p f o h w -> p f (o w) h")

        def grid(ap):
            return ap.rearrange("p f (a b) -> p f a b", b=WW)

        def each(eng, body, first=None):
            for k in range(KD):
                with eng.Fori(0, B) as b:
                    if first is not None:
                        first(k, b)
                    with eng.Fori(0, CB) as i:
                        body(k, b, i if k < 2 else (CB - 1) - i, i + b * CB + k * B * CB)

        with nc.Block() as block:
            @block.tensor
            def _(pe):
                def body(k, b, c, t):
                    pe.wait_ge(rest_ready, t)
                    pe.wait_ge(dts_ready, t)
                    for half in range(2):
                        mm = pe.matmul(ps_xd[0:104, :], xproj[:, k, half, :], piece(xc, k, b, c, half),
                                       start=(half == 0), stop=(half == 1))
                    mm.then_inc(xd_ready, 1)
                    pe.wait_ge(dts_ready, t + 1)
                    pe.wait_ge(delta_ready, t)
                    for half in range(2):
                        mm = pe.matmul(ps_dt[:, half, :], dtw[96:104, k, half * P:(half + 1) * P],
                                       dts[96:104, :], start=True, stop=True)
                    mm.then_inc(dt_ready, 1)
                    pe.wait_ge(split_ready, 2 * t + 2)

                    def add_y(n):
                        pe.wait_ge(hc_ready, t * NS + (n + 1 + FREE))
                        if n == 0:
                            pe.wait_ge(y_added, t)
                        for half in range(2):
                            mm = pe.matmul(ps_y[:, half, :], cm("ident"), h[n % 2][:, half, :],
                                           start=(n == 0), stop=(n == NS - 1))
                        mm.then_inc(y_summed, 1)

                    for n in range(NS):
                        pe.wait_ge(dbx_ready, t * NS + (n + 1))
                        pe.matmul(ps_b[n % 2][:, :], sel[:, n, :], split[:, :], start=True, stop=True).then_inc(b_ready, 1)
                        pe.wait_ge(c_copied, t * NS + n)
                        pe.matmul(ps_c[:, :], sel[:, NS + n, :], split[:, :], start=True, stop=True).then_inc(c_ready, 1)
                        if n >= 2:
                            add_y(n - 2)
                    add_y(NS - 2)
                    add_y(NS - 1)

                pe.sem_inc(dbx_ready, FREE)
                each(pe, body)

            @block.scalar
            def _(act):
                act.preload_act_table_set(LN_SET)
                act.wait_ge(a_clamped, 1)
                act.activation(neg_a[:, :, :, :], neg_a[:, :, :, :], ACT.Exp).then_inc(a_exp, 1)
                act.sem_inc(scanned, 2 * FREE)
                act.sem_inc(hc_ready, FREE)

                def body(k, b, c, t):
                    act.wait_ge(xd_ready, t + 1)
                    act.activation(split[:, :], ps_xd[0:96, :], ACT.Copy).then_inc(hi_ready, 1)
                    act.activation(dts[96:104, :], ps_xd[96:104, :], ACT.Copy).then_inc(dts_ready, 1)
                    act.wait_ge(rest_ready, t + 1)
                    act.activation(split[32:64, :], rest[32:64, :], ACT.Copy).then_inc(split_ready, 1)
                    act.activation(mid[64:96, :], rest[64:96, :], ACT.Copy).then_inc(mid_ready, 1)
                    act.wait_ge(xm_ready, t + 1)
                    act.activation(e[:, :, :], ln[:, :, :], ACT.Exp).then_inc(e_ready, 1)
                    act.wait_ge(e_ready, t + 1)
                    act.activation(ln[:, :, :], e[:, :, :], ACT.Ln, bias=1.0).then_inc(ln_ready, 1)
                    act.wait_ge(delta_ready, t + 1)
                    for n in range(NS):
                        act.wait_ge(scanned, t * 2 * NS + 2 * (n + 1))
                        for half in range(2):
                            act.activation(da[n % 2][:, half, :], delta[:, half, :], ACT.Exp,
                                           scale=neg_a[:, k, half, n:n + 1]).then_inc(da_ready, 1)
                        act.wait_ge(c_ready, t * NS + (n + 1))
                        act.wait_ge(hc_ready, t * NS + (n + 1))
                        act.activation(c_sb[n % 2][:, :], ps_c[:, :], ACT.Copy).then_inc(c_copied, 1)

                act.wait_ge(a_ready, 1)
                each(act, body)

            @block.vector
            def _(dve):
                dve.tensor_scalar(neg_a[:, :, :, :].rearrange("p k f n -> p (k f n)"), wa("a_log", 0, KD * 2 * NS),
                                  83.0, None, ALU.min).then_inc(a_clamped, 1)
                dve.wait_ge(a_exp, 1)
                dve.tensor_scalar(neg_a[:, :, :, :], neg_a[:, :, :, :], -1.0, None, ALU.mult).then_inc(a_ready, 1)
                dve.tensor_reduce(d_sum[:, :], wa("d_skip", 0, KD * 2).rearrange("p (k f) -> p f k", f=2), AX_X,
                                  ALU.add).then_inc(d_ready, 1)
                dve.wait_ge(d_ready, 1)
                for half in range(2):
                    dve.tensor_scalar(y[:, half], xc[:, half], d_sum[:, half:half + 1], None,
                                      ALU.mult).then_inc(y_started, 1)
                dve.wait_ge(y_started, 2)
                dve.sem_inc(y_summed, FREE)
                dve.sem_inc(state_saved, NS)

                def body(k, b, c, t):
                    g = b + k * B
                    dve.wait_ge(hi_ready, t + 1)
                    dve.wait_ge(split_ready, 2 * t)
                    dve.tensor_tensor(rest[:, :], ps_xd[0:96, :], split[:, :], ALU.subtract).then_inc(rest_ready, 1)
                    dve.wait_ge(dt_ready, t + 1)
                    for half in range(2):
                        ins = dve.tensor_scalar(ln[:, half, :], ps_dt[:, half, :], wa("dt_b", 2 * k + half), 40.0,
                                                ALU.add, ALU.min)
                    ins.then_inc(xm_ready, 1)
                    dve.wait_ge(mid_ready, t + 1)
                    dve.tensor_tensor(split[64:96, :], rest[64:96, :], mid[64:96, :],
                                      ALU.subtract).then_inc(split_ready, 1)
                    link = Steps(dve, soft_step, t * SOFT)
                    dve.wait_ge(e_ready, t + 1)
                    link(dve.tensor_scalar(r[:, :, :], e[:, :, :], 0.02, 1.0 / 3.0, ALU.min, ALU.mult))
                    dve.wait_ge(ln_ready, t + 1)
                    link(dve.scalar_tensor_tensor(ln[:, :, :], e[:, :, :], 0.02, ln[:, :, :], ALU.is_ge, ALU.mult))
                    link(dve.scalar_tensor_tensor(e[:, :, :], r[:, :, :], 0.5, r[:, :, :], ALU.subtract, ALU.mult))
                    link(dve.scalar_tensor_tensor(e[:, :, :], e[:, :, :], 1.0 / 3.0, r[:, :, :], ALU.add, ALU.mult))
                    link(dve.scalar_tensor_tensor(e[:, :, :], e[:, :, :], 9.0, ln[:, :, :], ALU.mult, ALU.max))
                    for half in range(2):
                        ins = dve.scalar_tensor_tensor(delta[:, half, :], ps_dt[:, half, :], wa("dt_b", 2 * k + half),
                                                       e[:, half, :], ALU.add, ALU.max)
                    ins.then_inc(delta_ready, 1)
                    dve.wait_ge(delta_ready, t + 1)
                    dve.tensor_tensor(grid(u[:, :, :]), grid(delta[:, :, :]), piece(xc, k, b, c),
                                      ALU.mult).then_inc(u_ready, 1)
                    dve.wait_ge(u_ready, t + 1)
                    dve.wait_ge(state_reset, g + 1)
                    order = slice(None) if k < 2 else slice(None, None, -1)
                    last = CH - 1 if k < 2 else 0
                    for n in range(NS):
                        s = n % 2
                        dve.wait_ge(b_ready, t * NS + (n + 1))
                        dve.tensor_tensor(dbx[s][:, :, :], u[:, :, :], halves(ps_b[s][:, :], 2),
                                          ALU.mult).then_inc(dbx_ready, 1)
                        dve.wait_ge(da_ready, t * 2 * NS + 2 * (n + 1))
                        dve.wait_ge(dbx_ready, t * NS + (n + 1 + FREE))
                        dve.wait_ge(y_summed, t * NS + (n + 1))
                        dve.wait_ge(state_saved, t * NS + (n + 1))
                        for half in range(2):
                            dve.tensor_tensor_scan(h[s][:, half, order], da[s][:, half, order], dbx[s][:, half, order],
                                                   state[:, half, n:n + 1], ALU.mult, ALU.add).then_inc(scanned, 1)
                    dve.wait_ge(y_summed, t * NS + (NS + FREE))
                    dve.wait_ge(y_added, t)
                    dve.tensor_tensor(piece(y, k, b, c), piece(y, k, b, c), grid(ps_y[:, :, :]),
                                      ALU.add).then_inc(y_added, 1)

                each(dve, body)

            @block.gpsimd
            def _(pool):
                def first(k, b):
                    pool.memset(state[:, :, :], 0.0).then_inc(state_reset, 1)

                def body(k, b, c, t):
                    last = CH - 1 if k < 2 else 0
                    for n in range(NS):
                        s = n % 2
                        pool.wait_ge(scanned, t * 2 * NS + (2 * (n + 1) + 2 * FREE))
                        end = h[s][:, :, last:last + 1]
                        pool.tensor_tensor(state[:, :, n:n + 1], end, cm("ones")[:, 0:2].rearrange("p (a b) -> p a b", b=1), ALU.mult).then_inc(state_saved, 1)
                        pool.wait_ge(state_saved, t * NS + (n + 1 + NS))
                        pool.wait_ge(c_copied, t * NS + (n + 1))
                        pool.tensor_tensor(h[s][:, :, :], h[s][:, :, :], halves(c_sb[s][:, :], 2),
                                           ALU.mult).then_inc(hc_ready, 1)

                each(pool, body, first)


def gated_output(nc, xt, cm, wa, gscale, gshift, y, z):
    with ExitStack() as ctx:
        p = Place(nc, ctx)
        xn = [p.sb(f"xn{s}", [P, CH]) for s in range(2)]
        psz = [p.ps(f"psz{s}", [P, 2, CH]) for s in range(2)]
        xn_ready = p.sem("z_xn_ready")
        z_mul = p.sem("z_mul")
        z_ready = p.sem("z_ready")
        with nc.Block() as block:
            @block.vector
            def _(dve):
                dve.sem_inc(z_mul, FREE)
                for b in range(B):
                    with dve.Fori(0, CB // 2) as i:
                        for s in range(2):
                            t = 2 * i + (s + b * CB)
                            dve.wait_ge(z_mul, t + 1)
                            dve.tensor_scalar(xn[s][:, :], xt[:, bass.ds(t * CH, CH)], gscale[:, b:b + 1],
                                              gshift[:, b:b + 1], ALU.mult, ALU.add).then_inc(xn_ready, 1)

            @block.tensor
            def _(pe):
                pe.sem_inc(z_ready, FREE)
                with pe.Fori(0, NC // 2) as i:
                    for s in range(2):
                        t = 2 * i + s
                        pe.wait_ge(xn_ready, t + 1)
                        pe.wait_ge(z_ready, t + 1)
                        for half in range(2):
                            mm = pe.matmul(psz[s][:, half, :], wa("win", (2 + half) * P, P), xn[s][:, :],
                                           start=True, stop=True)
                        mm.then_inc(z_mul, 1)

            @block.scalar
            def _(act):
                act.preload_act_table(ACT.Silu)
                with act.Fori(0, NC // 2) as i:
                    for s in range(2):
                        t = 2 * i + s
                        act.wait_ge(z_mul, t + (1 + FREE))
                        act.activation(z[:, :, bass.ds(t * CH, CH)], psz[s][:, :, :], ACT.Silu).then_inc(z_ready, 1)
    with ExitStack() as ctx:
        p = Place(nc, ctx)
        d = [p.sb(f"d{s}", [P, 2, CH]) for s in range(2)]
        sq = [p.sb(f"sq{s}", [P, 2, CH]) for s in range(2)]
        lv = [p.sb(f"lv{s}", [P, CH]) for s in range(2)]
        psm = [p.ps(f"psm{s}", [P, CH]) for s in range(2)]
        psv = [p.ps(f"psv{s}", [P, CH]) for s in range(2)]
        pso = [p.ps(f"pso{s}", [P, CH]) for s in range(2)]
        mean_ready = p.sem("mean_ready")
        d_ready = p.sem("d_ready")
        sq_ready = p.sem("sq_ready")
        var_ready = p.sem("lvar_ready")
        ln_ready = p.sem("lln_ready")
        rstd_ready = p.sem("rstd_ready")
        norm_step = p.sem("norm_step")
        gated = p.sem("gated")
        out_ready = p.sem("out_ready")
        x_added = p.sem("x_added")
        y_flat = y[:, :].rearrange("p f b h w -> p f (b h w)")
        with nc.Block() as block:
            @block.tensor
            def _(pe):
                with pe.Fori(0, NC // 2) as i:
                    for s in range(2):
                        t = 2 * i + s
                        for half in range(2):
                            mm = pe.matmul(psm[s][:, :], cm("ones256"), y_flat[:, half, bass.ds(t * CH, CH)],
                                           start=(half == 0), stop=(half == 1))
                        mm.then_inc(mean_ready, 1)
                    for s in range(2):
                        t = 2 * i + s
                        pe.wait_ge(sq_ready, t + 1)
                        for half in range(2):
                            mm = pe.matmul(psv[s][:, :], cm("ones256"), sq[s][:, half, :],
                                           start=(half == 0), stop=(half == 1))
                        mm.then_inc(var_ready, 1)
                    for s in range(2):
                        t = 2 * i + s
                        pe.wait_ge(gated, t + 1)
                        for half in range(2):
                            mm = pe.matmul(pso[s][:, :], wa("wout", half * P, P), d[s][:, half, :],
                                           start=(half == 0), stop=(half == 1))
                        mm.then_inc(out_ready, 1)

            @block.scalar
            def _(act):
                act.preload_act_table_set(LN_SET)
                with act.Fori(0, NC // 2) as i:
                    for s in range(2):
                        t = 2 * i + s
                        act.wait_ge(d_ready, t + 1)
                        act.activation(sq[s][:, :, :], d[s][:, :, :], ACT.Square).then_inc(sq_ready, 1)
                    for s in range(2):
                        t = 2 * i + s
                        act.wait_ge(var_ready, t + 1)
                        act.activation(lv[s][:, :], psv[s][:, :], ACT.Ln, bias=cm("eps")).then_inc(ln_ready, 1)
                        act.wait_ge(ln_ready, t + 1)
                        act.activation(lv[s][:, :], lv[s][:, :], ACT.Exp, scale=-0.5).then_inc(rstd_ready, 1)

            @block.vector
            def _(dve):
                with dve.Fori(0, NC // 2) as i:
                    for s in range(2):
                        t = 2 * i + s
                        dve.wait_ge(mean_ready, t + 1)
                        dve.tensor_tensor(d[s][:, :, :], y_flat[:, :, bass.ds(t * CH, CH)], halves(psm[s][:, :], 2),
                                          ALU.subtract).then_inc(d_ready, 1)
                    for s in range(2):
                        t = 2 * i + s
                        dve.wait_ge(rstd_ready, t + 1)
                        link = Steps(dve, norm_step, t * 2)
                        for half in range(2):
                            link(dve.scalar_tensor_tensor(d[s][:, half, :], d[s][:, half, :], wa("ln_w", half),
                                                          lv[s][:, :], ALU.mult, ALU.mult))
                        for half in range(2):
                            ins = dve.scalar_tensor_tensor(d[s][:, half, :], d[s][:, half, :], wa("ln_b", half),
                                                           z[:, half, bass.ds(t * CH, CH)], ALU.add, ALU.mult)
                        ins.then_inc(gated, 1)
                    for s in range(2):
                        t = 2 * i + s
                        dve.wait_ge(out_ready, t + 1)
                        x = xt[:, bass.ds(t * CH, CH)]
                        dve.tensor_tensor(x, x, pso[s][:, :], ALU.add).then_inc(x_added, 1)


def ema_gate(nc, xt, cm, wb, gscale, gshift):
    with ExitStack() as ctx:
        p = Place(nc, ctx)
        prim = p.sb("prim", [P, N])
        gate = p.sb("gate", [P, B, WW, HH])
        decay = p.sb("decay", [P, WW, HH])
        b01 = p.sb("b01", [P, 1])
        xn = [p.sb(f"exn{s}", [P, CH]) for s in range(2)]
        prod = [p.sb(f"prod{s}", [P, CH]) for s in range(2)]
        psg = [p.ps(f"psg{s}", [P, CH]) for s in range(2)]
        psp = [p.ps(f"psp{s}", [P, CH]) for s in range(2)]
        pso = [p.ps(f"epso{s}", [P, CH]) for s in range(2)]
        const_step = p.sem("ema_const")
        xn_ready = p.sem("e_xn_ready")
        expanded = p.sem("expanded")
        gate_ready = p.sem("gate_ready")
        prim_ready = p.sem("prim_ready")
        averaged = p.sem("averaged")
        sig_ready = p.sem("sig_ready")
        prod_ready = p.sem("prod_ready")
        out_ready = p.sem("e_out_ready")
        x_added = p.sem("e_x_added")
        with nc.Block() as block:
            @block.vector
            def _(dve):
                link = Steps(dve, const_step)
                link(dve.tensor_scalar(b01[:, :], wb("b_exp", 1), 0.1, None, ALU.mult))
                link(dve.memset(decay[:, :, :], 0.9))
                link(dve.memset(decay[:, :, 0:1], 0.0))
                dve.sem_inc(expanded, FREE)
                for b in range(B):
                    with dve.Fori(0, CB // 2) as i:
                        for s in range(2):
                            t = 2 * i + (s + b * CB)
                            dve.wait_ge(expanded, t + 1)
                            dve.tensor_scalar(xn[s][:, :], xt[:, bass.ds(t * CH, CH)], gscale[:, b:b + 1],
                                              gshift[:, b:b + 1], ALU.mult, ALU.add).then_inc(xn_ready, 1)
                        for s in range(2):
                            t = 2 * i + (s + b * CB)
                            dve.wait_ge(expanded, t + (1 + FREE))
                            dve.tensor_scalar(prim[:, bass.ds(t * CH, CH)], psp[s][:, :], wb("b_exp", 0), None,
                                              ALU.add).then_inc(prim_ready, 1)
                for b in range(B):
                    dve.wait_ge(gate_ready, FREE + (b + 1) * CB)
                    row = gate[:, b].rearrange("p w h -> p (w h)")
                    dve.tensor_tensor_scan(row, decay[:, :, :].rearrange("p w h -> p (w h)"), row, 0.0,
                                           ALU.mult, ALU.add).then_inc(averaged, 1)
                dve.sem_inc(out_ready, FREE)
                for b in range(B):
                    dve.wait_ge(sig_ready, (b + 1) * CB)
                    dve.wait_ge(prim_ready, FREE + (b + 1) * CB)
                    with dve.Fori(0, CB // 2) as i:
                        for s in range(2):
                            c = 2 * i + s
                            t = 2 * i + (s + b * CB)
                            dve.wait_ge(out_ready, t + 1)
                            dve.tensor_tensor(prod[s][:, :].rearrange("p (h w) -> p h w", w=WW),
                                              prim[:, bass.ds(t * CH, CH)].rearrange("p (h w) -> p h w", w=WW),
                                              gate[:, b, :, bass.ds(c * ROWS, ROWS)].rearrange("p w h -> p h w"),
                                              ALU.mult).then_inc(prod_ready, 1)
                        for s in range(2):
                            t = 2 * i + (s + b * CB)
                            dve.wait_ge(out_ready, t + (1 + FREE))
                            x = xt[:, bass.ds(t * CH, CH)]
                            dve.scalar_tensor_tensor(x, pso[s][:, :], wb("b_con", 0), x,
                                                     ALU.add, ALU.add).then_inc(x_added, 1)

            @block.tensor
            def _(pe):
                pe.sem_inc(gate_ready, FREE)
                pe.sem_inc(prim_ready, FREE)
                with pe.Fori(0, NC // 2) as i:
                    for s in range(2):
                        t = 2 * i + s
                        pe.wait_ge(xn_ready, t + 1)
                        pe.wait_ge(gate_ready, t + 1)
                        pe.wait_ge(prim_ready, t + 1)
                        pe.matmul(psg[s][:, :], wb("w_exp", P, P), xn[s][:, :], start=True, stop=True)
                        pe.matmul(psp[s][:, :], wb("w_exp", 0, P), xn[s][:, :], start=True, stop=True)\
                            .then_inc(expanded, 1)
                pe.sem_inc(x_added, FREE)
                with pe.Fori(0, NC // 2) as i:
                    for s in range(2):
                        t = 2 * i + s
                        pe.wait_ge(prod_ready, t + 1)
                        pe.wait_ge(x_added, t + 1)
                        pe.matmul(pso[s][:, :], wb("w_con", 0, P), prod[s][:, :], start=True, stop=True)\
                            .then_inc(out_ready, 1)

            @block.scalar
            def _(act):
                act.wait_ge(const_step, 1)
                for b in range(B):
                    with act.Fori(0, CB // 2) as i:
                        for s in range(2):
                            c = 2 * i + s
                            act.wait_ge(expanded, c + (b * CB + 1 + FREE))
                            act.activation(gate[:, b, :, bass.ds(c * ROWS, ROWS)].rearrange("p w h -> p h w"),
                                           psg[s][:, :].rearrange("p (h w) -> p h w", w=WW), ACT.Identity,
                                           bias=b01[:, :], scale=0.1).then_inc(gate_ready, 1)
                act.preload_act_table(ACT.Sigmoid)
                for b in range(B):
                    act.wait_ge(averaged, b + 1)
                    row = gate[:, b].rearrange("p w h -> p (w h)")
                    with act.Fori(0, CB) as c:
                        part = row[:, bass.ds(c * CH, CH)]
                        act.activation(part, part, ACT.Sigmoid).then_inc(sig_ready, 1)


def layer_norm(nc, xt, cm, u, name):
    G = 4
    with ExitStack() as ctx:
        p = Place(nc, ctx)
        d = [p.sb(f"{name}_d{s}", [P, CH]) for s in range(G)]
        sq = [p.sb(f"{name}_sq{s}", [P, CH]) for s in range(G)]
        lv = [p.sb(f"{name}_lv{s}", [P, CH]) for s in range(G)]
        psm = [p.ps(f"{name}_psm{s}", [P, CH]) for s in range(G)]
        psv = [p.ps(f"{name}_psv{s}", [P, CH]) for s in range(G)]
        mean_ready = p.sem(name + "_mean_ready")
        d_ready = p.sem(name + "_d_ready")
        sq_ready = p.sem(name + "_sq_ready")
        var_ready = p.sem(name + "_var_ready")
        ln_ready = p.sem(name + "_ln_ready")
        rstd_ready = p.sem(name + "_rstd_ready")
        u_ready = p.sem(name + "_u_ready")
        with nc.Block() as block:
            @block.tensor
            def _(pe):
                with pe.Fori(0, NC // G) as i:
                    for s in range(G):
                        t = i * G + s
                        pe.matmul(psm[s][:, :], cm("ones128"), xt[:, bass.ds(t * CH, CH)],
                                  start=True, stop=True).then_inc(mean_ready, 1)
                    for s in range(G):
                        t = i * G + s
                        pe.wait_ge(sq_ready, t + 1)
                        pe.matmul(psv[s][:, :], cm("ones128"), sq[s][:, :],
                                  start=True, stop=True).then_inc(var_ready, 1)

            @block.scalar
            def _(act):
                act.preload_act_table_set(LN_SET)
                with act.Fori(0, NC // G) as i:
                    for s in range(G):
                        t = i * G + s
                        act.wait_ge(d_ready, t + 1)
                        act.activation(sq[s][:, :], d[s][:, :], ACT.Square).then_inc(sq_ready, 1)
                    for s in range(G):
                        t = i * G + s
                        act.wait_ge(var_ready, t + 1)
                        act.activation(lv[s][:, :], psv[s][:, :], ACT.Ln, bias=cm("eps")).then_inc(ln_ready, 1)
                        act.wait_ge(ln_ready, t + 1)
                        act.activation(lv[s][:, :], lv[s][:, :], ACT.Exp, scale=-0.5).then_inc(rstd_ready, 1)

            @block.vector
            def _(dve):
                with dve.Fori(0, NC // G) as i:
                    dve.wait_ge(u_ready, i * G)
                    for s in range(G):
                        t = i * G + s
                        dve.wait_ge(mean_ready, t + 1)
                        dve.tensor_tensor(d[s][:, :], xt[:, bass.ds(t * CH, CH)], psm[s][:, :],
                                          ALU.subtract).then_inc(d_ready, 1)
                    for s in range(G):
                        t = i * G + s
                        dve.wait_ge(rstd_ready, t + 1)
                        dve.tensor_tensor(u[:, bass.ds(t * CH, CH)], d[s][:, :], lv[s][:, :],
                                          ALU.mult).then_inc(u_ready, 1)


def linear_attention(nc, xt, cm, wc, u):
    H, DH = 4, 32
    J = CH // P
    with ExitStack() as ctx:
        p = Place(nc, ctx)
        k = p.sb("k", [P, B, L])
        q_t = p.sb("q_t", [P, B, L])
        kmax = p.sb("kmax", [P, B, CB])
        nmax = p.sb("nmax", [P, B])
        ctxs = p.sb("ctxs", [P, B, P + 1])
        m_out = p.sb("m_out", [P, B, P])
        stats = p.sb("a_stats", [P, NC, 6])
        with ExitStack() as inner:
            p2 = Place(nc, inner)
            psk = [p2.ps(f"psk{s}", [P, CH]) for s in range(2)]
            ke = [p2.sb(f"ke{s}", [P, CH]) for s in range(2)]
            uf = [p2.sb(f"uf{s}", [P, CH]) for s in range(2)]
            kt = p2.sb("kt", [P, J, P])
            vt = p2.sb("vt", [P, J, P + 1])
            q1 = p2.sb("q1", [P, J * H, DH])
            qm = p2.sb("qm", [P, J * H])
            qs = p2.sb("qs", [P, J * H])
            ps_kt = p2.ps("ps_kt", [P, J, P])
            ps_v = p2.ps("ps_v", [P, J, P])
            ps_q = p2.ps("ps_q", [P, J * H, DH])
            ps_qt = p2.ps("ps_qt", [P, CH])
            ps_ctx = p2.ps("ps_ctx", [P, CH])
            k_mul = p2.sem("k_mul")
            k_copied = p2.sem("k_copied")
            kmax_ready = p2.sem("kmax_ready")
            nmax_step = p2.sem("nmax_step")
            nmax_ready = p2.sem("nmax_ready")
            ones_set = p2.sem("ones_set")
            uf_ready = p2.sem("uf_ready")
            ke_ready = p2.sem("ke_ready")
            kt_mul = p2.sem("kt_mul")
            vq_mul = p2.sem("vq_mul")
            kt_ready = p2.sem("kt_ready")
            vt_ready = p2.sem("vt_ready")
            ctx_mul = p2.sem("ctx_mul")
            ctx_added = p2.sem("ctx_added")
            q_step = p2.sem("q_step")
            q_shifted = p2.sem("q_shifted")
            q_exp = p2.sem("q_exp")
            q_norm = p2.sem("q_norm")
            qt_mul = p2.sem("qt_mul")
            qt_ready = p2.sem("qt_ready")

            def over_head(ap):
                a = [list(x) for x in ap.ap]
                return bass.AP(tensor=ap.tensor, offset=ap.offset, ap=a + [[0, DH]])

            with nc.Block() as block:
                @block.tensor
                def _(pe):
                    pe.sem_inc(k_copied, FREE)
                    with pe.Fori(0, NC // 2) as i:
                        for s in range(2):
                            t = 2 * i + s
                            pe.wait_ge(k_copied, t + 1)
                            pe.matmul(psk[s][:, :], wc("w_k", 0, P), u[:, bass.ds(t * CH, CH)],
                                      start=True, stop=True).then_inc(k_mul, 1)
                    with pe.Fori(0, NC // 2) as i:
                        for s in range(2):
                            t = 2 * i + s
                            pe.wait_ge(uf_ready, t + 1)
                            pe.wait_ge(vt_ready, t)
                            pe.wait_ge(q_shifted, t)
                            for j in range(J):
                                pe.matmul(ps_v[:, j, :], uf[s][:, j * P:(j + 1) * P], wc("w_v", 0, P),
                                          start=True, stop=True)
                                mm = pe.matmul(ps_q[:, j * H:(j + 1) * H, :], uf[s][:, j * P:(j + 1) * P],
                                               wc("w_q", 0, P), start=True, stop=True)
                            mm.then_inc(vq_mul, 1)
                            pe.wait_ge(ke_ready, t + 1)
                            pe.wait_ge(kt_ready, t)
                            for j in range(J):
                                mm = pe.transpose(ps_kt[:, j, :], ke[s][:, j * P:(j + 1) * P], cm("ident"))
                            mm.then_inc(kt_mul, 1)
                            pe.wait_ge(kt_ready, t + 1)
                            pe.wait_ge(vt_ready, t + 1)
                            pe.wait_ge(ctx_added, t)
                            for j in range(J):
                                mm = pe.matmul(ps_ctx[:, 0:P + 1], kt[:, j, :], vt[:, j, :],
                                               start=(j == 0), stop=(j == J - 1))
                            mm.then_inc(ctx_mul, 1)
                            pe.wait_ge(q_norm, t + 1)
                            pe.wait_ge(qt_ready, t)
                            for j in range(J):
                                mm = pe.transpose(ps_qt[:, j * P:(j + 1) * P],
                                                  q1[:, j * H:(j + 1) * H, :].rearrange("p h d -> p (h d)"), cm("ident"))
                            mm.then_inc(qt_mul, 1)

                @block.scalar
                def _(act):
                    act.preload_act_table(ACT.Exp)
                    k_flat = k[:, :, :].rearrange("p b l -> p (b l)")
                    q_flat = q_t[:, :, :].rearrange("p b l -> p (b l)")
                    with act.Fori(0, NC // 2) as i:
                        for s in range(2):
                            t = 2 * i + s
                            act.wait_ge(k_mul, t + 1)
                            act.activation(k_flat[:, bass.ds(t * CH, CH)], psk[s][:, :], ACT.Copy).then_inc(k_copied, 1)
                    act.wait_ge(nmax_ready, 1)
                    act.wait_ge(k_copied, NC + FREE)
                    for b in range(B):
                        with act.Fori(0, CB // 2) as i:
                            for s in range(2):
                                t = 2 * i + (s + b * CB)
                                act.activation(ke[s][:, :], k_flat[:, bass.ds(t * CH, CH)], ACT.Exp,
                                               bias=nmax[:, b:b + 1]).then_inc(ke_ready, 1)
                                act.wait_ge(q_shifted, t + 1)
                                act.activation(q1[:, :, :], q1[:, :, :], ACT.Exp).then_inc(q_exp, 1)
                                act.wait_ge(kt_mul, t + 1)
                                act.activation(kt[:, :, :], ps_kt[:, :, :], ACT.Copy).then_inc(kt_ready, 1)
                                act.wait_ge(qt_mul, t + 1)
                                act.activation(q_flat[:, bass.ds(t * CH, CH)], ps_qt[:, :], ACT.Copy,
                                               scale=DH ** -0.5).then_inc(qt_ready, 1)

                @block.vector
                def _(dve):
                    dve.memset(vt[:, :, P:P + 1], 1.0).then_inc(ones_set, 1)
                    dve.memset(ctxs[:, :, :], 0.0).then_inc(ones_set, 1)
                    kmax_flat = kmax[:, :, :].rearrange("p b c -> p (b c)")
                    k_flat = k[:, :, :].rearrange("p b l -> p (b l)")
                    with dve.Fori(0, NC // 2) as i:
                        for s in range(2):
                            t = 2 * i + s
                            dve.wait_ge(k_copied, t + (1 + FREE))
                            dve.tensor_reduce(kmax_flat[:, bass.ds(t, 1)], k_flat[:, bass.ds(t * CH, CH)], AX_X,
                                              ALU.max).then_inc(kmax_ready, 1)
                    dve.wait_ge(kmax_ready, NC)
                    dve.tensor_reduce(nmax[:, :], kmax[:, :, :], AX_X, ALU.max).then_inc(nmax_step, 1)
                    dve.wait_ge(nmax_step, 1)
                    dve.tensor_scalar(nmax[:, :], nmax[:, :], -1.0, None, ALU.mult).then_inc(nmax_ready, 1)
                    dve.wait_ge(ones_set, 2)
                    dve.sem_inc(vq_mul, FREE)
                    for b in range(B):
                        with dve.Fori(0, CB // 2) as i:
                            for s in range(2):
                                t = 2 * i + (s + b * CB)
                                dve.wait_ge(vq_mul, t + 1)
                                dve.tensor_copy(uf[s][:, :], u[:, bass.ds(t * CH, CH)]).then_inc(uf_ready, 1)
                                dve.wait_ge(vq_mul, t + (1 + FREE))
                                link = Steps(dve, q_step, t * 3)
                                link(dve.tensor_reduce(qm[:, :], ps_q[:, :, :], AX_X, ALU.max))
                                dve.wait_ge(qt_mul, t)
                                dve.tensor_tensor(q1[:, :, :], ps_q[:, :, :], over_head(qm[:, :]),
                                                  ALU.subtract).then_inc(q_shifted, 1)
                                dve.wait_ge(ctx_mul, t)
                                dve.tensor_copy(vt[:, :, 0:P], ps_v[:, :, :]).then_inc(vt_ready, 1)
                                dve.wait_ge(q_exp, t + 1)
                                link(dve.tensor_reduce(qs[:, :], q1[:, :, :], AX_X, ALU.add))
                                link(dve.reciprocal(qs[:, :], qs[:, :]))
                                dve.tensor_tensor(q1[:, :, :], q1[:, :, :], over_head(qs[:, :]),
                                                  ALU.mult).then_inc(q_norm, 1)
                                dve.wait_ge(ctx_mul, t + 1)
                                dve.wait_ge(ctx_added, t)
                                dve.tensor_tensor(ctxs[:, b, :], ctxs[:, b, :], ps_ctx[:, 0:P + 1],
                                                  ALU.add).then_inc(ctx_added, 1)
        with ExitStack() as inner:
            p2 = Place(nc, inner)
            mv = p2.sb("a_mv", [P, B, 2])
            ex = p2.sb("a_ex", [P, B, 2])
            g = p2.sb("a_g", [P, B, 2])
            var = p2.sb("a_var", [P, B])
            std = p2.sb("a_std", [P, B])
            sc = p2.sb("a_sc", [P, B])
            sh = p2.sb("a_sh", [P, B])
            kinv = p2.sb("kinv", [P, B])
            ps_m = p2.ps("ps_m", [P, B, P])
            ps_g = p2.ps("ps_g", [P, CH])
            ps_o = [p2.ps(f"ps_o{s}", [P, CH]) for s in range(2)]
            step = p2.sem("m_step")
            ctx_ready = p2.sem("ctx_ready")
            m_mul = p2.sem("m_mul")
            m_ready = p2.sem("m_ready")
            o_mul = p2.sem("o_mul")
            o_ready = p2.sem("o_ready")
            stats_ready = p2.sem("o_stats_ready")
            moments_ready = p2.sem("o_moments_ready")
            group_ready = p2.sem("o_group_ready")
            var_ready = p2.sem("o_var_ready")
            std_ready = p2.sem("o_std_ready")
            scale_ready = p2.sem("scale_ready")
            o_scaled = p2.sem("o_scaled")
            x_added = p2.sem("o_x_added")
            with nc.Block() as block:
                @block.vector
                def _(dve):
                    link = Steps(dve, step)
                    link(dve.reciprocal(kinv[:, :], ctxs[:, :, P]))
                    for b in range(B):
                        ins = dve.scalar_tensor_tensor(ctxs[:, b, 0:P], ctxs[:, b, 0:P], kinv[:, b:b + 1], cm("heads"),
                                                       ALU.mult, ALU.mult)
                    ins.then_inc(ctx_ready, 1)
                    dve.wait_ge(m_mul, 1)
                    dve.tensor_copy(m_out[:, :, :], ps_m[:, :, :]).then_inc(m_ready, 1)
                    with dve.Fori(0, NC) as t:
                        dve.wait_ge(o_ready, t + (1 + FREE))
                        dve.bn_stats(stats[:, bass.ds(t, 1), :].rearrange("p a s -> p (a s)"),
                                     u[:, bass.ds(t * CH, CH)]).then_inc(stats_ready, 1)
                    dve.wait_ge(stats_ready, NC)
                    for b in range(B):
                        link(dve.bn_aggr(mv[:, b, :], stats[:, b * CB:(b + 1) * CB, :].rearrange("p a s -> p (a s)")))
                    link(dve.tensor_tensor(ex[:, :, 1], mv[:, :, 0], mv[:, :, 0], ALU.mult))
                    link(dve.tensor_copy(ex[:, :, 0], mv[:, :, 0]))
                    dve.tensor_tensor(ex[:, :, 1], ex[:, :, 1], mv[:, :, 1], ALU.add).then_inc(moments_ready, 1)
                    dve.wait_ge(group_ready, 1)
                    link(dve.tensor_copy(g[:, :, :].rearrange("p b s -> p (b s)"), ps_g[:, 0:2 * B]))
                    link(dve.tensor_tensor(var[:, :], g[:, :, 0], g[:, :, 0], ALU.mult))
                    dve.tensor_tensor(var[:, :], g[:, :, 1], var[:, :], ALU.subtract).then_inc(var_ready, 1)
                    dve.wait_ge(std_ready, 1)
                    link(dve.reciprocal(std[:, :], std[:, :]))
                    link(dve.tensor_scalar(sc[:, :], std[:, :], wc("gn_w", 0), None, ALU.mult))
                    link(dve.tensor_tensor(sh[:, :], g[:, :, 0], sc[:, :], ALU.mult))
                    dve.tensor_scalar(sh[:, :], sh[:, :], -1.0, wc("gn_b", 0), ALU.mult, ALU.add).then_inc(scale_ready, 1)
                    with dve.Fori(0, NC) as t:
                        dve.wait_ge(o_scaled, t + 1)
                        x = xt[:, bass.ds(t * CH, CH)]
                        dve.tensor_tensor(x, x, u[:, bass.ds(t * CH, CH)], ALU.add).then_inc(x_added, 1)

                @block.tensor
                def _(pe):
                    pe.wait_ge(ctx_ready, 1)
                    for b in range(B):
                        mm = pe.matmul(ps_m[:, b, :], ctxs[:, b, 0:P], wc("w_o", 0, P), start=True, stop=True)
                    mm.then_inc(m_mul, 1)
                    pe.wait_ge(m_ready, 1)
                    pe.sem_inc(o_ready, FREE)
                    for b in range(B):
                        with pe.Fori(0, CB // 2) as i:
                            for s in range(2):
                                t = 2 * i + (s + b * CB)
                                pe.wait_ge(o_ready, t + 1)
                                pe.matmul(ps_o[s][:, :], m_out[:, b, :],
                                          q_t[:, :, :].rearrange("p b l -> p (b l)")[:, bass.ds(t * CH, CH)],
                                          start=True, stop=True).then_inc(o_mul, 1)
                    pe.wait_ge(moments_ready, 1)
                    pe.matmul(ps_g[:, 0:2 * B], cm("ones128"), ex[:, :, :].rearrange("p b s -> p (b s)"),
                              start=True, stop=True).then_inc(group_ready, 1)

                @block.scalar
                def _(act):
                    with act.Fori(0, NC // 2) as i:
                        for s in range(2):
                            t = 2 * i + s
                            act.wait_ge(o_mul, t + 1)
                            act.activation(u[:, bass.ds(t * CH, CH)], ps_o[s][:, :], ACT.Identity,
                                           bias=wc("b_out", 0)).then_inc(o_ready, 1)
                    act.wait_ge(var_ready, 1)
                    act.activation(std[:, :], var[:, :], ACT.Sqrt, bias=cm("eps")).then_inc(std_ready, 1)
                    act.wait_ge(scale_ready, 1)
                    for b in range(B):
                        with act.Fori(0, CB) as c:
                            part = u[:, bass.ds(c * CH + b * L, CH)]
                            act.activation(part, part, ACT.Identity, scale=sc[:, b:b + 1],
                                           bias=sh[:, b:b + 1]).then_inc(o_scaled, 1)


def spectral_ffn(nc, xt, cm, wd, d, u):
    S4, K, T2 = 4, 16, L // 2
    TB = T2 // P
    AR = 3
    ALLM = K * P
    with ExitStack() as ctx:
        p = Place(nc, ctx)
        msel = p.sb("msel", [P, K, 2, P])
        mu = p.sb("mu", [P, AR, P])
        reach = p.sb("reach", [P, CB])
        gain = p.sb("gain", [P, CB])
        with ExitStack() as inner:
            p2 = Place(nc, inner)
            mp = [p2.sb(f"mp{i}", [P, ALLM]) for i in range(2)]
            mm_ = [p2.sb(f"mm{i}", [P, ALLM]) for i in range(2)]
            mus = p2.sb("mus", [P, S4, AR * P])
            acc_p = p2.sb("acc_p", [P, ALLM])
            acc_m = p2.sb("acc_m", [P, ALLM])
            small = p2.sb("small", [P, 8, S4])
            sig = p2.sb("sig", [P, K])
            m_loaded = [p2.sem(f"m_loaded{i}") for i in range(2)]
            mu_loaded = p2.sem("mu_loaded")
            step = p2.sem("w_step")
            shifted = p2.sem("w_shifted")
            expd = p2.sem("w_exp")
            root = p2.sem("sig_root")
            MIXED = 14
            with nc.Block() as block:
                @block.sync
                def _(sp):
                    sp.dma_start(mus[:, :, :].rearrange("p i n -> p (i n)"), d["m_u"]).then_inc(mu_loaded, 16)
                    for i in range(S4):
                        if i >= 2:
                            sp.wait_ge(step, MIXED + 2 * (i - 1))
                        sp.dma_start(mp[i % 2][:, :], d["m_plus"][:, i * ALLM:(i + 1) * ALLM]).then_inc(m_loaded[i % 2], 16)
                        sp.dma_start(mm_[i % 2][:, :], d["m_minus"][:, i * ALLM:(i + 1) * ALLM]).then_inc(m_loaded[i % 2], 16)

                @block.scalar
                def _(act):
                    act.activation(sig[:, :], wd("sigma", 0, K), ACT.Sqrt).then_inc(root, 1)
                    act.wait_ge(root, 1)
                    act.activation(sig[:, :], sig[:, :], ACT.Sqrt).then_inc(root, 1)
                    act.wait_ge(shifted, 1)
                    act.activation(small[:, 1, :], small[:, 0, :], ACT.Exp).then_inc(expd, 1)

                @block.vector
                def _(dve):
                    link = Steps(dve, step)
                    lg, ex, pr, hot, w, one = (small[:, i, :] for i in (0, 1, 2, 3, 4, 5))
                    scal = small[:, 7, :]
                    link(dve.tensor_tensor(lg, wd("logw", 0, S4), wd("gumbel", 0, S4), ALU.add))
                    link(dve.tensor_reduce(scal[:, 0:1], lg, AX_X, ALU.max))
                    dve.tensor_scalar(lg, lg, scal[:, 0:1], None, ALU.subtract).then_inc(shifted, 1)
                    dve.wait_ge(expd, 1)
                    link(dve.tensor_reduce(scal[:, 1:2], ex, AX_X, ALU.add))
                    link(dve.reciprocal(scal[:, 1:2], scal[:, 1:2]))
                    link(dve.tensor_scalar(pr, ex, scal[:, 1:2], None, ALU.mult))
                    link(dve.tensor_reduce(scal[:, 2:3], pr, AX_X, ALU.max))
                    link(dve.tensor_scalar(hot, pr, scal[:, 2:3], None, ALU.is_ge))
                    link(dve.tensor_tensor(one, hot, cm("rank8")[:, 0:S4], ALU.mult))
                    link(dve.tensor_reduce(scal[:, 3:4], one, AX_X, ALU.max))
                    link(dve.tensor_scalar(hot, one, scal[:, 3:4], None, ALU.is_equal))
                    link(dve.tensor_tensor(w, hot, pr, ALU.subtract))
                    link(dve.tensor_tensor(w, w, pr, ALU.add))
                    for src, dst in ((hot, reach), (w, gain)):
                        dve.tensor_scalar(dst[:, :], cm("ones")[:, 0:CB], src[:, 0:1], None, ALU.mult).then_inc(shifted, 1)
                    dve.wait_ge(shifted, 3)
                    n_shift = 3
                    for i in range(1, S4):
                        for src, dst in ((hot, reach), (w, gain)):
                            dve.tensor_scalar(dst[:, 0:CB >> i], dst[:, 0:CB >> i], src[:, i:i + 1], None,
                                              ALU.add).then_inc(shifted, 1)
                            n_shift += 1
                        dve.wait_ge(shifted, n_shift)
                    link(dve.memset(acc_p[:, :], 0.0))
                    link(dve.memset(acc_m[:, :], 0.0))
                    assert link.n == MIXED
                    for i in range(S4):
                        dve.wait_ge(m_loaded[i % 2], 32 * (i // 2 + 1))
                        for src, acc in ((mp, acc_p), (mm_, acc_m)):
                            link(dve.scalar_tensor_tensor(acc[:, :], src[i % 2][:, :], hot[:, i:i + 1], acc[:, :],
                                                          ALU.mult, ALU.add))
                    dve.wait_ge(mu_loaded, 16)
                    flat = mu[:, :, :].rearrange("p i n -> p (i n)")
                    link(dve.tensor_scalar(flat, mus[:, 0, :], hot[:, 0:1], None, ALU.mult))
                    for i in range(1, S4):
                        link(dve.scalar_tensor_tensor(flat, mus[:, i, :], hot[:, i:i + 1], flat, ALU.mult, ALU.add))
                    a3, b3 = (a[:, :].rearrange("p (k n) -> p k n", k=K) for a in (acc_p, acc_m))
                    link(dve.tensor_tensor(msel[:, :, 0, :], a3, b3, ALU.add))
                    link(dve.tensor_tensor(msel[:, :, 1, :], a3, b3, ALU.subtract))
                    dve.wait_ge(root, 2)
                    sa = [list(x) for x in sig[:, :].ap]
                    every = bass.AP(tensor=sig[:, :].tensor, offset=sig[:, :].offset, ap=sa + [[0, P]])
                    for par in range(2):
                        link(dve.tensor_tensor(msel[:, :, par, :], msel[:, :, par, :], every, ALU.mult))
        acc = u
        utok = p.sb("utok", [P, B, 2, TB, P])
        with ExitStack() as inner:
            p2 = Place(nc, inner)
            upad = p2.sb("upad", [P, B, 4 + L])
            uf = [p2.sb(f"suf{s}", [P, CH]) for s in range(2)]
            ps_t = [p2.ps(f"ps_t{s}", [P, 2, 2, P]) for s in range(2)]
            ps_a = [p2.ps(f"ps_a{s}", [P, CH]) for s in range(2)]
            padded = p2.sem("u_padded")
            uf_ready = p2.sem("s_uf_ready")
            up_ready = p2.sem("s_up_ready")
            t_mul = p2.sem("s_t_mul")
            t_copied = p2.sem("s_t_copied")
            a_mul = p2.sem("s_a_mul")
            a_copied = p2.sem("s_a_copied")

            with nc.Block() as block:
                @block.vector
                def _(dve):
                    dve.memset(upad[:, :, 0:4], 0.0).then_inc(padded, 1)
                    dve.sem_inc(t_mul, FREE)
                    for b in range(B):
                        with dve.Fori(0, CB // 2) as i:
                            for s in range(2):
                                c = 2 * i + s
                                t = 2 * i + (s + b * CB)
                                dve.wait_ge(t_mul, t + 1)
                                dve.tensor_scalar(uf[s][:, ::-1], u[:, bass.ds(t * CH, CH)], reach[:, bass.ds(c, 1)], None,
                                                  ALU.mult).then_inc(uf_ready, 1)
                                dve.wait_ge(uf_ready, t + 1)
                                dve.tensor_scalar(upad[:, b, bass.ds(c * CH + 4, CH)], uf[s][:, ::-1], 1.0, None, ALU.mult).then_inc(up_ready, 1)
                                dve.wait_ge(a_mul, t + 1)
                                dve.tensor_scalar(acc[:, bass.ds(t * CH, CH)], ps_a[s][:, :], 1.0, None, ALU.mult).then_inc(a_copied, 1)

                @block.tensor
                def _(pe):
                    pe.wait_ge(padded, 1)
                    pe.sem_inc(t_copied, FREE)
                    pe.sem_inc(a_copied, FREE)
                    for b in range(B):
                        with pe.Fori(0, CB // 2) as i:
                            for s in range(2):
                                c = 2 * i + s
                                t = 2 * i + (s + b * CB)
                                pe.wait_ge(uf_ready, t + 1)
                                pe.wait_ge(t_copied, t + 1)
                                for par in range(2):
                                    for j in range(2):
                                        mm = pe.transpose(ps_t[s][:, par, j, :],
                                                          uf[s][:, (2 * P + 1) - 2 * P * j - par:(4 * P) - 2 * P * j - par:2], cm("ident"))
                                mm.then_inc(t_mul, 1)
                                pe.wait_ge(up_ready, t + 1)
                                pe.wait_ge(a_copied, t + 1)
                                for a in range(AR):
                                    mm = pe.matmul(ps_a[s][:, :], mu[:, a, :], upad[:, b, bass.ds(c * CH + (4 - a), CH)],
                                                   start=(a == 0), stop=(a == AR - 1))
                                mm.then_inc(a_mul, 1)

                @block.scalar
                def _(act):
                    for b in range(B):
                        with act.Fori(0, CB // 2) as i:
                            for s in range(2):
                                c = 2 * i + s
                                t = 2 * i + (s + b * CB)
                                act.wait_ge(t_mul, t + (1 + FREE))
                                act.activation(utok[:, b, :, bass.ds(c * 2, 2), :], ps_t[s][:, :, :, :],
                                               ACT.Copy).then_inc(t_copied, 1)
        with ExitStack() as inner:
            p2 = Place(nc, inner)
            even = [p2.sb(f"even{s}", [P, T2]) for s in range(2)]
            odd = [p2.sb(f"odd{s}", [P, T2 + 1]) for s in range(2)]
            mk = [p2.sb(f"mk{s}", [P, 2, P]) for s in range(2)]
            yk = [p2.sb(f"yk{s}", [P, 2, CH]) for s in range(2)]
            ps_y = [p2.ps(f"sps_y{s}", [P, 2, CH]) for s in range(2)]
            ps_o = [p2.ps(f"sps_o{s}", [P, CH]) for s in range(2)]
            strips_loaded = [p2.sem(f"strips_loaded{s}") for s in range(2)]
            mk_ready = p2.sem("mk_ready")
            k_done = p2.sem("k_done")
            y_mul = p2.sem("s_y_mul")
            ye_copied = p2.sem("s_ye_copied")
            yo_copied = p2.sem("s_yo_copied")
            o_mul = p2.sem("s_o_mul")
            o_added = p2.sem("s_o_added")
            x_added = p2.sem("s_x_added")
            units = [(b, par, c) for b in range(B) for par in range(2) for c in range(T2 // CH)]
            UN = len(units)
            PW = T2 + P + 1
            phi = d["phi"]
            with nc.Block() as block:
                @block.sync
                def _(sp):
                    sp.sem_inc(k_done, FREE)
                    with sp.Fori(0, K // 2) as i:
                        for s in range(2):
                            k = 2 * i + s
                            sp.wait_ge(k_done, k + 1)
                            for tile, par, off, w in ((even[s], 0, 2, T2), (odd[s], 1, 1, T2 + 1)):
                                row = phi[bass.ds(k, 1), par * PW + off:par * PW + off + w]
                                src = bass.AP(tensor=row.tensor, offset=row.offset, ap=[[1, P], [1, w]])
                                sp.dma_start(tile[:, :], src).then_inc(strips_loaded[s], 16)

                @block.tensor
                def _(pe):
                    pe.sem_inc(ye_copied, FREE)
                    pe.sem_inc(yo_copied, FREE)
                    pe.sem_inc(o_added, FREE)
                    with pe.Fori(0, K // 2) as i:
                        for s in range(2):
                            k = 2 * i + s

                            def mix(n):
                                pe.wait_ge(ye_copied, k * UN + (n + 1 + FREE))
                                pe.wait_ge(yo_copied, k * UN + (n + 1 + FREE))
                                pe.wait_ge(o_added, k * UN + (n + 1))
                                if n == 0:
                                    pe.wait_ge(mk_ready, k + 1)
                                for par in range(2):
                                    mm = pe.matmul(ps_o[n % 2][:, :], mk[s][:, par, :], yk[n % 2][:, par, :],
                                                   start=(par == 0), stop=(par == 1))
                                mm.then_inc(o_mul, 1)

                            pe.wait_ge(strips_loaded[s], i * 32 + 32)
                            for n, (b, par, c) in enumerate(units):
                                pe.wait_ge(ye_copied, k * UN + (n + 1))
                                pe.wait_ge(yo_copied, k * UN + (n + 1))
                                tiles = 4 * c + 4
                                for j in range(tiles):
                                    lo = max(0, (j - 4 * c) * P)
                                    at = c * CH - j * P + lo
                                    w = CH - lo
                                    pe.matmul(ps_y[n % 2][:, 0, lo:CH], utok[:, b, par, j, :], even[s][:, at:at + w],
                                              start=(j == 0), stop=(j == tiles - 1))
                                for j in range(tiles):
                                    lo = max(0, (j - 4 * c) * P)
                                    at = c * CH - j * P + lo + par
                                    w = CH - lo
                                    mm = pe.matmul(ps_y[n % 2][:, 1, lo:CH], utok[:, b, 1 - par, j, :],
                                                   odd[s][:, at:at + w], start=(j == 0), stop=(j == tiles - 1))
                                mm.then_inc(y_mul, 1)
                                if n:
                                    mix(n - 1)
                            mix(UN - 1)

                @block.scalar
                def _(act):
                    act.sem_inc(o_mul, FREE * UN)
                    with act.Fori(0, K // 2) as i:
                        for s in range(2):
                            k = 2 * i + s
                            act.wait_ge(o_mul, k * UN + UN)
                            act.activation(mk[s][:, :, :], msel[:, bass.ds(k, 1), :, :].rearrange("p o a e -> p (o a) e"),
                                           ACT.Copy).then_inc(mk_ready, 1)
                            for n in range(UN):
                                act.wait_ge(y_mul, k * UN + (n + 1))
                                act.activation(yk[n % 2][:, 0, :], ps_y[n % 2][:, 0, :], ACT.Copy).then_inc(ye_copied, 1)

                @block.vector
                def _(dve):
                    with dve.Fori(0, K // 2) as i:
                        for s in range(2):
                            k = 2 * i + s

                            def add(n):
                                dve.wait_ge(o_mul, k * UN + (n + 1 + FREE * UN))
                                b, par, c = units[n]
                                at = b * L + 2 * c * CH + par
                                part = acc[:, at:at + 2 * CH - par:2]
                                dve.tensor_tensor(part, part, ps_o[n % 2][:, :], ALU.add).then_inc(o_added, 1)

                            for n in range(UN):
                                dve.wait_ge(y_mul, k * UN + (n + 1))
                                if n == UN - 1:
                                    dve.sem_inc(k_done, 1)
                                dve.tensor_copy(yk[n % 2][:, 1, :], ps_y[n % 2][:, 1, :]).then_inc(yo_copied, 1)
                                if n:
                                    add(n - 1)
                            add(UN - 1)
                    dve.wait_ge(o_added, K * UN + FREE)
                    with dve.Fori(0, CB) as c:
                        for b in range(B):
                            x = xt[:, bass.ds(c * CH + b * L, CH)]
                            dve.scalar_tensor_tensor(x, acc[:, bass.ds(c * CH + b * L, CH)], gain[:, bass.ds(c, 1)], x,
                                                     ALU.mult, ALU.add).then_inc(x_added, 1)


def additive_attention(nc, xt, cm, we, u):
    A, R = 16, 8
    QB = P // R
    TI = L // P
    SEG = 8
    ST = TI // SEG
    TS = 4
    with ExitStack() as ctx:
        p = Place(nc, ctx)
        g_rep = p.sb("g_rep", [P, B, L])
        f_bias = p.sb("f_bias", [P, B, L // R])
        xtok = p.sb("xtok", [P, B * TI, P + 1])
        w2 = p.sb("w2", [P, R])
        with ExitStack() as inner:
            p2 = Place(nc, inner)
            uf = [p2.sb(f"auf{s}", [P, CH]) for s in range(2)]
            fm = [p2.sb(f"fm{s}", [P, CH // R, R]) for s in range(2)]
            ps_g = [p2.ps(f"aps_g{s}", [P, CH]) for s in range(2)]
            ps_f = [p2.ps(f"aps_f{s}", [P, CH]) for s in range(2)]
            ps_t = [p2.ps(f"aps_t{s}", [P, CH]) for s in range(2)]
            const_ready = p2.sem("a3_const")
            uf_ready = p2.sem("a_uf_ready")
            mul_ready = p2.sem("a_mul_ready")
            t_copied = p2.sem("a_t_copied")
            fm_ready = p2.sem("fm_ready")
            f_summed = p2.sem("f_summed")
            f_ready = p2.sem("f_ready")
            f_flat = f_bias[:, :, :].rearrange("p b n -> p (b n)")
            g_flat = g_rep[:, :, :].rearrange("p b n -> p (b n)")
            with nc.Block() as block:
                @block.vector
                def _(dve):
                    dve.memset(xtok[:, :, P:P + 1], 1.0).then_inc(const_ready, 1)
                    dve.tensor_scalar(w2[:, :], cm("row8"), we("w2", 0), None, ALU.mult).then_inc(const_ready, 1)
                    dve.sem_inc(mul_ready, FREE)
                    row = [list(x) for x in cm("row8").ap]
                    pick = bass.AP(tensor=cm("row8").tensor, offset=cm("row8").offset,
                                   ap=[row[0], [0, CH // R], row[1]])
                    with dve.Fori(0, NC // 2) as i:
                        for s in range(2):
                            t = 2 * i + s
                            dve.wait_ge(mul_ready, t + 1)
                            dve.tensor_copy(uf[s][:, :], u[:, bass.ds(t * CH, CH)]).then_inc(uf_ready, 1)
                        for s in range(2):
                            t = 2 * i + s
                            dve.wait_ge(mul_ready, t + (1 + FREE))
                            dve.tensor_tensor(fm[s][:, :, :], ps_f[s][:, :].rearrange("p (n r) -> p n r", r=R), pick,
                                              ALU.mult).then_inc(fm_ready, 1)
                        for s in range(2):
                            t = 2 * i + s
                            dve.wait_ge(fm_ready, t + 1)
                            dve.tensor_reduce(f_flat[:, bass.ds(t * (CH // R), CH // R)], fm[s][:, :, :], AX_X,
                                              ALU.add).then_inc(f_summed, 1)
                    dve.wait_ge(f_summed, NC)
                    dve.tensor_scalar(f_flat, f_flat, we("b1", 0), None, ALU.add).then_inc(f_ready, 1)

                @block.tensor
                def _(pe):
                    pe.sem_inc(t_copied, FREE)
                    with pe.Fori(0, NC // 2) as i:
                        for s in range(2):
                            t = 2 * i + s
                            pe.wait_ge(uf_ready, t + 1)
                            pe.wait_ge(t_copied, t + 1)
                            for j in range(CH // P):
                                pe.transpose(ps_t[s][:, j * P:(j + 1) * P], uf[s][:, j * P:(j + 1) * P], cm("ident"))
                            pe.matmul(ps_g[s][:, :], we("w1g", 0, P), uf[s][:, :], start=True, stop=True)
                            pe.matmul(ps_f[s][:, :], we("w1f", 0, P), uf[s][:, :], start=True, stop=True)\
                                .then_inc(mul_ready, 1)

                @block.scalar
                def _(act):
                    with act.Fori(0, NC // 2) as i:
                        for s in range(2):
                            t = 2 * i + s
                            act.wait_ge(mul_ready, t + (1 + FREE))
                            act.activation(g_flat[:, bass.ds(t * CH, CH)], ps_g[s][:, :], ACT.Copy)
                            act.activation(xtok[:, bass.ds(t * 4, 4), 0:P],
                                           ps_t[s][:, :].rearrange("p (j c) -> p j c", c=P), ACT.Copy)\
                                .then_inc(t_copied, 1)
        acc = p.sb("a_acc", [P, B * TI, P + 1])
        with ExitStack() as inner:
            p2 = Place(nc, inner)
            th = [p2.sb(f"th{s}", [P, SEG * P]) for s in range(TS)]
            et = [p2.sb(f"et{s}", [P, SEG, P]) for s in range(2)]
            ps_s = [p2.ps(f"ps_s{s}", [P, SEG, P]) for s in range(2)]
            ps_o = [p2.ps(f"aps_o{s}", [P, CH]) for s in range(2)]
            tanh_ready = p2.sem("tanh_ready")
            scored = p2.sem("scored")
            e_ready = p2.sem("ae_ready")
            e_masked = p2.sem("e_masked")
            o_mul = p2.sem("ao_mul")
            o_added = p2.sem("ao_added")

            def units(eng, diagonal, full):
                with eng.Fori(0, B * ST) as bq:
                    for r in range(SEG):
                        diagonal(bq * SEG + r, bq * SEG + r, r + 1, r % 2, bq * SEG)
                x0 = B * TI
                for seg in range(ST - 1):
                    n = TI - SEG * (seg + 1)
                    with eng.Fori(0, B) as b:
                        with eng.Fori(0, n // 2) as i:
                            for s in range(2):
                                full(2 * i + b * n + (x0 + s), 2 * i + b * TI + (SEG * (seg + 1) + s), s,
                                     b * TI + seg * SEG)
                    x0 += B * n

            with nc.Block() as block:
                @block.scalar
                def _(act):
                    act.preload_act_table(ACT.Tanh)
                    act.sem_inc(scored, TS)
                    act.sem_inc(o_mul, FREE)
                    f_flat = f_bias[:, :, :].rearrange("p b n -> p (b n)")
                    g_flat = g_rep[:, :, :].rearrange("p b n -> p (b n)")

                    def unit(x, tile, m, s, key0):
                        for q in range(QB):
                            act.wait_ge(scored, x * QB + (q + 1))
                            act.activation(th[q % TS][:, 0:m * P], g_flat[:, bass.ds(key0 * P, m * P)], ACT.Tanh,
                                           bias=f_flat[:, bass.ds(tile * QB + q, 1)]).then_inc(tanh_ready, 1)
                        act.wait_ge(scored, x * QB + (QB + TS))
                        act.wait_ge(o_mul, x + 1)
                        act.activation(et[s][:, 0:m, :], ps_s[s][:, 0:m, :], ACT.Exp,
                                       bias=we("b2", 0)).then_inc(e_ready, 1)

                    units(act, lambda x, tile, m, s, key0: unit(x, tile, m, s, key0),
                          lambda x, tile, s, key0: unit(x, tile, SEG, s, key0))

                @block.tensor
                def _(pe):
                    pe.sem_inc(e_ready, FREE)
                    pe.sem_inc(o_added, FREE)

                    def unit(x, tile, m, s, key0, diagonal):
                        pe.wait_ge(e_ready, x + 1)
                        for q in range(QB):
                            pe.wait_ge(tanh_ready, x * QB + (q + 1))
                            for j in range(m):
                                mm = pe.matmul(ps_s[s][:, j, q * R:(q + 1) * R], th[q % TS][:, j * P:(j + 1) * P],
                                               w2[:, :], start=True, stop=True)
                            mm.then_inc(scored, 1)
                        if diagonal:
                            pe.wait_ge(e_masked, x + 1)
                        pe.wait_ge(e_ready, x + (1 + FREE))
                        pe.wait_ge(o_added, x + 1)
                        for j in range(m):
                            mm = pe.matmul(ps_o[s][:, 0:P + 1], et[s][:, j, :],
                                           xtok[:, bass.ds(key0 + j, 1), :].rearrange("p a c -> p (a c)"),
                                           start=(j == 0), stop=(j == m - 1))
                        mm.then_inc(o_mul, 1)

                    units(pe, lambda x, tile, m, s, key0: unit(x, tile, m, s, key0, True),
                          lambda x, tile, s, key0: unit(x, tile, SEG, s, key0, False))

                @block.vector
                def _(dve):
                    def diagonal(x, tile, m, s, key0):
                        dve.wait_ge(e_ready, x + (1 + FREE))
                        dve.tensor_tensor(et[s][:, m - 1, :], et[s][:, m - 1, :], cm("later"),
                                          ALU.mult).then_inc(e_masked, 1)
                        dve.wait_ge(o_mul, x + (1 + FREE))
                        dve.tensor_copy(acc[:, bass.ds(tile, 1), :].rearrange("p a c -> p (a c)"),
                                        ps_o[s][:, 0:P + 1]).then_inc(o_added, 1)

                    def full(x, tile, s, key0):
                        dve.wait_ge(o_mul, x + (1 + FREE))
                        dve.wait_ge(o_added, x + FREE)
                        part = acc[:, bass.ds(tile, 1), :].rearrange("p a c -> p (a c)")
                        dve.tensor_tensor(part, part, ps_o[s][:, 0:P + 1], ALU.add).then_inc(o_added, 1)

                    units(dve, diagonal, full)
        with ExitStack() as inner:
            p2 = Place(nc, inner)
            rden = p2.sb("rden", [P, B * TI])
            wn = [p2.sb(f"wn{s}", [P, CH // P, P]) for s in range(2)]
            ps_x = [p2.ps(f"aps_x{s}", [P, CH]) for s in range(2)]
            den_step = p2.sem("den_step")
            wn_ready = p2.sem("wn_ready")
            x_mul = p2.sem("ax_mul")
            x_added = p2.sem("ax_added")
            with nc.Block() as block:
                @block.vector
                def _(dve):
                    link = Steps(dve, den_step)
                    link(dve.tensor_scalar(rden[:, :], acc[:, :, P], 1e-10, None, ALU.add))
                    link(dve.reciprocal(rden[:, :], rden[:, :]))
                    with dve.Fori(0, NC // 2) as i:
                        for s in range(2):
                            t = 2 * i + s
                            part = rden[:, bass.ds(t * 4, 4)]
                            dve.tensor_tensor(wn[s][:, :, :], acc[:, bass.ds(t * 4, 4), 0:P], inside(part, P),
                                              ALU.mult).then_inc(wn_ready, 1)
                        for s in range(2):
                            t = 2 * i + s
                            dve.wait_ge(x_mul, t + 1)
                            x = xt[:, bass.ds(t * CH, CH)]
                            dve.tensor_tensor(x, x, ps_x[s][:, :], ALU.add).then_inc(x_added, 1)

                @block.tensor
                def _(pe):
                    with pe.Fori(0, NC // 2) as i:
                        for s in range(2):
                            t = 2 * i + s
                            pe.wait_ge(wn_ready, t + 1)
                            for j in range(CH // P):
                                mm = pe.transpose(ps_x[s][:, j * P:(j + 1) * P], wn[s][:, j, :], cm("ident"))
                            mm.then_inc(x_mul, 1)


def expert_ffn(nc, xt, cm, wf, u, out):
    E, J, T = 8, CH // P, N // P
    with ExitStack() as ctx:
        p = Place(nc, ctx)
        lg = p.sb("lg", [P, T, E])
        wt = p.sb("wt", [P, T, E])
        with ExitStack() as inner:
            p2 = Place(nc, inner)
            hot = p2.sb("f_hot", [P, T, E])
            hot2 = p2.sb("f_hot2", [P, T, E])
            sc = p2.sb("f_sc", [P, T, E])
            m1 = p2.sb("f_m1", [P, T])
            m2 = p2.sb("f_m2", [P, T])
            mx = p2.sb("f_mx", [P, T])
            uf = [p2.sb(f"fuf{s}", [P, CH]) for s in range(2)]
            ps_l = [p2.ps(f"ps_l{s}", [P, J, E]) for s in range(2)]
            uf_ready = p2.sem("f_uf_ready")
            l_mul = p2.sem("l_mul")
            l_ready = p2.sem("l_ready")
            step = p2.sem("f_step")
            shifted = p2.sem("f_shifted")
            expd = p2.sem("f_expd")
            rb = wf("router_b", 0, E)
            with nc.Block() as block:
                @block.scalar
                def _(act):
                    act.wait_ge(shifted, 1)
                    act.activation(lg[:, :, :], lg[:, :, :], ACT.Exp).then_inc(expd, 1)

                @block.tensor
                def _(pe):
                    with pe.Fori(0, NC // 2) as i:
                        for s in range(2):
                            t = 2 * i + s
                            pe.wait_ge(uf_ready, t + 1)
                            for j in range(J):
                                mm = pe.matmul(ps_l[s][:, j, :], uf[s][:, j * P:(j + 1) * P], wf("router", 0, E),
                                               start=True, stop=True)
                            mm.then_inc(l_mul, 1)

                @block.vector
                def _(dve):
                    with dve.Fori(0, NC // 2) as i:
                        for s in range(2):
                            t = 2 * i + s
                            dve.tensor_copy(uf[s][:, :], u[:, bass.ds(t * CH, CH)]).then_inc(uf_ready, 1)
                        for s in range(2):
                            t = 2 * i + s
                            dve.wait_ge(l_mul, t + 1)
                            dve.tensor_tensor(lg[:, bass.ds(t * J, J), :], ps_l[s][:, :, :], halves(rb, J),
                                              ALU.add).then_inc(l_ready, 1)
                    dve.wait_ge(l_ready, NC)
                    link = Steps(dve, step)
                    link(dve.tensor_reduce(mx[:, :], lg[:, :, :], AX_X, ALU.max))
                    dve.tensor_tensor(lg[:, :, :], lg[:, :, :], inside(mx[:, :], E), ALU.subtract).then_inc(shifted, 1)
                    dve.wait_ge(expd, 1)
                    link(dve.tensor_reduce(mx[:, :], lg[:, :, :], AX_X, ALU.add))
                    link(dve.reciprocal(mx[:, :], mx[:, :]))
                    link(dve.tensor_tensor(lg[:, :, :], lg[:, :, :], inside(mx[:, :], E), ALU.mult))
                    link(dve.tensor_copy(wt[:, :, :], lg[:, :, :]))
                    for m, one in ((m1, hot), (m2, hot2)):
                        link(dve.tensor_reduce(m[:, :], wt[:, :, :], AX_X, ALU.max))
                        link(dve.tensor_tensor(sc[:, :, :], wt[:, :, :], inside(m[:, :], E), ALU.is_ge))
                        link(dve.tensor_tensor(sc[:, :, :], sc[:, :, :], halves(cm("rank8"), T), ALU.mult))
                        link(dve.tensor_reduce(mx[:, :], sc[:, :, :], AX_X, ALU.max))
                        link(dve.tensor_tensor(one[:, :, :], sc[:, :, :], inside(mx[:, :], E), ALU.is_equal))
                        if m is m1:
                            link(dve.scalar_tensor_tensor(wt[:, :, :], one[:, :, :], -2.0, wt[:, :, :],
                                                          ALU.mult, ALU.add))
                    link(dve.tensor_tensor(mx[:, :], m1[:, :], m2[:, :], ALU.add))
                    link(dve.reciprocal(mx[:, :], mx[:, :]))
                    link(dve.tensor_tensor(hot[:, :, :], hot[:, :, :], hot2[:, :, :], ALU.add))
                    link(dve.tensor_tensor(wt[:, :, :], hot[:, :, :], lg[:, :, :], ALU.mult))
                    link(dve.tensor_tensor(wt[:, :, :], wt[:, :, :], inside(mx[:, :], E), ALU.mult))
        with ExitStack() as inner:
            p2 = Place(nc, inner)
            uf = [p2.sb(f"guf{s}", [P, CH]) for s in range(2)]
            xf = [p2.sb(f"gxf{s}", [P, CH]) for s in range(2)]
            w1 = [p2.sb(f"gw{s}", [P, J, E]) for s in range(2)]
            wts = [p2.sb(f"gwt{s}", [E, CH]) for s in range(2)]
            xr = [p2.sb(f"gxr{s}", [P, J, P]) for s in range(2)]
            o = [p2.sb(f"go{s}", [P, J, P]) for s in range(2)]
            ps_e = [p2.ps(f"ps_e{s}", [P, 2, CH]) for s in range(2)]
            ps_w = p2.ps("ps_w", [E, CH])
            ps_r = [p2.ps(f"ps_r{s}", [P, J, P]) for s in range(2)]
            fixed = p2.sem("g_fixed")
            w_mul = p2.sem("gw_mul")
            w_copied = p2.sem("gw_copied")
            r_mul = p2.sem("gr_mul")
            r_copied = p2.sem("gr_copied")
            e_mul = p2.sem("ge_mul")
            e_used = p2.sem("ge_used")
            step = p2.sem("g_step")
            o_stored = [p2.sem(f"go_stored{s}") for s in range(2)]
            o_ready = p2.sem("go_ready")
            with nc.Block() as block:
                @block.tensor
                def _(pe):
                    pe.sem_inc(e_used, FREE)
                    with pe.Fori(0, NC // 2) as i:
                        for s in range(2):
                            t = 2 * i + s
                            pe.wait_ge(fixed, 3 * t + 3)
                            pe.wait_ge(w_copied, t)
                            for j in range(J):
                                mm = pe.transpose(ps_w[:, j * P:(j + 1) * P], w1[s][:, j, :], cm("ident"))
                            mm.then_inc(w_mul, 1)
                            pe.wait_ge(w_copied, t + 1)
                            for j in range(J):
                                some = slice(j * P, (j + 1) * P)
                                pe.matmul(ps_r[s][:, j, :], xf[s][:, some], cm("ident"), start=True, stop=False)
                                mm = pe.matmul(ps_r[s][:, j, :], wts[s][:, some], wf("expert_b", 0, P)[0:E, :],
                                               start=False, stop=True)
                            mm.then_inc(r_mul, 1)
                            for j in range(J):
                                pe.wait_ge(e_used, t * J + (j + 1))
                                for h in range(2):
                                    mm = pe.matmul(ps_e[j % 2][:, h, :], uf[s][:, j * P:(j + 1) * P],
                                                   wf("expert_w", h * CH, CH), start=True, stop=True)
                                mm.then_inc(e_mul, 1)

                @block.scalar
                def _(act):
                    act.sem_inc(e_mul, FREE * J)
                    act.sem_inc(r_mul, FREE)
                    with act.Fori(0, NC // 2) as i:
                        for s in range(2):
                            t = 2 * i + s
                            act.wait_ge(e_mul, t * J + J)
                            act.wait_ge(r_mul, t + 1)
                            act.activation(uf[s][:, :], u[:, bass.ds(t * CH, CH)], ACT.Copy).then_inc(fixed, 1)
                            act.activation(xf[s][:, :], xt[:, bass.ds(t * CH, CH)], ACT.Copy).then_inc(fixed, 1)
                            act.wait_ge(o_ready, t + 1)
                            act.activation(w1[s][:, :, :], wt[:, bass.ds(t * J, J), :], ACT.Copy).then_inc(fixed, 1)
                            act.wait_ge(w_mul, t + 1)
                            act.activation(wts[s][:, :], ps_w[:, :], ACT.Copy).then_inc(w_copied, 1)
                            act.wait_ge(r_mul, t + (1 + FREE))
                            act.activation(xr[s][:, :, :], ps_r[s][:, :, :], ACT.Copy).then_inc(r_copied, 1)

                @block.vector
                def _(dve):
                    dve.sem_inc(o_ready, FREE)
                    for s in range(2):
                        dve.sem_inc(o_stored[s], 16)
                    with dve.Fori(0, NC // 2) as i:
                        for s in range(2):
                            t = 2 * i + s
                            dve.wait_ge(r_copied, t + 1)
                            dve.wait_ge(o_stored[s], i * 16 + 16)
                            for j in range(J):
                                dve.wait_ge(e_mul, t * J + (j + 1 + FREE * J))
                                link = Steps(dve, step, (t * J + j) * (E - 1))
                                for e in range(E):
                                    ins = dve.scalar_tensor_tensor(
                                        o[s][:, j, :], ps_e[j % 2][:, e // 4, (e % 4) * P:(e % 4 + 1) * P],
                                                    w1[s][:, j, e:e + 1], xr[s][:, j, :] if e == 0 else o[s][:, j, :],
                                        ALU.mult, ALU.add)
                                    if e < E - 1:
                                        link(ins)
                                ins.then_inc(e_used, 1)
                            dve.wait_ge(e_used, t * J + (J + FREE))
                            dve.sem_inc(o_ready, 1)

                @block.sync
                def _(sp):
                    with sp.Fori(0, NC // 2) as i:
                        for s in range(2):
                            t = 2 * i + s
                            sp.wait_ge(o_ready, t + (1 + FREE))
                            sp.dma_start(out[bass.ds(t * CH, CH), :].rearrange("(j p) c -> p j c", p=P),
                                         o[s][:, :, :]).then_inc(o_stored[s], 16)
                    for s in range(2):
                        sp.wait_ge(o_stored[s], 16 * (NC // 2) + 16)


def pack(parts):
    import numpy as np
    at, n = {}, 0
    for name, a in parts:
        at[name] = (n, a.shape[1])
        n += a.shape[1]
    return np.ascontiguousarray(np.concatenate([a for _, a in parts], axis=1)), at


def getter(tensor, at):
    def get(name, i=None, n=1):
        o, w = at[name]
        return tensor[:, o:o + w] if i is None else tensor[:, o + i:o + i + n]
    return get


def constants():
    import numpy as np
    f = np.float32
    i = np.arange(P)
    parts = [
        ("ident", np.eye(P, dtype=f)),
        ("gmat", ((i[:, None] // 4) == (i[None, :] // 4)).astype(f) / 4),
        ("ones128", np.full((P, P), 1 / 128, f)),
        ("ones256", np.full((P, P), 1 / 256, f)),
        ("heads", ((i[:, None] // 32) == (i[None, :] // 32)).astype(f)),
        ("later", (i[None, :] > i[:, None]).astype(f)),
        ("row8", ((i[:, None] % 8) == np.arange(8)[None, :]).astype(f)),
        ("rank8", np.broadcast_to(8 - np.arange(8, dtype=f), (P, 8))),
        ("eps", np.full((P, 1), 1e-5, f)),
        ("ones", np.ones((P, P), f)),
    ]
    return pack(parts)


def columns(**arrays):
    return list(arrays.items())


def layouts(a):
    import numpy as np

    def per_half(v):
        v = v.reshape(2, P, -1)
        return np.concatenate([v[0], v[1]], axis=1)

    def every(v):
        return np.broadcast_to(v.reshape(1, -1), (P, v.size))

    x_cm = np.ascontiguousarray(a["x"].reshape(N, P).T)
    xp = a["L0_conv_x_proj_w"]
    bc, dt = xp[:, 8:40], xp[:, 0:8]
    xproj = np.concatenate([bc, bc, bc, dt], axis=1)
    xproj = xproj.reshape(KD, 104, 2, P).transpose(3, 0, 2, 1)
    dtw = a["L0_conv_dt_w"].transpose(2, 0, 1).reshape(8, KD * 256)
    wa, wa_at = pack(columns(
        win=a["L0_conv_w_in"].T,
        conv_w=per_half(a["L0_conv_conv_w"].reshape(256, 9)),
        conv_b=per_half(a["L0_conv_conv_b"]),
        dt_b=a["L0_conv_dt_b"].reshape(KD * 2, P).T,
        a_log=a["L0_conv_A_logs"].reshape(KD * 2, P, NS).transpose(1, 0, 2).reshape(P, KD * 2 * NS),
        d_skip=a["L0_conv_Ds"].reshape(KD * 2, P).T,
        ln_w=per_half(a["L0_conv_ln_w"]), ln_b=per_half(a["L0_conv_ln_b"]),
        wout=per_half(a["L0_conv_w_out"].T),
    ))
    wb, wb_at = pack(columns(
        w_exp=a["L1_conv_W_exp"].T, b_exp=a["L1_conv_b_exp"].reshape(2, P).T,
        w_con=a["L1_conv_W_con"].T, b_con=a["L1_conv_b_con"].reshape(1, P).T,
    ))
    qkv = a["L2_attn_W_qkv"].T
    col = lambda v: v.reshape(1, P).T
    wc, wc_at = pack(columns(
        w_q=qkv[:, 0:P], w_k=qkv[:, P:2 * P], w_v=qkv[:, 2 * P:3 * P], w_o=a["L2_attn_W_out"].T,
        b_out=col(a["L2_attn_b_out"]), gn_w=col(a["L2_attn_gn_w"]), gn_b=col(a["L2_attn_gn_b"]),
    ))
    wd, wd_at = pack(columns(
        sigma=every(a["L2_ffn_sigma"]), logw=every(a["L2_ffn_log_weights"]), gumbel=every(a["L2_ffn_gumbel"]),
    ))
    w1, eight = a["L3_attn_W1"], 8
    we, we_at = pack(columns(
        w1f=np.repeat(w1[:P], eight, axis=1), w1g=np.repeat(w1[P:], eight, axis=1),
        b1=np.repeat(a["L3_attn_b1"], eight)[:, None], w2=np.repeat(a["L3_attn_w2"][:, 0], eight)[:, None],
        b2=every(a["L3_attn_b2"]),
    ))
    wf, wf_at = pack(columns(
        router=a["L3_ffn_router_w"], router_b=every(a["L3_ffn_router_b"]),
        expert_w=a["L3_ffn_expert_w"].transpose(1, 0, 2).reshape(P, 8 * P),
        expert_b=np.concatenate([a["L3_ffn_expert_b"], np.zeros((P - 8, P), np.float32)]),
    ))
    phi = np.zeros((16, 2, L // 2 + P + 1), np.float32)
    phi[:, :, P + 1:] = a["L2_ffn_phi"].reshape(L // 2, 2, 16).transpose(2, 1, 0)
    more = {"wc": wc, "wd": wd, "we": we, "wf": wf, "phi": phi.reshape(16, -1),
            "m_u": a["L2_ffn_M_u"].transpose(2, 0, 1, 3).reshape(P, -1),
            "m_plus": a["L2_ffn_M_phi_plus"].transpose(2, 0, 1, 3).reshape(P, -1),
            "m_minus": a["L2_ffn_M_phi_minus"].transpose(2, 0, 1, 3).reshape(P, -1)}
    sel = np.zeros((96, 32, P), np.float32)
    for n in range(32):
        sel[n::32, n, :] = 1
    cmn, cmn_at = constants()
    arrays = {"x_cm": x_cm, "common": cmn, "wa": wa, "wb": wb,
              "xproj": np.ascontiguousarray(xproj.reshape(P, -1)), "dtw": np.ascontiguousarray(dtw),
              "sel": sel.reshape(96, -1)}
    arrays.update({n: np.ascontiguousarray(v) for n, v in more.items()})
    return arrays, {"common": cmn_at, "wa": wa_at, "wb": wb_at, "wc": wc_at, "wd": wd_at, "we": we_at, "wf": wf_at}


def load(nc, pairs, name):
    with ExitStack() as ctx:
        p = Place(nc, ctx)
        loaded = p.sem(name + "_loaded")
        with nc.Block() as block:
            @block.sync
            def _(sp):
                for tile, array in pairs:
                    sp.dma_start(tile, array).then_inc(loaded, 16)
                sp.wait_ge(loaded, 16 * len(pairs))


def store_cm(nc, xt, dram, name):
    with ExitStack() as ctx:
        p = Place(nc, ctx)
        stored = p.sem(name + "_stored")
        with nc.Block() as block:
            @block.sync
            def _(sp):
                sp.dma_start(dram, xt[:, :]).then_inc(stored, 16)
                sp.wait_ge(stored, 16)


def scan_layer(nc, cm, d, at, gscale, gshift):
    with ExitStack() as ctx:
        p = Place(nc, ctx)
        wat = p.sb("wa_sb", list(d["wa"].shape))
        wa = getter(wat, at["wa"])
        y = p.sb("y", [P, 2, B, HH, WW])
        load(nc, [(wat[:, :], d["wa"])], "wa")
        with ExitStack() as inner:
            p2 = Place(nc, inner)
            xc = p2.sb("xc", [P, 2, B, HH, WW])
            xt = y[:, 0].rearrange("p b h w -> p (b h w)")
            wide_sel = y[0:96, 1, 0].rearrange("p h w -> p (h w)")
            load_residual(nc, xt, d["x_cm"], "l0")
            group_stats(nc, xt, cm, gscale, gshift, "gn0")
            conv_branch(nc, xt, cm, wa, gscale, gshift, xc)
            sel = p2.sb("sel_sb", [96, 2 * NS, P], BF16)
            xproj = p2.sb("xproj_sb", [P, KD, 2, 104])
            dtw = p2.sb("dtw_sb", [P, KD, 2 * P])
            sel_cast = p2.sem("sel_cast")
            load(nc, [(wide_sel, d["sel"]), (xproj[:, :, :, :].rearrange("p k f r -> p (k f r)"), d["xproj"]),
                      (dtw[96:104, :, :].rearrange("p k c -> p (k c)"), d["dtw"])], "scan_w")
            with nc.Block() as block:
                @block.vector
                def _(dve):
                    dve.tensor_copy(sel[:, :, :].rearrange("p n m -> p (n m)"), wide_sel).then_inc(sel_cast, 1)
            selective_scan(nc, cm, wa, sel, xproj, dtw, xc, y)
        z = p.sb("z", [P, 2, N])
        xt = p.sb("xt0", [P, N])
        load_residual(nc, xt, d["x_cm"], "l0b")
        gated_output(nc, xt, cm, wa, gscale, gshift, y, z)
        store_cm(nc, xt, d["spill"], "l0c")


def build(nc, d, at, out):
    with ExitStack() as top:
        p = Place(nc, top)
        cmt = p.sb("common_sb", list(d["common"].shape))
        cm = getter(cmt, at["common"])
        gscale = p.sb("gscale", [P, B])
        gshift = p.sb("gshift", [P, B])
        load(nc, [(cmt[:, :], d["common"])], "common")
        scan_layer(nc, cm, d, at, gscale, gshift)
        xt = p.sb("xt", [P, N])
        tiles = {name: p.sb(name + "_sb", list(d[name].shape)) for name in ("wb", "wc", "wd", "we", "wf")}
        w = {name: getter(tile, at[name]) for name, tile in tiles.items()}
        load_residual(nc, xt, d["spill"], "l1")
        load(nc, [(tile[:, :], d[name]) for name, tile in tiles.items()], "weights")
        group_stats(nc, xt, cm, gscale, gshift, "gn1")
        ema_gate(nc, xt, cm, w["wb"], gscale, gshift)
        u = p.sb("normed", [P, N])
        layer_norm(nc, xt, cm, u, "n2a")
        linear_attention(nc, xt, cm, w["wc"], u)
        layer_norm(nc, xt, cm, u, "n2f")
        spectral_ffn(nc, xt, cm, w["wd"], d, u)
        layer_norm(nc, xt, cm, u, "n3a")
        additive_attention(nc, xt, cm, w["we"], u)
        layer_norm(nc, xt, cm, u, "n3f")
        expert_ffn(nc, xt, cm, w["wf"], u, out)


def kernel(**inputs):
    import numpy as np
    import concourse.bacc as bacc
    from concourse.bass_utils import run_bass_kernel_spmd

    arrays, at = layouts({name: np.asarray(v) for name, v in inputs.items()})
    nc = bacc.Bacc("TRN2", target_bir_lowering=False, num_devices=1)
    d = {name: nc.dram_tensor(f"in_{name}_dram", v.shape, mybir.dt.from_np(v.dtype), kind="ExternalInput").ap()
         for name, v in arrays.items()}
    d["spill"] = nc.dram_tensor("residual_spill", [P, N], F32).ap()
    out = nc.dram_tensor("out_0_dram", [N, P], F32, kind="ExternalOutput").ap()
    build(nc, d, at, out)
    r = run_bass_kernel_spmd(nc, [{f"in_{name}_dram": v for name, v in arrays.items()}], core_ids=[0])
    return r.results[0]["out_0_dram"].reshape(B, HH, WW, P)
```

```python
from contextlib import ExitStack

import concourse.bass as bass
from concourse import mybir

F32 = mybir.dt.float32
BF16 = mybir.dt.bfloat16
ACT = mybir.ActivationFunctionType
ALU = mybir.AluOpType
AX_X = mybir.AxisListType.X

P = 128
B = 2
HH = WW = 64
L = HH * WW
N = B * L
CH = 512
NC = N // CH
CB = L // CH
ROWS = CH // WW
PAD = WW + 2
FREE = 2
KD = 4
NS = 16
LN_SET = "natural_log_exp_and_others"


def halves(ap, n):
    a = [list(x) for x in ap.ap]
    return bass.AP(tensor=ap.tensor, offset=ap.offset, ap=[a[0], [0, n]] + a[1:])


def inside(ap, n):
    return bass.AP(tensor=ap.tensor, offset=ap.offset, ap=[list(x) for x in ap.ap] + [[0, n]])


class Place:

    def __init__(self, nc, ctx):
        self.nc, self.ctx, self.sems = nc, ctx, []
        ctx.callback(self.clear)

    def sb(self, name, shape, dt=F32):
        return self.ctx.enter_context(self.nc.sbuf_tensor(name, shape, dt))

    def ps(self, name, shape, dt=F32):
        return self.ctx.enter_context(self.nc.psum_tensor(name, shape, dt))

    def sem(self, name):
        self.sems.append(self.nc.alloc_semaphore(name))
        return self.sems[-1]

    def clear(self):
        if self.sems:
            with self.nc.Block() as block:
                @block.gpsimd
                def _(pool):
                    for s in self.sems:
                        pool.sem_clear(s)
            for s in self.sems:
                self.nc.release_semaphore(s)


class Steps:

    def __init__(self, eng, sem, base=0):
        self.eng, self.sem, self.base, self.n = eng, sem, base, 0

    def __call__(self, ins):
        self.n += 1
        ins.then_inc(self.sem, 1)
        self.eng.wait_ge(self.sem, self.base + self.n)


def load_residual(nc, xt, x_cm, name):
    with ExitStack() as ctx:
        p = Place(nc, ctx)
        x_loaded = p.sem(name + "_x_loaded")
        with nc.Block() as block:
            @block.sync
            def _(sp):
                for q in range(4):
                    w = N // 4
                    sp.dma_start(xt[:, q * w:(q + 1) * w], x_cm[:, q * w:(q + 1) * w]).then_inc(x_loaded, 16)
                sp.wait_ge(x_loaded, 64)


def group_stats(nc, xt, cm, gscale, gshift, name):
    with ExitStack() as ctx:
        p = Place(nc, ctx)
        stats = p.sb(name + "_stats", [P, NC, 6])
        mv = p.sb(name + "_mv", [P, B, 2])
        ex = p.sb(name + "_ex", [P, B, 2])
        g = p.sb(name + "_g", [P, B, 2])
        var = p.sb(name + "_var", [P, B])
        std = p.sb(name + "_std", [P, B])
        pg = p.ps(name + "_pg", [P, CH])
        stats_ready = p.sem(name + "_stats_ready")
        step = p.sem(name + "_step")
        moments_ready = p.sem(name + "_moments_ready")
        group_ready = p.sem(name + "_group_ready")
        var_ready = p.sem(name + "_var_ready")
        std_ready = p.sem(name + "_std_ready")
        with nc.Block() as block:
            @block.vector
            def _(dve):
                with dve.Fori(0, NC) as i:
                    dve.bn_stats(stats[:, bass.ds(i, 1), :].rearrange("p a s -> p (a s)"),
                                 xt[:, bass.ds(i * CH, CH)]).then_inc(stats_ready, 1)
                dve.wait_ge(stats_ready, NC)
                link = Steps(dve, step)
                for b in range(B):
                    link(dve.bn_aggr(mv[:, b, :], stats[:, b * CB:(b + 1) * CB, :].rearrange("p a s -> p (a s)")))
                link(dve.tensor_tensor(ex[:, :, 1], mv[:, :, 0], mv[:, :, 0], ALU.mult))
                link(dve.tensor_copy(ex[:, :, 0], mv[:, :, 0]))
                dve.tensor_tensor(ex[:, :, 1], ex[:, :, 1], mv[:, :, 1], ALU.add).then_inc(moments_ready, 1)
                dve.wait_ge(group_ready, 1)
                link(dve.tensor_copy(g[:, :, :].rearrange("p b s -> p (b s)"), pg[:, 0:2 * B]))
                link(dve.tensor_tensor(var[:, :], g[:, :, 0], g[:, :, 0], ALU.mult))
                dve.tensor_tensor(var[:, :], g[:, :, 1], var[:, :], ALU.subtract).then_inc(var_ready, 1)
                dve.wait_ge(std_ready, 1)
                link(dve.reciprocal(gscale[:, :], std[:, :]))
                link(dve.scalar_tensor_tensor(gshift[:, :], g[:, :, 0], -1.0, gscale[:, :], ALU.mult, ALU.mult))

            @block.tensor
            def _(pe):
                pe.wait_ge(moments_ready, 1)
                pe.matmul(pg[:, 0:2 * B], cm("gmat"), ex[:, :, :].rearrange("p b s -> p (b s)"),
                          start=True, stop=True).then_inc(group_ready, 1)

            @block.scalar
            def _(act):
                act.wait_ge(var_ready, 1)
                act.activation(std[:, :], var[:, :], ACT.Sqrt, bias=cm("eps")).then_inc(std_ready, 1)


def conv_branch(nc, xt, cm, wa, gscale, gshift, xc):
    with ExitStack() as ctx:
        p = Place(nc, ctx)
        pad = p.sb("xi_pad", [P, B, PAD, PAD])
        diag = p.sb("conv_diag", [P, 2, 9, P])
        psx = [p.ps(f"psx{s}", [P, CH]) for s in range(2)]
        psc = [p.ps(f"psc{s}", [P, CH]) for s in range(2)]
        pad_zeroed = p.sem("pad_zeroed")
        diag_ready = p.sem("diag_ready")
        xn_ready = p.sem("xn_ready")
        xi_ready = p.sem("xi_ready")
        xi_padded = p.sem("xi_padded")
        conv_ready = p.sem("conv_ready")
        xc_ready = p.sem("xc_ready")
        with nc.Block() as block:
            @block.gpsimd
            def _(pool):
                pool.memset(pad[:, :, :, :], 0.0).then_inc(pad_zeroed, 1)

            @block.vector
            def _(dve):
                for b in range(B):
                    with dve.Fori(0, CB) as c:
                        x = xt[:, bass.ds(c * CH + b * L, CH)]
                        dve.tensor_scalar(x, x, gscale[:, b:b + 1], gshift[:, b:b + 1],
                                          ALU.mult, ALU.add).then_inc(xn_ready, 1)
                for half in range(2):
                    for tap in range(9):
                        dve.tensor_scalar(diag[:, half, tap, :], cm("ident"), wa("conv_w", 9 * half + tap), None,
                                          ALU.mult).then_inc(diag_ready, 1)
                dve.wait_ge(pad_zeroed, 1)
                for half in range(2):
                    for b in range(B):
                        if half == 1:
                            dve.wait_ge(conv_ready, (b + 1) * CB)
                        with dve.Fori(0, CB // 2) as i:
                            for s in range(2):
                                c = 2 * i + s
                                dve.wait_ge(xi_ready, c + (half * NC + b * CB + 1))
                                dve.tensor_copy(pad[:, b, bass.ds(c * ROWS + 1, ROWS), 1:1 + WW],
                                                psx[s][:, :].rearrange("p (h w) -> p h w", w=WW)).then_inc(xi_padded, 1)

            @block.tensor
            def _(pe):
                pe.sem_inc(xi_padded, FREE)
                pe.sem_inc(xc_ready, FREE)
                for half in range(2):
                    with pe.Fori(0, NC // 2) as i:
                        for s in range(2):
                            t = 2 * i + s
                            if half == 0:
                                pe.wait_ge(xn_ready, t + 1)
                            pe.wait_ge(xi_padded, t + (half * NC + 1))
                            pe.matmul(psx[s][:, :], wa("win", half * P, P), xt[:, bass.ds(t * CH, CH)],
                                      start=True, stop=True).then_inc(xi_ready, 1)
                    pe.wait_ge(diag_ready, 18)
                    for b in range(B):
                        pe.wait_ge(xi_padded, FREE + half * NC + (b + 1) * CB)
                        with pe.Fori(0, CB // 2) as i:
                            for s in range(2):
                                c = 2 * i + s
                                pe.wait_ge(xc_ready, c + (half * NC + b * CB + 1))
                                for tap in range(9):
                                    dy, dx = divmod(tap, 3)
                                    mm = pe.matmul(psc[s][:, :], diag[:, half, tap, :],
                                                   pad[:, b, bass.ds(c * ROWS + dy, ROWS), dx:dx + WW],
                                                   start=(tap == 0), stop=(tap == 8))
                                mm.then_inc(conv_ready, 1)

            @block.scalar
            def _(act):
                act.preload_act_table(ACT.Silu)
                for half in range(2):
                    with act.Fori(0, NC // 2) as i:
                        for s in range(2):
                            t = 2 * i + s
                            act.wait_ge(conv_ready, t + (half * NC + 1))
                            act.activation(xc[:, half].rearrange("p b h w -> p (b h w)")[:, bass.ds(t * CH, CH)],
                                           psc[s][:, :], ACT.Silu, bias=wa("conv_b", half)).then_inc(xc_ready, 1)


def selective_scan(nc, cm, wa, sel, xproj, dtw, xc, y):
    with ExitStack() as ctx:
        p = Place(nc, ctx)
        neg_a = p.sb("neg_a", [P, KD, 2, NS])
        d_sum = p.sb("d_sum", [P, 2])
        sq_bias = p.sb("sq_bias", [P, 1])
        split = [p.sb(f"bc_split{s}", [96, CH], BF16) for s in range(2)]
        mid = p.sb("bc_mid", [96, CH], BF16)
        rest = p.sb("bc_rest", [96, CH])
        dts = p.sb("dts", [P, CH])
        poly = p.sb("poly", [P, 2, CH])
        delta = [p.sb(f"delta{s}", [P, 2, CH]) for s in range(2)]
        u = [p.sb(f"u{s}", [P, 2, CH]) for s in range(2)]
        c_sb = [p.sb(f"c_sb{s}", [P, CH]) for s in range(2)]
        da = [p.sb(f"da{s}", [P, 2, CH]) for s in range(2)]
        dbx = [p.sb(f"dbx{s}", [P, 2, CH]) for s in range(2)]
        h = [p.sb(f"h{s}", [P, 2, CH]) for s in range(2)]
        state = p.sb("state", [P, 2, 2, NS])
        ps_xd = p.ps("ps_xd", [P, CH])
        ps_dt = p.ps("ps_dt", [P, 2, CH])
        ps_b = [p.ps(f"ps_b{s}", [P, CH]) for s in range(2)]
        ps_c = p.ps("ps_c", [P, CH])
        ps_y = p.ps("ps_y", [P, 2, CH])
        a_clamped = p.sem("a_clamped")
        d_ready = p.sem("d_ready")
        a_exp = p.sem("a_exp")
        a_ready = p.sem("a_ready")
        y_started = p.sem("y_started")
        xd_ready = p.sem("xd_ready")
        hi_ready = p.sem("hi_ready")
        dts_ready = p.sem("dts_ready")
        rest_ready = p.sem("rest_ready")
        mid_ready = p.sem("mid_ready")
        split_mid_ready = p.sem("split_mid_ready")
        split_low_ready = p.sem("split_low_ready")
        dt_ready = p.sem("dt_ready")
        abs_ready = p.sem("abs_ready")
        e_ready = p.sem("e_ready")
        ln_ready = p.sem("ln_ready")
        sq_ready = p.sem("sq_ready")
        far_ready = p.sem("far_ready")
        near_ready = p.sem("near_ready")
        log_ready = p.sem("log_ready")
        relu_ready = p.sem("relu_ready")
        delta_ready = p.sem("delta_ready")
        u_ready = p.sem("u_ready")
        b_ready = p.sem("b_ready")
        c_ready = p.sem("c_ready")
        c_copied = p.sem("c_copied")
        da_ready = p.sem("da_ready")
        dbx_ready = p.sem("dbx_ready")
        scanned = p.sem("scanned")
        state_reset = p.sem("state_reset")
        state_saved = p.sem("state_saved")
        hc_ready = p.sem("hc_ready")
        y_summed = p.sem("y_summed")
        y_added = p.sem("y_added")
        H2 = 2 * NS
        LAST = 1

        def piece(t_x, k, b, c, half=None):
            c = c if k < 2 else c * -1 + (CB - 1)
            some = bass.ds(c * ROWS, ROWS)
            if half is not None:
                v = t_x[:, half, b:b + 1, some, :] if k % 2 == 0 else t_x[:, half, b:b + 1, :, some]
                return v.rearrange("p o h w -> p (o h) w" if k % 2 == 0 else "p o h w -> p (o w) h")
            v = t_x[:, :, b:b + 1, some, :] if k % 2 == 0 else t_x[:, :, b:b + 1, :, some]
            return v.rearrange("p f o h w -> p f (o h) w" if k % 2 == 0 else "p f o h w -> p f (o w) h")

        def grid(ap):
            return ap.rearrange("p f (a b) -> p f a b", b=WW)

        def pieces(eng, prepare, work):
            G = KD * B

            def at(g, c):
                g, c = (g - 1, c + CB) if isinstance(c, int) and c < 0 else (g, c)
                g, c = (g + 1, c - CB) if isinstance(c, int) and c >= CB else (g, c)
                return (g // B, g % B, c, c + g * CB) if 0 <= g < G else None

            for n in range(NS):
                prepare(n, *at(0, 0), 0)
            for g in range(G):
                def one(c, s):
                    work(g, *at(g, c), s, at(g, c - 1), at(g, c + 1))
                one(0, 0)
                with eng.Fori(0, CB // 2 - 1) as i:
                    for s in range(2):
                        one(2 * i + (s + 1), (s + 1) % 2)
                one(CB - 1, 1)

        with nc.Block() as block:
            @block.tensor
            def _(pe):
                pe.sem_inc(rest_ready, LAST)
                pe.sem_inc(dts_ready, LAST)
                pe.sem_inc(relu_ready, LAST)
                pe.sem_inc(y_added, LAST)
                pe.sem_inc(c_copied, LAST)
                pe.sem_inc(dbx_ready, FREE)

                def prepare(n, k, b, c, t, s):
                    if n == 1:
                        pe.wait_ge(rest_ready, t + 1)
                        pe.wait_ge(dts_ready, t + 1)
                        for half in range(2):
                            mm = pe.matmul(ps_xd[0:104, :], xproj[:, k, half, :], piece(xc, k, b, c, half),
                                           start=(half == 0), stop=(half == 1))
                        mm.then_inc(xd_ready, 1)
                    if n == 3:
                        pe.wait_ge(dts_ready, t + (1 + LAST))
                        pe.wait_ge(relu_ready, t + 1)
                        for half in range(2):
                            mm = pe.matmul(ps_dt[:, half, :], dtw[96:104, k, half * P:(half + 1) * P],
                                           dts[96:104, :], start=True, stop=True)
                        mm.then_inc(dt_ready, 1)

                def add_y(n, t):
                    for half in range(2):
                        pe.wait_ge(hc_ready, t * H2 + (2 * n + half + 1 + 2 * FREE))
                        if n == 0:
                            pe.wait_ge(y_added, t + 1)
                        pe.matmul(ps_y[:, half, :], cm("ident"), h[n % 2][:, half, :],
                                  start=(n == 0), stop=(n == NS - 1)).then_inc(y_summed, 1)

                def work(g, k, b, c, t, s, before, after):
                    pe.wait_ge(split_mid_ready, t + 1)
                    pe.wait_ge(split_low_ready, t + 1)
                    for n in range(NS):
                        pe.wait_ge(dbx_ready, t * NS + (n + 1))
                        pe.matmul(ps_b[n % 2][:, :], sel[:, n, :], split[s][:, :], start=True, stop=True).then_inc(b_ready, 1)
                        pe.wait_ge(c_copied, t * NS + (n + 1))
                        pe.matmul(ps_c[:, :], sel[:, NS + n, :], split[s][:, :], start=True, stop=True).then_inc(c_ready, 1)
                        if n >= 2:
                            add_y(n - 2, t)
                        elif before:
                            add_y(n - 2 + NS, before[3])
                        if after:
                            prepare(n, *after, 1 - s)
                    if not after:
                        add_y(NS - 2, t)
                        add_y(NS - 1, t)

                pieces(pe, prepare, work)

            @block.scalar
            def _(act):
                act.preload_act_table_set(LN_SET)
                act.wait_ge(a_clamped, 1)
                act.activation(neg_a[:, :, :, :], neg_a[:, :, :, :], ACT.Exp).then_inc(a_exp, 1)
                act.sem_inc(scanned, 2 * FREE)
                act.sem_inc(hc_ready, 2 * FREE)
                act.sem_inc(delta_ready, LAST)

                def prepare(n, k, b, c, t, s):
                    if n == 2:
                        act.wait_ge(xd_ready, t + 1)
                        act.activation(split[s][:, :], ps_xd[0:96, :], ACT.Copy).then_inc(hi_ready, 1)
                        act.activation(dts[96:104, :], ps_xd[96:104, :], ACT.Copy).then_inc(dts_ready, 1)
                    if n == 4:
                        act.wait_ge(rest_ready, t + (1 + LAST))
                        act.activation(split[s][32:64, :], rest[32:64, :], ACT.Copy).then_inc(split_mid_ready, 1)
                        act.activation(mid[64:96, :], rest[64:96, :], ACT.Copy).then_inc(mid_ready, 1)
                    if n == 5:
                        act.wait_ge(dt_ready, t + 1)
                        if not isinstance(t, int) or t >= 2:
                            act.wait_ge(dbx_ready, t * NS + (FREE - NS))
                        for half in range(2):
                            ins = act.activation(u[s][:, half, :], ps_dt[:, half, :], ACT.Abs,
                                                 bias=wa("dt_b", 2 * k + half))
                        ins.then_inc(abs_ready, 1)
                    if n == 6:
                        act.wait_ge(abs_ready, t + 1)
                        act.activation(u[s][:, :, :], u[s][:, :, :], ACT.Exp, scale=-1.0).then_inc(e_ready, 1)
                    if n == 7:
                        act.wait_ge(e_ready, t + 1)
                        act.activation(delta[s][:, :, :], u[s][:, :, :], ACT.Ln, bias=1.0).then_inc(ln_ready, 1)
                    if n == 8:
                        act.wait_ge(delta_ready, t + 1)
                        act.activation(poly[:, :, :], u[s][:, :, :], ACT.Square, scale=3.0 ** -0.5,
                                       bias=sq_bias[:, :]).then_inc(sq_ready, 1)
                    if n == 11:
                        act.wait_ge(far_ready, t + 1)
                        act.wait_ge(near_ready, t + 1)
                        for half in range(2):
                            ins = act.activation(u[s][:, half, :], ps_dt[:, half, :], ACT.Relu,
                                                 bias=wa("dt_b", 2 * k + half))
                        ins.then_inc(relu_ready, 1)

                def save(n, g, k, t):
                    last = CH - 1 if k < 2 else 0
                    for half in range(2):
                        act.wait_ge(scanned, t * H2 + (2 * n + half + 1 + 2 * FREE))
                        act.activation(state[:, g % 2, half, n:n + 1], h[n % 2][:, half, last:last + 1],
                                       ACT.Copy).then_inc(state_saved, 1)

                def work(g, k, b, c, t, s, before, after):
                    act.wait_ge(delta_ready, t + (1 + LAST))
                    for n in range(NS):
                        for half in range(2):
                            act.wait_ge(scanned, t * H2 + (2 * n + half + 1))
                            act.activation(da[n % 2][:, half, :], delta[s][:, half, :], ACT.Exp,
                                           scale=neg_a[:, k, half, n:n + 1]).then_inc(da_ready, 1)
                        if n:
                            save(n - 1, g, k, t)
                        elif before:
                            save(NS - 1, before[0] * B + before[1], before[0], before[3])
                        act.wait_ge(c_ready, t * NS + (n + 1))
                        act.wait_ge(hc_ready, t * H2 + (2 * n + 2))
                        act.activation(c_sb[n % 2][:, :], ps_c[:, :], ACT.Copy).then_inc(c_copied, 1)
                        if after:
                            prepare(n, *after, 1 - s)
                    if not after:
                        save(NS - 1, g, k, t)

                act.wait_ge(a_ready, 2)
                pieces(act, prepare, work)

            @block.vector
            def _(dve):
                dve.tensor_scalar(neg_a[:, :, :, :].rearrange("p k f n -> p (k f n)"), wa("a_log", 0, KD * 2 * NS),
                                  83.0, None, ALU.min).then_inc(a_clamped, 1)
                dve.wait_ge(a_exp, 1)
                dve.tensor_scalar(neg_a[:, :, :, :], neg_a[:, :, :, :], -1.0, None, ALU.mult).then_inc(a_ready, 1)
                dve.memset(sq_bias[:, :], -(3.0 ** 0.5) / 4.0).then_inc(a_ready, 1)
                dve.tensor_reduce(d_sum[:, :], wa("d_skip", 0, KD * 2).rearrange("p (k f) -> p f k", f=2), AX_X,
                                  ALU.add).then_inc(d_ready, 1)
                dve.wait_ge(d_ready, 1)
                for half in range(2):
                    dve.tensor_scalar(y[:, half], xc[:, half], d_sum[:, half:half + 1], None,
                                      ALU.mult).then_inc(y_started, 1)
                dve.wait_ge(y_started, 2)
                dve.sem_inc(y_summed, 2 * FREE)
                dve.sem_inc(state_saved, H2)

                def prepare(n, k, b, c, t, s):
                    if n == 3:
                        dve.wait_ge(hi_ready, t + 1)
                        dve.tensor_tensor(rest[:, :], ps_xd[0:96, :], split[s][:, :], ALU.subtract).then_inc(rest_ready, 1)
                    if n == 5:
                        dve.wait_ge(mid_ready, t + 1)
                        dve.tensor_tensor(split[s][64:96, :], rest[64:96, :], mid[64:96, :],
                                          ALU.subtract).then_inc(split_low_ready, 1)
                    if n == 8:
                        dve.wait_ge(ln_ready, t + 1)
                        dve.scalar_tensor_tensor(delta[s][:, :, :], u[s][:, :, :], 0.02, delta[s][:, :, :],
                                                 ALU.is_lt, ALU.add).then_inc(far_ready, 1)
                    if n == 9:
                        dve.wait_ge(sq_ready, t + 1)
                        dve.scalar_tensor_tensor(poly[:, :, :], poly[:, :, :], 13.0 / 16.0, u[s][:, :, :],
                                                 ALU.add, ALU.mult).then_inc(near_ready, 1)
                    if n == 10:
                        dve.wait_ge(far_ready, t + 1)
                        dve.wait_ge(near_ready, t + 1)
                        dve.tensor_tensor(poly[:, :, :], poly[:, :, :], delta[s][:, :, :],
                                          ALU.min).then_inc(log_ready, 1)

                def y_add(k, b, c, t):
                    part = piece(y, k, b, c)
                    dve.wait_ge(y_summed, t * H2 + (H2 + 2 * FREE))
                    dve.wait_ge(y_added, t + 1)
                    dve.tensor_tensor(part, part, grid(ps_y[:, :, :]), ALU.add).then_inc(y_added, 1)

                def work(g, k, b, c, t, s, before, after):
                    if isinstance(c, int) and c == 0:
                        dve.wait_ge(state_reset, max(g, 1))
                    dve.wait_ge(u_ready, t + 1)
                    order = slice(None) if k < 2 else slice(None, None, -1)
                    for n in range(NS):
                        r = n % 2
                        dve.wait_ge(b_ready, t * NS + (n + 1))
                        dve.tensor_tensor(dbx[r][:, :, :], u[s][:, :, :], halves(ps_b[r][:, :], 2),
                                          ALU.mult).then_inc(dbx_ready, 1)
                        if n == 1 and before:
                            y_add(*before)
                        dve.wait_ge(dbx_ready, t * NS + (n + 1 + FREE))
                        for half in range(2):
                            dve.wait_ge(da_ready, t * H2 + (2 * n + half + 1))
                            dve.wait_ge(y_summed, t * H2 + (2 * n + half + 1))
                            dve.wait_ge(state_saved, t * H2 + (2 * n + half + 1))
                            dve.tensor_tensor_scan(h[r][:, half, order], da[r][:, half, order], dbx[r][:, half, order],
                                                   state[:, g % 2, half, n:n + 1], ALU.mult, ALU.add).then_inc(scanned, 1)
                        if after:
                            prepare(n, *after, 1 - s)
                    if not after:
                        y_add(k, b, c, t)

                pieces(dve, prepare, work)

            @block.gpsimd
            def _(pool):
                pool.memset(state[:, :, :, :], 0.0).then_inc(state_reset, 1)

                def prepare(n, k, b, c, t, s):
                    if n == 12:
                        pool.wait_ge(log_ready, t + 1)
                        pool.wait_ge(relu_ready, t + (1 + LAST))
                        pool.tensor_tensor(delta[s][:, :, :], poly[:, :, :], u[s][:, :, :], ALU.add).then_inc(delta_ready, 1)
                    if n == 13:
                        pool.wait_ge(delta_ready, t + (1 + LAST))
                        pool.tensor_tensor(grid(u[s][:, :, :]), grid(delta[s][:, :, :]), piece(xc, k, b, c),
                                           ALU.mult).then_inc(u_ready, 1)

                def work(g, k, b, c, t, s, before, after):
                    if g > 0 and isinstance(c, int) and c == 0:
                        pool.memset(state[:, (g + 1) % 2, :, :], 0.0).then_inc(state_reset, 1)
                    for n in range(NS):
                        for half in range(2):
                            part = h[n % 2][:, half, :]
                            pool.wait_ge(c_copied, t * NS + (n + 1 + LAST))
                            pool.wait_ge(state_saved, t * H2 + (2 * n + half + 1 + H2))
                            pool.tensor_tensor(part, part, c_sb[n % 2][:, :], ALU.mult).then_inc(hc_ready, 1)
                        if after:
                            prepare(n, *after, 1 - s)

                pieces(pool, prepare, work)


def gated_output(nc, xt, cm, wa, gscale, gshift, y, z):
    with ExitStack() as ctx:
        p = Place(nc, ctx)
        xn = [p.sb(f"xn{s}", [P, CH]) for s in range(2)]
        psz = [p.ps(f"psz{s}", [P, 2, CH]) for s in range(2)]
        xn_ready = p.sem("z_xn_ready")
        z_mul = p.sem("z_mul")
        z_ready = p.sem("z_ready")
        with nc.Block() as block:
            @block.vector
            def _(dve):
                dve.sem_inc(z_mul, FREE)
                for b in range(B):
                    with dve.Fori(0, CB // 2) as i:
                        for s in range(2):
                            t = 2 * i + (s + b * CB)
                            dve.wait_ge(z_mul, t + 1)
                            dve.tensor_scalar(xn[s][:, :], xt[:, bass.ds(t * CH, CH)], gscale[:, b:b + 1],
                                              gshift[:, b:b + 1], ALU.mult, ALU.add).then_inc(xn_ready, 1)

            @block.tensor
            def _(pe):
                pe.sem_inc(z_ready, FREE)
                with pe.Fori(0, NC // 2) as i:
                    for s in range(2):
                        t = 2 * i + s
                        pe.wait_ge(xn_ready, t + 1)
                        pe.wait_ge(z_ready, t + 1)
                        for half in range(2):
                            mm = pe.matmul(psz[s][:, half, :], wa("win", (2 + half) * P, P), xn[s][:, :],
                                           start=True, stop=True)
                        mm.then_inc(z_mul, 1)

            @block.scalar
            def _(act):
                act.preload_act_table(ACT.Silu)
                with act.Fori(0, NC // 2) as i:
                    for s in range(2):
                        t = 2 * i + s
                        act.wait_ge(z_mul, t + (1 + FREE))
                        act.activation(z[:, :, bass.ds(t * CH, CH)], psz[s][:, :, :], ACT.Silu).then_inc(z_ready, 1)
    with ExitStack() as ctx:
        p = Place(nc, ctx)
        d = [p.sb(f"d{s}", [P, 2, CH]) for s in range(2)]
        sq = [p.sb(f"sq{s}", [P, 2, CH]) for s in range(2)]
        lv = [p.sb(f"lv{s}", [P, CH]) for s in range(2)]
        psm = [p.ps(f"psm{s}", [P, CH]) for s in range(2)]
        psv = [p.ps(f"psv{s}", [P, CH]) for s in range(2)]
        pso = [p.ps(f"pso{s}", [P, CH]) for s in range(2)]
        mean_ready = p.sem("mean_ready")
        d_ready = p.sem("d_ready")
        sq_ready = p.sem("sq_ready")
        var_ready = p.sem("lvar_ready")
        ln_ready = p.sem("lln_ready")
        rstd_ready = p.sem("rstd_ready")
        norm_step = p.sem("norm_step")
        gated = p.sem("gated")
        out_ready = p.sem("out_ready")
        x_added = p.sem("x_added")
        y_flat = y[:, :].rearrange("p f b h w -> p f (b h w)")
        with nc.Block() as block:
            @block.tensor
            def _(pe):
                with pe.Fori(0, NC // 2) as i:
                    for s in range(2):
                        t = 2 * i + s
                        for half in range(2):
                            mm = pe.matmul(psm[s][:, :], cm("ones256"), y_flat[:, half, bass.ds(t * CH, CH)],
                                           start=(half == 0), stop=(half == 1))
                        mm.then_inc(mean_ready, 1)
                    for s in range(2):
                        t = 2 * i + s
                        pe.wait_ge(sq_ready, t + 1)
                        for half in range(2):
                            mm = pe.matmul(psv[s][:, :], cm("ones256"), sq[s][:, half, :],
                                           start=(half == 0), stop=(half == 1))
                        mm.then_inc(var_ready, 1)
                    for s in range(2):
                        t = 2 * i + s
                        pe.wait_ge(gated, t + 1)
                        for half in range(2):
                            mm = pe.matmul(pso[s][:, :], wa("wout", half * P, P), d[s][:, half, :],
                                           start=(half == 0), stop=(half == 1))
                        mm.then_inc(out_ready, 1)

            @block.scalar
            def _(act):
                act.preload_act_table_set(LN_SET)
                with act.Fori(0, NC // 2) as i:
                    for s in range(2):
                        t = 2 * i + s
                        act.wait_ge(d_ready, t + 1)
                        act.activation(sq[s][:, :, :], d[s][:, :, :], ACT.Square).then_inc(sq_ready, 1)
                    for s in range(2):
                        t = 2 * i + s
                        act.wait_ge(var_ready, t + 1)
                        act.activation(lv[s][:, :], psv[s][:, :], ACT.Ln, bias=cm("eps")).then_inc(ln_ready, 1)
                        act.wait_ge(ln_ready, t + 1)
                        act.activation(lv[s][:, :], lv[s][:, :], ACT.Exp, scale=-0.5).then_inc(rstd_ready, 1)

            @block.vector
            def _(dve):
                with dve.Fori(0, NC // 2) as i:
                    for s in range(2):
                        t = 2 * i + s
                        dve.wait_ge(mean_ready, t + 1)
                        dve.tensor_tensor(d[s][:, :, :], y_flat[:, :, bass.ds(t * CH, CH)], halves(psm[s][:, :], 2),
                                          ALU.subtract).then_inc(d_ready, 1)
                    for s in range(2):
                        t = 2 * i + s
                        dve.wait_ge(rstd_ready, t + 1)
                        link = Steps(dve, norm_step, t * 2)
                        for half in range(2):
                            link(dve.scalar_tensor_tensor(d[s][:, half, :], d[s][:, half, :], wa("ln_w", half),
                                                          lv[s][:, :], ALU.mult, ALU.mult))
                        for half in range(2):
                            ins = dve.scalar_tensor_tensor(d[s][:, half, :], d[s][:, half, :], wa("ln_b", half),
                                                           z[:, half, bass.ds(t * CH, CH)], ALU.add, ALU.mult)
                        ins.then_inc(gated, 1)
                    for s in range(2):
                        t = 2 * i + s
                        dve.wait_ge(out_ready, t + 1)
                        x = xt[:, bass.ds(t * CH, CH)]
                        dve.tensor_tensor(x, x, pso[s][:, :], ALU.add).then_inc(x_added, 1)


def ema_gate(nc, xt, cm, wb, gscale, gshift):
    with ExitStack() as ctx:
        p = Place(nc, ctx)
        prim = p.sb("prim", [P, N])
        gate = p.sb("gate", [P, B, WW, HH])
        decay = p.sb("decay", [P, WW, HH])
        b01 = p.sb("b01", [P, 1])
        xn = [p.sb(f"exn{s}", [P, CH]) for s in range(2)]
        prod = [p.sb(f"prod{s}", [P, CH]) for s in range(2)]
        psg = [p.ps(f"psg{s}", [P, CH]) for s in range(2)]
        psp = [p.ps(f"psp{s}", [P, CH]) for s in range(2)]
        pso = [p.ps(f"epso{s}", [P, CH]) for s in range(2)]
        const_step = p.sem("ema_const")
        xn_ready = p.sem("e_xn_ready")
        expanded = p.sem("expanded")
        gate_ready = p.sem("gate_ready")
        prim_ready = p.sem("prim_ready")
        averaged = p.sem("averaged")
        sig_ready = p.sem("sig_ready")
        prod_ready = p.sem("prod_ready")
        out_ready = p.sem("e_out_ready")
        x_added = p.sem("e_x_added")
        with nc.Block() as block:
            @block.vector
            def _(dve):
                link = Steps(dve, const_step)
                link(dve.tensor_scalar(b01[:, :], wb("b_exp", 1), 0.1, None, ALU.mult))
                link(dve.memset(decay[:, :, :], 0.9))
                link(dve.memset(decay[:, :, 0:1], 0.0))
                dve.sem_inc(expanded, FREE)
                for b in range(B):
                    with dve.Fori(0, CB // 2) as i:
                        for s in range(2):
                            t = 2 * i + (s + b * CB)
                            dve.wait_ge(expanded, t + 1)
                            dve.tensor_scalar(xn[s][:, :], xt[:, bass.ds(t * CH, CH)], gscale[:, b:b + 1],
                                              gshift[:, b:b + 1], ALU.mult, ALU.add).then_inc(xn_ready, 1)
                        for s in range(2):
                            t = 2 * i + (s + b * CB)
                            dve.wait_ge(expanded, t + (1 + FREE))
                            dve.tensor_scalar(prim[:, bass.ds(t * CH, CH)], psp[s][:, :], wb("b_exp", 0), None,
                                              ALU.add).then_inc(prim_ready, 1)
                for b in range(B):
                    dve.wait_ge(gate_ready, FREE + (b + 1) * CB)
                    row = gate[:, b].rearrange("p w h -> p (w h)")
                    dve.tensor_tensor_scan(row, decay[:, :, :].rearrange("p w h -> p (w h)"), row, 0.0,
                                           ALU.mult, ALU.add).then_inc(averaged, 1)
                dve.sem_inc(out_ready, FREE)
                for b in range(B):
                    dve.wait_ge(sig_ready, (b + 1) * CB)
                    dve.wait_ge(prim_ready, FREE + (b + 1) * CB)
                    with dve.Fori(0, CB // 2) as i:
                        for s in range(2):
                            c = 2 * i + s
                            t = 2 * i + (s + b * CB)
                            dve.wait_ge(out_ready, t + 1)
                            dve.tensor_tensor(prod[s][:, :].rearrange("p (h w) -> p h w", w=WW),
                                              prim[:, bass.ds(t * CH, CH)].rearrange("p (h w) -> p h w", w=WW),
                                              gate[:, b, :, bass.ds(c * ROWS, ROWS)].rearrange("p w h -> p h w"),
                                              ALU.mult).then_inc(prod_ready, 1)
                        for s in range(2):
                            t = 2 * i + (s + b * CB)
                            dve.wait_ge(out_ready, t + (1 + FREE))
                            x = xt[:, bass.ds(t * CH, CH)]
                            dve.scalar_tensor_tensor(x, pso[s][:, :], wb("b_con", 0), x,
                                                     ALU.add, ALU.add).then_inc(x_added, 1)

            @block.tensor
            def _(pe):
                pe.sem_inc(gate_ready, FREE)
                pe.sem_inc(prim_ready, FREE)
                with pe.Fori(0, NC // 2) as i:
                    for s in range(2):
                        t = 2 * i + s
                        pe.wait_ge(xn_ready, t + 1)
                        pe.wait_ge(gate_ready, t + 1)
                        pe.wait_ge(prim_ready, t + 1)
                        pe.matmul(psg[s][:, :], wb("w_exp", P, P), xn[s][:, :], start=True, stop=True)
                        pe.matmul(psp[s][:, :], wb("w_exp", 0, P), xn[s][:, :], start=True, stop=True)\
                            .then_inc(expanded, 1)
                pe.sem_inc(x_added, FREE)
                with pe.Fori(0, NC // 2) as i:
                    for s in range(2):
                        t = 2 * i + s
                        pe.wait_ge(prod_ready, t + 1)
                        pe.wait_ge(x_added, t + 1)
                        pe.matmul(pso[s][:, :], wb("w_con", 0, P), prod[s][:, :], start=True, stop=True)\
                            .then_inc(out_ready, 1)

            @block.scalar
            def _(act):
                act.wait_ge(const_step, 1)
                for b in range(B):
                    with act.Fori(0, CB // 2) as i:
                        for s in range(2):
                            c = 2 * i + s
                            act.wait_ge(expanded, c + (b * CB + 1 + FREE))
                            act.activation(gate[:, b, :, bass.ds(c * ROWS, ROWS)].rearrange("p w h -> p h w"),
                                           psg[s][:, :].rearrange("p (h w) -> p h w", w=WW), ACT.Identity,
                                           bias=b01[:, :], scale=0.1).then_inc(gate_ready, 1)
                act.preload_act_table(ACT.Sigmoid)
                for b in range(B):
                    act.wait_ge(averaged, b + 1)
                    row = gate[:, b].rearrange("p w h -> p (w h)")
                    with act.Fori(0, CB) as c:
                        part = row[:, bass.ds(c * CH, CH)]
                        act.activation(part, part, ACT.Sigmoid).then_inc(sig_ready, 1)


def layer_norm(nc, xt, cm, u, name):
    G = 4
    with ExitStack() as ctx:
        p = Place(nc, ctx)
        d = [p.sb(f"{name}_d{s}", [P, CH]) for s in range(G)]
        sq = [p.sb(f"{name}_sq{s}", [P, CH]) for s in range(G)]
        lv = [p.sb(f"{name}_lv{s}", [P, CH]) for s in range(G)]
        psm = [p.ps(f"{name}_psm{s}", [P, CH]) for s in range(G)]
        psv = [p.ps(f"{name}_psv{s}", [P, CH]) for s in range(G)]
        mean_ready = p.sem(name + "_mean_ready")
        d_ready = p.sem(name + "_d_ready")
        sq_ready = p.sem(name + "_sq_ready")
        var_ready = p.sem(name + "_var_ready")
        ln_ready = p.sem(name + "_ln_ready")
        rstd_ready = p.sem(name + "_rstd_ready")
        u_ready = p.sem(name + "_u_ready")
        with nc.Block() as block:
            @block.tensor
            def _(pe):
                with pe.Fori(0, NC // G) as i:
                    for s in range(G):
                        t = i * G + s
                        pe.matmul(psm[s][:, :], cm("ones128"), xt[:, bass.ds(t * CH, CH)],
                                  start=True, stop=True).then_inc(mean_ready, 1)
                    for s in range(G):
                        t = i * G + s
                        pe.wait_ge(sq_ready, t + 1)
                        pe.matmul(psv[s][:, :], cm("ones128"), sq[s][:, :],
                                  start=True, stop=True).then_inc(var_ready, 1)

            @block.scalar
            def _(act):
                act.preload_act_table_set(LN_SET)
                with act.Fori(0, NC // G) as i:
                    for s in range(G):
                        t = i * G + s
                        act.wait_ge(d_ready, t + 1)
                        act.activation(sq[s][:, :], d[s][:, :], ACT.Square).then_inc(sq_ready, 1)
                    for s in range(G):
                        t = i * G + s
                        act.wait_ge(var_ready, t + 1)
                        act.activation(lv[s][:, :], psv[s][:, :], ACT.Ln, bias=cm("eps")).then_inc(ln_ready, 1)
                        act.wait_ge(ln_ready, t + 1)
                        act.activation(lv[s][:, :], lv[s][:, :], ACT.Exp, scale=-0.5).then_inc(rstd_ready, 1)

            @block.vector
            def _(dve):
                with dve.Fori(0, NC // G) as i:
                    dve.wait_ge(u_ready, i * G)
                    for s in range(G):
                        t = i * G + s
                        dve.wait_ge(mean_ready, t + 1)
                        dve.tensor_tensor(d[s][:, :], xt[:, bass.ds(t * CH, CH)], psm[s][:, :],
                                          ALU.subtract).then_inc(d_ready, 1)
                    for s in range(G):
                        t = i * G + s
                        dve.wait_ge(rstd_ready, t + 1)
                        dve.tensor_tensor(u[:, bass.ds(t * CH, CH)], d[s][:, :], lv[s][:, :],
                                          ALU.mult).then_inc(u_ready, 1)


def linear_attention(nc, xt, cm, wc, u):
    H, DH = 4, 32
    J = CH // P
    with ExitStack() as ctx:
        p = Place(nc, ctx)
        k = p.sb("k", [P, B, L])
        q_t = p.sb("q_t", [P, B, L])
        kmax = p.sb("kmax", [P, B, CB])
        nmax = p.sb("nmax", [P, B])
        ctxs = p.sb("ctxs", [P, B, P + 1])
        m_out = p.sb("m_out", [P, B, P])
        stats = p.sb("a_stats", [P, NC, 6])
        with ExitStack() as inner:
            p2 = Place(nc, inner)
            psk = [p2.ps(f"psk{s}", [P, CH]) for s in range(2)]
            ke = [p2.sb(f"ke{s}", [P, CH]) for s in range(2)]
            uf = [p2.sb(f"uf{s}", [P, CH]) for s in range(2)]
            kt = p2.sb("kt", [P, J, P])
            vt = p2.sb("vt", [P, J, P + 1])
            q1 = p2.sb("q1", [P, J * H, DH])
            qm = p2.sb("qm", [P, J * H])
            qs = p2.sb("qs", [P, J * H])
            ps_kt = p2.ps("ps_kt", [P, J, P])
            ps_v = p2.ps("ps_v", [P, J, P])
            ps_q = p2.ps("ps_q", [P, J * H, DH])
            ps_qt = p2.ps("ps_qt", [P, CH])
            ps_ctx = p2.ps("ps_ctx", [P, CH])
            k_mul = p2.sem("k_mul")
            k_copied = p2.sem("k_copied")
            kmax_ready = p2.sem("kmax_ready")
            nmax_step = p2.sem("nmax_step")
            nmax_ready = p2.sem("nmax_ready")
            ones_set = p2.sem("ones_set")
            uf_ready = p2.sem("uf_ready")
            ke_ready = p2.sem("ke_ready")
            kt_mul = p2.sem("kt_mul")
            vq_mul = p2.sem("vq_mul")
            kt_ready = p2.sem("kt_ready")
            vt_ready = p2.sem("vt_ready")
            ctx_mul = p2.sem("ctx_mul")
            ctx_added = p2.sem("ctx_added")
            q_step = p2.sem("q_step")
            q_shifted = p2.sem("q_shifted")
            q_exp = p2.sem("q_exp")
            q_norm = p2.sem("q_norm")
            qt_mul = p2.sem("qt_mul")
            qt_ready = p2.sem("qt_ready")

            def over_head(ap):
                a = [list(x) for x in ap.ap]
                return bass.AP(tensor=ap.tensor, offset=ap.offset, ap=a + [[0, DH]])

            with nc.Block() as block:
                @block.tensor
                def _(pe):
                    pe.sem_inc(k_copied, FREE)
                    with pe.Fori(0, NC // 2) as i:
                        for s in range(2):
                            t = 2 * i + s
                            pe.wait_ge(k_copied, t + 1)
                            pe.matmul(psk[s][:, :], wc("w_k", 0, P), u[:, bass.ds(t * CH, CH)],
                                      start=True, stop=True).then_inc(k_mul, 1)
                    with pe.Fori(0, NC // 2) as i:
                        for s in range(2):
                            t = 2 * i + s
                            pe.wait_ge(uf_ready, t + 1)
                            pe.wait_ge(vt_ready, t)
                            pe.wait_ge(q_shifted, t)
                            for j in range(J):
                                pe.matmul(ps_v[:, j, :], uf[s][:, j * P:(j + 1) * P], wc("w_v", 0, P),
                                          start=True, stop=True)
                                mm = pe.matmul(ps_q[:, j * H:(j + 1) * H, :], uf[s][:, j * P:(j + 1) * P],
                                               wc("w_q", 0, P), start=True, stop=True)
                            mm.then_inc(vq_mul, 1)
                            pe.wait_ge(ke_ready, t + 1)
                            pe.wait_ge(kt_ready, t)
                            for j in range(J):
                                mm = pe.transpose(ps_kt[:, j, :], ke[s][:, j * P:(j + 1) * P], cm("ident"))
                            mm.then_inc(kt_mul, 1)
                            pe.wait_ge(kt_ready, t + 1)
                            pe.wait_ge(vt_ready, t + 1)
                            pe.wait_ge(ctx_added, t)
                            for j in range(J):
                                mm = pe.matmul(ps_ctx[:, 0:P + 1], kt[:, j, :], vt[:, j, :],
                                               start=(j == 0), stop=(j == J - 1))
                            mm.then_inc(ctx_mul, 1)
                            pe.wait_ge(q_norm, t + 1)
                            pe.wait_ge(qt_ready, t)
                            for j in range(J):
                                mm = pe.transpose(ps_qt[:, j * P:(j + 1) * P],
                                                  q1[:, j * H:(j + 1) * H, :].rearrange("p h d -> p (h d)"), cm("ident"))
                            mm.then_inc(qt_mul, 1)

                @block.scalar
                def _(act):
                    act.preload_act_table(ACT.Exp)
                    k_flat = k[:, :, :].rearrange("p b l -> p (b l)")
                    q_flat = q_t[:, :, :].rearrange("p b l -> p (b l)")
                    with act.Fori(0, NC // 2) as i:
                        for s in range(2):
                            t = 2 * i + s
                            act.wait_ge(k_mul, t + 1)
                            act.activation(k_flat[:, bass.ds(t * CH, CH)], psk[s][:, :], ACT.Copy).then_inc(k_copied, 1)
                    act.wait_ge(nmax_ready, 1)
                    act.wait_ge(k_copied, NC + FREE)
                    for b in range(B):
                        with act.Fori(0, CB // 2) as i:
                            for s in range(2):
                                t = 2 * i + (s + b * CB)
                                act.activation(ke[s][:, :], k_flat[:, bass.ds(t * CH, CH)], ACT.Exp,
                                               bias=nmax[:, b:b + 1]).then_inc(ke_ready, 1)
                                act.wait_ge(q_shifted, t + 1)
                                act.activation(q1[:, :, :], q1[:, :, :], ACT.Exp).then_inc(q_exp, 1)
                                act.wait_ge(kt_mul, t + 1)
                                act.activation(kt[:, :, :], ps_kt[:, :, :], ACT.Copy).then_inc(kt_ready, 1)
                                act.wait_ge(qt_mul, t + 1)
                                act.activation(q_flat[:, bass.ds(t * CH, CH)], ps_qt[:, :], ACT.Copy,
                                               scale=DH ** -0.5).then_inc(qt_ready, 1)

                @block.vector
                def _(dve):
                    dve.memset(vt[:, :, P:P + 1], 1.0).then_inc(ones_set, 1)
                    dve.memset(ctxs[:, :, :], 0.0).then_inc(ones_set, 1)
                    kmax_flat = kmax[:, :, :].rearrange("p b c -> p (b c)")
                    k_flat = k[:, :, :].rearrange("p b l -> p (b l)")
                    with dve.Fori(0, NC // 2) as i:
                        for s in range(2):
                            t = 2 * i + s
                            dve.wait_ge(k_copied, t + (1 + FREE))
                            dve.tensor_reduce(kmax_flat[:, bass.ds(t, 1)], k_flat[:, bass.ds(t * CH, CH)], AX_X,
                                              ALU.max).then_inc(kmax_ready, 1)
                    dve.wait_ge(kmax_ready, NC)
                    dve.tensor_reduce(nmax[:, :], kmax[:, :, :], AX_X, ALU.max).then_inc(nmax_step, 1)
                    dve.wait_ge(nmax_step, 1)
                    dve.tensor_scalar(nmax[:, :], nmax[:, :], -1.0, None, ALU.mult).then_inc(nmax_ready, 1)
                    dve.wait_ge(ones_set, 2)
                    dve.sem_inc(vq_mul, FREE)
                    for b in range(B):
                        with dve.Fori(0, CB // 2) as i:
                            for s in range(2):
                                t = 2 * i + (s + b * CB)
                                dve.wait_ge(vq_mul, t + 1)
                                dve.tensor_copy(uf[s][:, :], u[:, bass.ds(t * CH, CH)]).then_inc(uf_ready, 1)
                                dve.wait_ge(vq_mul, t + (1 + FREE))
                                link = Steps(dve, q_step, t * 3)
                                link(dve.tensor_reduce(qm[:, :], ps_q[:, :, :], AX_X, ALU.max))
                                dve.wait_ge(qt_mul, t)
                                dve.tensor_tensor(q1[:, :, :], ps_q[:, :, :], over_head(qm[:, :]),
                                                  ALU.subtract).then_inc(q_shifted, 1)
                                dve.wait_ge(ctx_mul, t)
                                dve.tensor_copy(vt[:, :, 0:P], ps_v[:, :, :]).then_inc(vt_ready, 1)
                                dve.wait_ge(q_exp, t + 1)
                                link(dve.tensor_reduce(qs[:, :], q1[:, :, :], AX_X, ALU.add))
                                link(dve.reciprocal(qs[:, :], qs[:, :]))
                                dve.tensor_tensor(q1[:, :, :], q1[:, :, :], over_head(qs[:, :]),
                                                  ALU.mult).then_inc(q_norm, 1)
                                dve.wait_ge(ctx_mul, t + 1)
                                dve.wait_ge(ctx_added, t)
                                dve.tensor_tensor(ctxs[:, b, :], ctxs[:, b, :], ps_ctx[:, 0:P + 1],
                                                  ALU.add).then_inc(ctx_added, 1)
        with ExitStack() as inner:
            p2 = Place(nc, inner)
            mv = p2.sb("a_mv", [P, B, 2])
            ex = p2.sb("a_ex", [P, B, 2])
            g = p2.sb("a_g", [P, B, 2])
            var = p2.sb("a_var", [P, B])
            std = p2.sb("a_std", [P, B])
            sc = p2.sb("a_sc", [P, B])
            sh = p2.sb("a_sh", [P, B])
            kinv = p2.sb("kinv", [P, B])
            ps_m = p2.ps("ps_m", [P, B, P])
            ps_g = p2.ps("ps_g", [P, CH])
            ps_o = [p2.ps(f"ps_o{s}", [P, CH]) for s in range(2)]
            step = p2.sem("m_step")
            ctx_ready = p2.sem("ctx_ready")
            m_mul = p2.sem("m_mul")
            m_ready = p2.sem("m_ready")
            o_mul = p2.sem("o_mul")
            o_ready = p2.sem("o_ready")
            stats_ready = p2.sem("o_stats_ready")
            moments_ready = p2.sem("o_moments_ready")
            group_ready = p2.sem("o_group_ready")
            var_ready = p2.sem("o_var_ready")
            std_ready = p2.sem("o_std_ready")
            scale_ready = p2.sem("scale_ready")
            o_scaled = p2.sem("o_scaled")
            x_added = p2.sem("o_x_added")
            with nc.Block() as block:
                @block.vector
                def _(dve):
                    link = Steps(dve, step)
                    link(dve.reciprocal(kinv[:, :], ctxs[:, :, P]))
                    for b in range(B):
                        ins = dve.scalar_tensor_tensor(ctxs[:, b, 0:P], ctxs[:, b, 0:P], kinv[:, b:b + 1], cm("heads"),
                                                       ALU.mult, ALU.mult)
                    ins.then_inc(ctx_ready, 1)
                    dve.wait_ge(m_mul, 1)
                    dve.tensor_copy(m_out[:, :, :], ps_m[:, :, :]).then_inc(m_ready, 1)
                    with dve.Fori(0, NC) as t:
                        dve.wait_ge(o_ready, t + (1 + FREE))
                        dve.bn_stats(stats[:, bass.ds(t, 1), :].rearrange("p a s -> p (a s)"),
                                     u[:, bass.ds(t * CH, CH)]).then_inc(stats_ready, 1)
                    dve.wait_ge(stats_ready, NC)
                    for b in range(B):
                        link(dve.bn_aggr(mv[:, b, :], stats[:, b * CB:(b + 1) * CB, :].rearrange("p a s -> p (a s)")))
                    link(dve.tensor_tensor(ex[:, :, 1], mv[:, :, 0], mv[:, :, 0], ALU.mult))
                    link(dve.tensor_copy(ex[:, :, 0], mv[:, :, 0]))
                    dve.tensor_tensor(ex[:, :, 1], ex[:, :, 1], mv[:, :, 1], ALU.add).then_inc(moments_ready, 1)
                    dve.wait_ge(group_ready, 1)
                    link(dve.tensor_copy(g[:, :, :].rearrange("p b s -> p (b s)"), ps_g[:, 0:2 * B]))
                    link(dve.tensor_tensor(var[:, :], g[:, :, 0], g[:, :, 0], ALU.mult))
                    dve.tensor_tensor(var[:, :], g[:, :, 1], var[:, :], ALU.subtract).then_inc(var_ready, 1)
                    dve.wait_ge(std_ready, 1)
                    link(dve.reciprocal(std[:, :], std[:, :]))
                    link(dve.tensor_scalar(sc[:, :], std[:, :], wc("gn_w", 0), None, ALU.mult))
                    link(dve.tensor_tensor(sh[:, :], g[:, :, 0], sc[:, :], ALU.mult))
                    dve.tensor_scalar(sh[:, :], sh[:, :], -1.0, wc("gn_b", 0), ALU.mult, ALU.add).then_inc(scale_ready, 1)
                    with dve.Fori(0, NC) as t:
                        dve.wait_ge(o_scaled, t + 1)
                        x = xt[:, bass.ds(t * CH, CH)]
                        dve.tensor_tensor(x, x, u[:, bass.ds(t * CH, CH)], ALU.add).then_inc(x_added, 1)

                @block.tensor
                def _(pe):
                    pe.wait_ge(ctx_ready, 1)
                    for b in range(B):
                        mm = pe.matmul(ps_m[:, b, :], ctxs[:, b, 0:P], wc("w_o", 0, P), start=True, stop=True)
                    mm.then_inc(m_mul, 1)
                    pe.wait_ge(m_ready, 1)
                    pe.sem_inc(o_ready, FREE)
                    for b in range(B):
                        with pe.Fori(0, CB // 2) as i:
                            for s in range(2):
                                t = 2 * i + (s + b * CB)
                                pe.wait_ge(o_ready, t + 1)
                                pe.matmul(ps_o[s][:, :], m_out[:, b, :],
                                          q_t[:, :, :].rearrange("p b l -> p (b l)")[:, bass.ds(t * CH, CH)],
                                          start=True, stop=True).then_inc(o_mul, 1)
                    pe.wait_ge(moments_ready, 1)
                    pe.matmul(ps_g[:, 0:2 * B], cm("ones128"), ex[:, :, :].rearrange("p b s -> p (b s)"),
                              start=True, stop=True).then_inc(group_ready, 1)

                @block.scalar
                def _(act):
                    with act.Fori(0, NC // 2) as i:
                        for s in range(2):
                            t = 2 * i + s
                            act.wait_ge(o_mul, t + 1)
                            act.activation(u[:, bass.ds(t * CH, CH)], ps_o[s][:, :], ACT.Identity,
                                           bias=wc("b_out", 0)).then_inc(o_ready, 1)
                    act.wait_ge(var_ready, 1)
                    act.activation(std[:, :], var[:, :], ACT.Sqrt, bias=cm("eps")).then_inc(std_ready, 1)
                    act.wait_ge(scale_ready, 1)
                    for b in range(B):
                        with act.Fori(0, CB) as c:
                            part = u[:, bass.ds(c * CH + b * L, CH)]
                            act.activation(part, part, ACT.Identity, scale=sc[:, b:b + 1],
                                           bias=sh[:, b:b + 1]).then_inc(o_scaled, 1)


def spectral_ffn(nc, xt, cm, wd, d, u):
    S4, K, T2 = 4, 16, L // 2
    TB = T2 // P
    AR = 3
    ALLM = K * P
    with ExitStack() as ctx:
        p = Place(nc, ctx)
        msel = p.sb("msel", [P, K, 2, P])
        mu = p.sb("mu", [P, AR, P])
        reach = p.sb("reach", [P, CB])
        gain = p.sb("gain", [P, CB])
        with ExitStack() as inner:
            p2 = Place(nc, inner)
            mp = [p2.sb(f"mp{i}", [P, ALLM]) for i in range(2)]
            mm_ = [p2.sb(f"mm{i}", [P, ALLM]) for i in range(2)]
            mus = p2.sb("mus", [P, S4, AR * P])
            acc_p = p2.sb("acc_p", [P, ALLM])
            acc_m = p2.sb("acc_m", [P, ALLM])
            small = p2.sb("small", [P, 8, S4])
            sig = p2.sb("sig", [P, K])
            m_loaded = [p2.sem(f"m_loaded{i}") for i in range(2)]
            mu_loaded = p2.sem("mu_loaded")
            step = p2.sem("w_step")
            shifted = p2.sem("w_shifted")
            expd = p2.sem("w_exp")
            root = p2.sem("sig_root")
            MIXED = 14
            with nc.Block() as block:
                @block.sync
                def _(sp):
                    sp.dma_start(mus[:, :, :].rearrange("p i n -> p (i n)"), d["m_u"]).then_inc(mu_loaded, 16)
                    for i in range(S4):
                        if i >= 2:
                            sp.wait_ge(step, MIXED + 2 * (i - 1))
                        sp.dma_start(mp[i % 2][:, :], d["m_plus"][:, i * ALLM:(i + 1) * ALLM]).then_inc(m_loaded[i % 2], 16)
                        sp.dma_start(mm_[i % 2][:, :], d["m_minus"][:, i * ALLM:(i + 1) * ALLM]).then_inc(m_loaded[i % 2], 16)

                @block.scalar
                def _(act):
                    act.activation(sig[:, :], wd("sigma", 0, K), ACT.Sqrt).then_inc(root, 1)
                    act.wait_ge(root, 1)
                    act.activation(sig[:, :], sig[:, :], ACT.Sqrt).then_inc(root, 1)
                    act.wait_ge(shifted, 1)
                    act.activation(small[:, 1, :], small[:, 0, :], ACT.Exp).then_inc(expd, 1)

                @block.vector
                def _(dve):
                    link = Steps(dve, step)
                    lg, ex, pr, hot, w, one = (small[:, i, :] for i in (0, 1, 2, 3, 4, 5))
                    scal = small[:, 7, :]
                    link(dve.tensor_tensor(lg, wd("logw", 0, S4), wd("gumbel", 0, S4), ALU.add))
                    link(dve.tensor_reduce(scal[:, 0:1], lg, AX_X, ALU.max))
                    dve.tensor_scalar(lg, lg, scal[:, 0:1], None, ALU.subtract).then_inc(shifted, 1)
                    dve.wait_ge(expd, 1)
                    link(dve.tensor_reduce(scal[:, 1:2], ex, AX_X, ALU.add))
                    link(dve.reciprocal(scal[:, 1:2], scal[:, 1:2]))
                    link(dve.tensor_scalar(pr, ex, scal[:, 1:2], None, ALU.mult))
                    link(dve.tensor_reduce(scal[:, 2:3], pr, AX_X, ALU.max))
                    link(dve.tensor_scalar(hot, pr, scal[:, 2:3], None, ALU.is_ge))
                    link(dve.tensor_tensor(one, hot, cm("rank8")[:, 0:S4], ALU.mult))
                    link(dve.tensor_reduce(scal[:, 3:4], one, AX_X, ALU.max))
                    link(dve.tensor_scalar(hot, one, scal[:, 3:4], None, ALU.is_equal))
                    link(dve.tensor_tensor(w, hot, pr, ALU.subtract))
                    link(dve.tensor_tensor(w, w, pr, ALU.add))
                    for src, dst in ((hot, reach), (w, gain)):
                        dve.tensor_scalar(dst[:, :], cm("ones")[:, 0:CB], src[:, 0:1], None, ALU.mult).then_inc(shifted, 1)
                    dve.wait_ge(shifted, 3)
                    n_shift = 3
                    for i in range(1, S4):
                        for src, dst in ((hot, reach), (w, gain)):
                            dve.tensor_scalar(dst[:, 0:CB >> i], dst[:, 0:CB >> i], src[:, i:i + 1], None,
                                              ALU.add).then_inc(shifted, 1)
                            n_shift += 1
                        dve.wait_ge(shifted, n_shift)
                    link(dve.memset(acc_p[:, :], 0.0))
                    link(dve.memset(acc_m[:, :], 0.0))
                    assert link.n == MIXED
                    for i in range(S4):
                        dve.wait_ge(m_loaded[i % 2], 32 * (i // 2 + 1))
                        for src, acc in ((mp, acc_p), (mm_, acc_m)):
                            link(dve.scalar_tensor_tensor(acc[:, :], src[i % 2][:, :], hot[:, i:i + 1], acc[:, :],
                                                          ALU.mult, ALU.add))
                    dve.wait_ge(mu_loaded, 16)
                    flat = mu[:, :, :].rearrange("p i n -> p (i n)")
                    link(dve.tensor_scalar(flat, mus[:, 0, :], hot[:, 0:1], None, ALU.mult))
                    for i in range(1, S4):
                        link(dve.scalar_tensor_tensor(flat, mus[:, i, :], hot[:, i:i + 1], flat, ALU.mult, ALU.add))
                    a3, b3 = (a[:, :].rearrange("p (k n) -> p k n", k=K) for a in (acc_p, acc_m))
                    link(dve.tensor_tensor(msel[:, :, 0, :], a3, b3, ALU.add))
                    link(dve.tensor_tensor(msel[:, :, 1, :], a3, b3, ALU.subtract))
                    dve.wait_ge(root, 2)
                    sa = [list(x) for x in sig[:, :].ap]
                    every = bass.AP(tensor=sig[:, :].tensor, offset=sig[:, :].offset, ap=sa + [[0, P]])
                    for par in range(2):
                        link(dve.tensor_tensor(msel[:, :, par, :], msel[:, :, par, :], every, ALU.mult))
        acc = u
        utok = p.sb("utok", [P, B, 2, TB, P])
        with ExitStack() as inner:
            p2 = Place(nc, inner)
            upad = p2.sb("upad", [P, B, 4 + L])
            uf = [p2.sb(f"suf{s}", [P, CH]) for s in range(2)]
            ps_t = [p2.ps(f"ps_t{s}", [P, 2, 2, P]) for s in range(2)]
            ps_a = [p2.ps(f"ps_a{s}", [P, CH]) for s in range(2)]
            padded = p2.sem("u_padded")
            uf_ready = p2.sem("s_uf_ready")
            up_ready = p2.sem("s_up_ready")
            t_mul = p2.sem("s_t_mul")
            t_copied = p2.sem("s_t_copied")
            a_mul = p2.sem("s_a_mul")
            a_copied = p2.sem("s_a_copied")

            with nc.Block() as block:
                @block.vector
                def _(dve):
                    dve.memset(upad[:, :, 0:4], 0.0).then_inc(padded, 1)
                    dve.sem_inc(t_mul, FREE)
                    for b in range(B):
                        with dve.Fori(0, CB // 2) as i:
                            for s in range(2):
                                c = 2 * i + s
                                t = 2 * i + (s + b * CB)
                                dve.wait_ge(t_mul, t + 1)
                                dve.tensor_scalar(uf[s][:, ::-1], u[:, bass.ds(t * CH, CH)], reach[:, bass.ds(c, 1)], None,
                                                  ALU.mult).then_inc(uf_ready, 1)
                                dve.wait_ge(uf_ready, t + 1)
                                dve.tensor_scalar(upad[:, b, bass.ds(c * CH + 4, CH)], uf[s][:, ::-1], 1.0, None, ALU.mult).then_inc(up_ready, 1)
                                dve.wait_ge(a_mul, t + 1)
                                dve.tensor_scalar(acc[:, bass.ds(t * CH, CH)], ps_a[s][:, :], 1.0, None, ALU.mult).then_inc(a_copied, 1)

                @block.tensor
                def _(pe):
                    pe.wait_ge(padded, 1)
                    pe.sem_inc(t_copied, FREE)
                    pe.sem_inc(a_copied, FREE)
                    for b in range(B):
                        with pe.Fori(0, CB // 2) as i:
                            for s in range(2):
                                c = 2 * i + s
                                t = 2 * i + (s + b * CB)
                                pe.wait_ge(uf_ready, t + 1)
                                pe.wait_ge(t_copied, t + 1)
                                for par in range(2):
                                    for j in range(2):
                                        mm = pe.transpose(ps_t[s][:, par, j, :],
                                                          uf[s][:, (2 * P + 1) - 2 * P * j - par:(4 * P) - 2 * P * j - par:2], cm("ident"))
                                mm.then_inc(t_mul, 1)
                                pe.wait_ge(up_ready, t + 1)
                                pe.wait_ge(a_copied, t + 1)
                                for a in range(AR):
                                    mm = pe.matmul(ps_a[s][:, :], mu[:, a, :], upad[:, b, bass.ds(c * CH + (4 - a), CH)],
                                                   start=(a == 0), stop=(a == AR - 1))
                                mm.then_inc(a_mul, 1)

                @block.scalar
                def _(act):
                    for b in range(B):
                        with act.Fori(0, CB // 2) as i:
                            for s in range(2):
                                c = 2 * i + s
                                t = 2 * i + (s + b * CB)
                                act.wait_ge(t_mul, t + (1 + FREE))
                                act.activation(utok[:, b, :, bass.ds(c * 2, 2), :], ps_t[s][:, :, :, :],
                                               ACT.Copy).then_inc(t_copied, 1)
        with ExitStack() as inner:
            p2 = Place(nc, inner)
            even = [p2.sb(f"even{s}", [P, T2]) for s in range(2)]
            odd = [p2.sb(f"odd{s}", [P, T2 + 1]) for s in range(2)]
            mk = [p2.sb(f"mk{s}", [P, 2, P]) for s in range(2)]
            yk = [p2.sb(f"yk{s}", [P, 2, CH]) for s in range(2)]
            ps_y = [p2.ps(f"sps_y{s}", [P, 2, CH]) for s in range(2)]
            ps_o = [p2.ps(f"sps_o{s}", [P, CH]) for s in range(2)]
            strips_loaded = [p2.sem(f"strips_loaded{s}") for s in range(2)]
            mk_ready = p2.sem("mk_ready")
            k_done = p2.sem("k_done")
            y_mul = p2.sem("s_y_mul")
            ye_copied = p2.sem("s_ye_copied")
            yo_copied = p2.sem("s_yo_copied")
            o_mul = p2.sem("s_o_mul")
            o_added = p2.sem("s_o_added")
            x_added = p2.sem("s_x_added")
            units = [(b, par, c) for b in range(B) for par in range(2) for c in range(T2 // CH)]
            UN = len(units)
            PW = T2 + P + 1
            phi = d["phi"]
            with nc.Block() as block:
                @block.sync
                def _(sp):
                    sp.sem_inc(k_done, FREE)
                    with sp.Fori(0, K // 2) as i:
                        for s in range(2):
                            k = 2 * i + s
                            sp.wait_ge(k_done, k + 1)
                            for tile, par, off, w in ((even[s], 0, 2, T2), (odd[s], 1, 1, T2 + 1)):
                                row = phi[bass.ds(k, 1), par * PW + off:par * PW + off + w]
                                src = bass.AP(tensor=row.tensor, offset=row.offset, ap=[[1, P], [1, w]])
                                sp.dma_start(tile[:, :], src).then_inc(strips_loaded[s], 16)

                @block.tensor
                def _(pe):
                    pe.sem_inc(ye_copied, FREE)
                    pe.sem_inc(yo_copied, FREE)
                    pe.sem_inc(o_added, FREE)
                    with pe.Fori(0, K // 2) as i:
                        for s in range(2):
                            k = 2 * i + s

                            def mix(n):
                                pe.wait_ge(ye_copied, k * UN + (n + 1 + FREE))
                                pe.wait_ge(yo_copied, k * UN + (n + 1 + FREE))
                                pe.wait_ge(o_added, k * UN + (n + 1))
                                if n == 0:
                                    pe.wait_ge(mk_ready, k + 1)
                                for par in range(2):
                                    mm = pe.matmul(ps_o[n % 2][:, :], mk[s][:, par, :], yk[n % 2][:, par, :],
                                                   start=(par == 0), stop=(par == 1))
                                mm.then_inc(o_mul, 1)

                            pe.wait_ge(strips_loaded[s], i * 32 + 32)
                            for n, (b, par, c) in enumerate(units):
                                pe.wait_ge(ye_copied, k * UN + (n + 1))
                                pe.wait_ge(yo_copied, k * UN + (n + 1))
                                tiles = 4 * c + 4
                                for j in range(tiles):
                                    lo = max(0, (j - 4 * c) * P)
                                    at = c * CH - j * P + lo
                                    w = CH - lo
                                    pe.matmul(ps_y[n % 2][:, 0, lo:CH], utok[:, b, par, j, :], even[s][:, at:at + w],
                                              start=(j == 0), stop=(j == tiles - 1))
                                for j in range(tiles):
                                    lo = max(0, (j - 4 * c) * P)
                                    at = c * CH - j * P + lo + par
                                    w = CH - lo
                                    mm = pe.matmul(ps_y[n % 2][:, 1, lo:CH], utok[:, b, 1 - par, j, :],
                                                   odd[s][:, at:at + w], start=(j == 0), stop=(j == tiles - 1))
                                mm.then_inc(y_mul, 1)
                                if n:
                                    mix(n - 1)
                            mix(UN - 1)

                @block.scalar
                def _(act):
                    act.sem_inc(o_mul, FREE * UN)
                    with act.Fori(0, K // 2) as i:
                        for s in range(2):
                            k = 2 * i + s
                            act.wait_ge(o_mul, k * UN + UN)
                            act.activation(mk[s][:, :, :], msel[:, bass.ds(k, 1), :, :].rearrange("p o a e -> p (o a) e"),
                                           ACT.Copy).then_inc(mk_ready, 1)
                            for n in range(UN):
                                act.wait_ge(y_mul, k * UN + (n + 1))
                                act.activation(yk[n % 2][:, 0, :], ps_y[n % 2][:, 0, :], ACT.Copy).then_inc(ye_copied, 1)

                @block.vector
                def _(dve):
                    with dve.Fori(0, K // 2) as i:
                        for s in range(2):
                            k = 2 * i + s

                            def add(n):
                                dve.wait_ge(o_mul, k * UN + (n + 1 + FREE * UN))
                                b, par, c = units[n]
                                at = b * L + 2 * c * CH + par
                                part = acc[:, at:at + 2 * CH - par:2]
                                dve.tensor_tensor(part, part, ps_o[n % 2][:, :], ALU.add).then_inc(o_added, 1)

                            for n in range(UN):
                                dve.wait_ge(y_mul, k * UN + (n + 1))
                                if n == UN - 1:
                                    dve.sem_inc(k_done, 1)
                                dve.tensor_copy(yk[n % 2][:, 1, :], ps_y[n % 2][:, 1, :]).then_inc(yo_copied, 1)
                                if n:
                                    add(n - 1)
                            add(UN - 1)
                    dve.wait_ge(o_added, K * UN + FREE)
                    with dve.Fori(0, CB) as c:
                        for b in range(B):
                            x = xt[:, bass.ds(c * CH + b * L, CH)]
                            dve.scalar_tensor_tensor(x, acc[:, bass.ds(c * CH + b * L, CH)], gain[:, bass.ds(c, 1)], x,
                                                     ALU.mult, ALU.add).then_inc(x_added, 1)


def additive_attention(nc, xt, cm, we, u):
    A, R = 16, 8
    QB = P // R
    TI = L // P
    SEG = 8
    ST = TI // SEG
    QG = 4
    with ExitStack() as ctx:
        p = Place(nc, ctx)
        g_rep = p.sb("g_rep", [P, B, L])
        f_bias = p.sb("f_bias", [P, B, L // R])
        xtok = p.sb("xtok", [P, B * TI, P + 1])
        w2 = p.sb("w2", [P, QG, QG * R])
        with ExitStack() as inner:
            p2 = Place(nc, inner)
            uf = [p2.sb(f"auf{s}", [P, CH]) for s in range(2)]
            fm = [p2.sb(f"fm{s}", [P, CH // R, R]) for s in range(2)]
            ps_g = [p2.ps(f"aps_g{s}", [P, CH]) for s in range(2)]
            ps_f = [p2.ps(f"aps_f{s}", [P, CH]) for s in range(2)]
            ps_t = [p2.ps(f"aps_t{s}", [P, CH]) for s in range(2)]
            const_ready = p2.sem("a3_const")
            uf_ready = p2.sem("a_uf_ready")
            mul_ready = p2.sem("a_mul_ready")
            t_copied = p2.sem("a_t_copied")
            fm_ready = p2.sem("fm_ready")
            f_summed = p2.sem("f_summed")
            f_ready = p2.sem("f_ready")
            f_flat = f_bias[:, :, :].rearrange("p b n -> p (b n)")
            g_flat = g_rep[:, :, :].rearrange("p b n -> p (b n)")
            with nc.Block() as block:
                @block.vector
                def _(dve):
                    dve.memset(xtok[:, :, P:P + 1], 1.0).then_inc(const_ready, 1)
                    dve.memset(w2[:, :, :], 0.0).then_inc(const_ready, 1)
                    dve.wait_ge(const_ready, 2)
                    for m in range(QG):
                        dve.tensor_scalar(w2[:, m, m * R:(m + 1) * R], cm("row8"), we("w2", 0), None,
                                          ALU.mult).then_inc(const_ready, 1)
                    dve.sem_inc(mul_ready, FREE)
                    row = [list(x) for x in cm("row8").ap]
                    pick = bass.AP(tensor=cm("row8").tensor, offset=cm("row8").offset,
                                   ap=[row[0], [0, CH // R], row[1]])
                    with dve.Fori(0, NC // 2) as i:
                        for s in range(2):
                            t = 2 * i + s
                            dve.wait_ge(mul_ready, t + 1)
                            dve.tensor_copy(uf[s][:, :], u[:, bass.ds(t * CH, CH)]).then_inc(uf_ready, 1)
                        for s in range(2):
                            t = 2 * i + s
                            dve.wait_ge(mul_ready, t + (1 + FREE))
                            dve.tensor_tensor(fm[s][:, :, :], ps_f[s][:, :].rearrange("p (n r) -> p n r", r=R), pick,
                                              ALU.mult).then_inc(fm_ready, 1)
                        for s in range(2):
                            t = 2 * i + s
                            dve.wait_ge(fm_ready, t + 1)
                            dve.tensor_reduce(f_flat[:, bass.ds(t * (CH // R), CH // R)], fm[s][:, :, :], AX_X,
                                              ALU.add).then_inc(f_summed, 1)
                    dve.wait_ge(f_summed, NC)
                    dve.tensor_scalar(f_flat, f_flat, we("b1", 0), None, ALU.add).then_inc(f_ready, 1)

                @block.tensor
                def _(pe):
                    pe.sem_inc(t_copied, FREE)
                    with pe.Fori(0, NC // 2) as i:
                        for s in range(2):
                            t = 2 * i + s
                            pe.wait_ge(uf_ready, t + 1)
                            pe.wait_ge(t_copied, t + 1)
                            for j in range(CH // P):
                                pe.transpose(ps_t[s][:, j * P:(j + 1) * P], uf[s][:, j * P:(j + 1) * P], cm("ident"))
                            pe.matmul(ps_g[s][:, :], we("w1g", 0, P), uf[s][:, :], start=True, stop=True)
                            pe.matmul(ps_f[s][:, :], we("w1f", 0, P), uf[s][:, :], start=True, stop=True)\
                                .then_inc(mul_ready, 1)

                @block.scalar
                def _(act):
                    with act.Fori(0, NC // 2) as i:
                        for s in range(2):
                            t = 2 * i + s
                            act.wait_ge(mul_ready, t + (1 + FREE))
                            act.activation(g_flat[:, bass.ds(t * CH, CH)], ps_g[s][:, :], ACT.Copy)
                            act.activation(xtok[:, bass.ds(t * 4, 4), 0:P],
                                           ps_t[s][:, :].rearrange("p (j c) -> p j c", c=P), ACT.Copy)\
                                .then_inc(t_copied, 1)
        acc = p.sb("a_acc", [P, B * TI, P + 1])
        with ExitStack() as inner:
            p2 = Place(nc, inner)
            th = [[u[:, (g * QG + j) * SEG * P:(g * QG + j + 1) * SEG * P] for j in range(QG)] for g in range(2)]
            e = [p2.sb(f"ae{s}", [P, SEG * P]) for s in range(2)]
            et = [p2.sb(f"et{s}", [P, SEG, P]) for s in range(2)]
            ps_s = [p2.ps(f"ps_s{s}", [P, SEG * P]) for s in range(2)]
            ps_e = p2.ps("ps_e", [P, SEG, P])
            ps_o = [p2.ps(f"aps_o{s}", [P, CH]) for s in range(2)]
            tanh_ready = p2.sem("tanh_ready")
            scored = p2.sem("scored")
            e_ready = p2.sem("ae_ready")
            e_turned = p2.sem("ae_turned")
            et_ready = p2.sem("et_ready")
            o_mul = p2.sem("ao_mul")
            o_added = p2.sem("ao_added")

            def units(eng, run):
                with eng.Fori(0, B * ST) as g:
                    run(g * SEG, g * SEG, g * SEG, True)
                x0 = B * TI
                for seg in range(ST - 1):
                    n = ST - seg - 1
                    with eng.Fori(0, B) as b:
                        with eng.Fori(0, n) as i:
                            run(i * SEG + b * (n * SEG) + x0, i * SEG + b * TI + SEG * (seg + 1),
                                b * TI + seg * SEG, False)
                    x0 += B * n * SEG

            with nc.Block() as block:
                @block.scalar
                def _(act):
                    act.preload_act_table(ACT.Tanh)
                    act.sem_inc(scored, FREE)
                    act.sem_inc(e_turned, FREE)
                    f_flat = f_bias[:, :, :].rearrange("p b n -> p (b n)")
                    g_flat = g_rep[:, :, :].rearrange("p b n -> p (b n)")

                    def run(x0, tile0, key0, diagonal):
                        def exp(k):
                            w = (k + 1 if diagonal else SEG) * P
                            x = x0 + k
                            act.wait_ge(scored, x * QG + (QG + FREE))
                            act.wait_ge(e_turned, x + 1)
                            act.activation(e[k % 2][:, 0:w], ps_s[k % 2][:, 0:w], ACT.Exp,
                                           bias=we("b2", 0)).then_inc(e_ready, 1)

                        for k in range(SEG):
                            w = (k + 1 if diagonal else SEG) * P
                            for g in range(QG):
                                act.wait_ge(scored, (x0 + k) * QG + (g + 1))
                                for j in range(QG):
                                    act.activation(th[g % 2][j][:, 0:w], g_flat[:, bass.ds(key0 * P, w)], ACT.Tanh,
                                                   bias=f_flat[:, bass.ds((tile0 + k) * QB + (QG * j + g), 1)])\
                                        .then_inc(tanh_ready, 1)
                                if g == 0 and k > 0:
                                    exp(k - 1)
                        exp(SEG - 1)

                    units(act, run)

                @block.tensor
                def _(pe):
                    pe.sem_inc(e_ready, FREE)
                    pe.sem_inc(et_ready, 1)
                    pe.sem_inc(o_added, FREE)

                    def run(x0, tile0, key0, diagonal):
                        def turn(k):
                            m = k + 1 if diagonal else SEG
                            pe.wait_ge(e_ready, x0 + (k + 1 + FREE))
                            pe.wait_ge(et_ready, x0 + (k + 1))
                            for j in range(m):
                                mm = pe.transpose(ps_e[:, j, :], e[k % 2][:, j * P:(j + 1) * P], cm("ident"))
                            mm.then_inc(e_turned, 1)

                        def weigh(k):
                            m = k + 1 if diagonal else SEG
                            pe.wait_ge(et_ready, x0 + (k + 2))
                            pe.wait_ge(o_added, x0 + (k + 1))
                            for j in range(m):
                                mm = pe.matmul(ps_o[k % 2][:, 0:P + 1], et[k % 2][:, j, :],
                                               xtok[:, bass.ds(key0 + j, 1), :].rearrange("p a c -> p (a c)"),
                                               start=(j == 0), stop=(j == m - 1))
                            mm.then_inc(o_mul, 1)

                        for k in range(SEG):
                            w = (k + 1 if diagonal else SEG) * P
                            pe.wait_ge(e_ready, x0 + (k + 1))
                            for g in range(QG):
                                pe.wait_ge(tanh_ready, (x0 + k) * QB + (QG * (g + 1)))
                                for h in range(0, w, CH):
                                    c = min(CH, w - h)
                                    for j in range(QG):
                                        mm = pe.matmul(ps_s[k % 2][32 * j:32 * (j + 1), h:h + c], w2[:, g, :],
                                                       th[g % 2][j][:, h:h + c], start=(g == 0), stop=(g == QG - 1))
                                mm.then_inc(scored, 1)
                                if g == 1 and k > 0:
                                    turn(k - 1)
                                if g == 2 and k > 0:
                                    weigh(k - 1)
                        turn(SEG - 1)
                        weigh(SEG - 1)

                    units(pe, run)

                @block.vector
                def _(dve):
                    dve.sem_inc(o_mul, FREE)

                    def run(x0, tile0, key0, diagonal):
                        for k in range(SEG):
                            dve.wait_ge(e_turned, x0 + (k + 1 + FREE))
                            dve.wait_ge(o_mul, x0 + (k + 1))
                            m = k if diagonal else SEG
                            if m > 0:
                                ins = dve.tensor_copy(et[k % 2][:, 0:m, :], ps_e[:, 0:m, :])
                            if diagonal:
                                ins = dve.tensor_tensor(et[k % 2][:, k, :], ps_e[:, k, :], cm("later"), ALU.mult)
                            ins.then_inc(et_ready, 1)
                            part = acc[:, bass.ds(tile0 + k, 1), :].rearrange("p a c -> p (a c)")
                            dve.wait_ge(o_mul, x0 + (k + 1 + FREE))
                            if diagonal:
                                dve.tensor_copy(part, ps_o[k % 2][:, 0:P + 1]).then_inc(o_added, 1)
                            else:
                                dve.wait_ge(o_added, x0 + (k + FREE))
                                dve.tensor_tensor(part, part, ps_o[k % 2][:, 0:P + 1], ALU.add).then_inc(o_added, 1)

                    units(dve, run)
        with ExitStack() as inner:
            p2 = Place(nc, inner)
            rden = p2.sb("rden", [P, B * TI])
            wn = [p2.sb(f"wn{s}", [P, CH // P, P]) for s in range(2)]
            ps_x = [p2.ps(f"aps_x{s}", [P, CH]) for s in range(2)]
            den_step = p2.sem("den_step")
            wn_ready = p2.sem("wn_ready")
            x_mul = p2.sem("ax_mul")
            x_added = p2.sem("ax_added")
            with nc.Block() as block:
                @block.vector
                def _(dve):
                    link = Steps(dve, den_step)
                    link(dve.tensor_scalar(rden[:, :], acc[:, :, P], 1e-10, None, ALU.add))
                    link(dve.reciprocal(rden[:, :], rden[:, :]))
                    with dve.Fori(0, NC // 2) as i:
                        for s in range(2):
                            t = 2 * i + s
                            part = rden[:, bass.ds(t * 4, 4)]
                            dve.tensor_tensor(wn[s][:, :, :], acc[:, bass.ds(t * 4, 4), 0:P], inside(part, P),
                                              ALU.mult).then_inc(wn_ready, 1)
                        for s in range(2):
                            t = 2 * i + s
                            dve.wait_ge(x_mul, t + 1)
                            x = xt[:, bass.ds(t * CH, CH)]
                            dve.tensor_tensor(x, x, ps_x[s][:, :], ALU.add).then_inc(x_added, 1)

                @block.tensor
                def _(pe):
                    with pe.Fori(0, NC // 2) as i:
                        for s in range(2):
                            t = 2 * i + s
                            pe.wait_ge(wn_ready, t + 1)
                            for j in range(CH // P):
                                mm = pe.transpose(ps_x[s][:, j * P:(j + 1) * P], wn[s][:, j, :], cm("ident"))
                            mm.then_inc(x_mul, 1)


def expert_ffn(nc, xt, cm, wf, u, out):
    E, J, T = 8, CH // P, N // P
    with ExitStack() as ctx:
        p = Place(nc, ctx)
        lg = p.sb("lg", [P, T, E])
        wt = p.sb("wt", [P, T, E])
        with ExitStack() as inner:
            p2 = Place(nc, inner)
            hot = p2.sb("f_hot", [P, T, E])
            hot2 = p2.sb("f_hot2", [P, T, E])
            sc = p2.sb("f_sc", [P, T, E])
            m1 = p2.sb("f_m1", [P, T])
            m2 = p2.sb("f_m2", [P, T])
            mx = p2.sb("f_mx", [P, T])
            uf = [p2.sb(f"fuf{s}", [P, CH]) for s in range(2)]
            ps_l = [p2.ps(f"ps_l{s}", [P, J, E]) for s in range(2)]
            uf_ready = p2.sem("f_uf_ready")
            l_mul = p2.sem("l_mul")
            l_ready = p2.sem("l_ready")
            step = p2.sem("f_step")
            shifted = p2.sem("f_shifted")
            expd = p2.sem("f_expd")
            rb = wf("router_b", 0, E)
            with nc.Block() as block:
                @block.scalar
                def _(act):
                    act.wait_ge(shifted, 1)
                    act.activation(lg[:, :, :], lg[:, :, :], ACT.Exp).then_inc(expd, 1)

                @block.tensor
                def _(pe):
                    with pe.Fori(0, NC // 2) as i:
                        for s in range(2):
                            t = 2 * i + s
                            pe.wait_ge(uf_ready, t + 1)
                            for j in range(J):
                                mm = pe.matmul(ps_l[s][:, j, :], uf[s][:, j * P:(j + 1) * P], wf("router", 0, E),
                                               start=True, stop=True)
                            mm.then_inc(l_mul, 1)

                @block.vector
                def _(dve):
                    with dve.Fori(0, NC // 2) as i:
                        for s in range(2):
                            t = 2 * i + s
                            dve.tensor_copy(uf[s][:, :], u[:, bass.ds(t * CH, CH)]).then_inc(uf_ready, 1)
                        for s in range(2):
                            t = 2 * i + s
                            dve.wait_ge(l_mul, t + 1)
                            dve.tensor_tensor(lg[:, bass.ds(t * J, J), :], ps_l[s][:, :, :], halves(rb, J),
                                              ALU.add).then_inc(l_ready, 1)
                    dve.wait_ge(l_ready, NC)
                    link = Steps(dve, step)
                    link(dve.tensor_reduce(mx[:, :], lg[:, :, :], AX_X, ALU.max))
                    dve.tensor_tensor(lg[:, :, :], lg[:, :, :], inside(mx[:, :], E), ALU.subtract).then_inc(shifted, 1)
                    dve.wait_ge(expd, 1)
                    link(dve.tensor_reduce(mx[:, :], lg[:, :, :], AX_X, ALU.add))
                    link(dve.reciprocal(mx[:, :], mx[:, :]))
                    link(dve.tensor_tensor(lg[:, :, :], lg[:, :, :], inside(mx[:, :], E), ALU.mult))
                    link(dve.tensor_copy(wt[:, :, :], lg[:, :, :]))
                    for m, one in ((m1, hot), (m2, hot2)):
                        link(dve.tensor_reduce(m[:, :], wt[:, :, :], AX_X, ALU.max))
                        link(dve.tensor_tensor(sc[:, :, :], wt[:, :, :], inside(m[:, :], E), ALU.is_ge))
                        link(dve.tensor_tensor(sc[:, :, :], sc[:, :, :], halves(cm("rank8"), T), ALU.mult))
                        link(dve.tensor_reduce(mx[:, :], sc[:, :, :], AX_X, ALU.max))
                        link(dve.tensor_tensor(one[:, :, :], sc[:, :, :], inside(mx[:, :], E), ALU.is_equal))
                        if m is m1:
                            link(dve.scalar_tensor_tensor(wt[:, :, :], one[:, :, :], -2.0, wt[:, :, :],
                                                          ALU.mult, ALU.add))
                    link(dve.tensor_tensor(mx[:, :], m1[:, :], m2[:, :], ALU.add))
                    link(dve.reciprocal(mx[:, :], mx[:, :]))
                    link(dve.tensor_tensor(hot[:, :, :], hot[:, :, :], hot2[:, :, :], ALU.add))
                    link(dve.tensor_tensor(wt[:, :, :], hot[:, :, :], lg[:, :, :], ALU.mult))
                    link(dve.tensor_tensor(wt[:, :, :], wt[:, :, :], inside(mx[:, :], E), ALU.mult))
        with ExitStack() as inner:
            p2 = Place(nc, inner)
            uf = [p2.sb(f"guf{s}", [P, CH]) for s in range(2)]
            xf = [p2.sb(f"gxf{s}", [P, CH]) for s in range(2)]
            w1 = [p2.sb(f"gw{s}", [P, J, E]) for s in range(2)]
            wts = [p2.sb(f"gwt{s}", [E, CH]) for s in range(2)]
            xr = [p2.sb(f"gxr{s}", [P, J, P]) for s in range(2)]
            o = [p2.sb(f"go{s}", [P, J, P]) for s in range(2)]
            ps_e = [p2.ps(f"ps_e{s}", [P, 2, CH]) for s in range(2)]
            ps_w = p2.ps("ps_w", [E, CH])
            ps_r = [p2.ps(f"ps_r{s}", [P, J, P]) for s in range(2)]
            fixed = p2.sem("g_fixed")
            w_mul = p2.sem("gw_mul")
            w_copied = p2.sem("gw_copied")
            r_mul = p2.sem("gr_mul")
            r_copied = p2.sem("gr_copied")
            e_mul = p2.sem("ge_mul")
            e_used = p2.sem("ge_used")
            step = p2.sem("g_step")
            o_stored = [p2.sem(f"go_stored{s}") for s in range(2)]
            o_ready = p2.sem("go_ready")
            with nc.Block() as block:
                @block.tensor
                def _(pe):
                    pe.sem_inc(e_used, FREE)
                    with pe.Fori(0, NC // 2) as i:
                        for s in range(2):
                            t = 2 * i + s
                            pe.wait_ge(fixed, 3 * t + 3)
                            pe.wait_ge(w_copied, t)
                            for j in range(J):
                                mm = pe.transpose(ps_w[:, j * P:(j + 1) * P], w1[s][:, j, :], cm("ident"))
                            mm.then_inc(w_mul, 1)
                            pe.wait_ge(w_copied, t + 1)
                            for j in range(J):
                                some = slice(j * P, (j + 1) * P)
                                pe.matmul(ps_r[s][:, j, :], xf[s][:, some], cm("ident"), start=True, stop=False)
                                mm = pe.matmul(ps_r[s][:, j, :], wts[s][:, some], wf("expert_b", 0, P)[0:E, :],
                                               start=False, stop=True)
                            mm.then_inc(r_mul, 1)
                            for j in range(J):
                                pe.wait_ge(e_used, t * J + (j + 1))
                                for h in range(2):
                                    mm = pe.matmul(ps_e[j % 2][:, h, :], uf[s][:, j * P:(j + 1) * P],
                                                   wf("expert_w", h * CH, CH), start=True, stop=True)
                                mm.then_inc(e_mul, 1)

                @block.scalar
                def _(act):
                    act.sem_inc(e_mul, FREE * J)
                    act.sem_inc(r_mul, FREE)
                    with act.Fori(0, NC // 2) as i:
                        for s in range(2):
                            t = 2 * i + s
                            act.wait_ge(e_mul, t * J + J)
                            act.wait_ge(r_mul, t + 1)
                            act.activation(uf[s][:, :], u[:, bass.ds(t * CH, CH)], ACT.Copy).then_inc(fixed, 1)
                            act.activation(xf[s][:, :], xt[:, bass.ds(t * CH, CH)], ACT.Copy).then_inc(fixed, 1)
                            act.wait_ge(o_ready, t + 1)
                            act.activation(w1[s][:, :, :], wt[:, bass.ds(t * J, J), :], ACT.Copy).then_inc(fixed, 1)
                            act.wait_ge(w_mul, t + 1)
                            act.activation(wts[s][:, :], ps_w[:, :], ACT.Copy).then_inc(w_copied, 1)
                            act.wait_ge(r_mul, t + (1 + FREE))
                            act.activation(xr[s][:, :, :], ps_r[s][:, :, :], ACT.Copy).then_inc(r_copied, 1)

                @block.vector
                def _(dve):
                    dve.sem_inc(o_ready, FREE)
                    for s in range(2):
                        dve.sem_inc(o_stored[s], 16)
                    with dve.Fori(0, NC // 2) as i:
                        for s in range(2):
                            t = 2 * i + s
                            dve.wait_ge(r_copied, t + 1)
                            dve.wait_ge(o_stored[s], i * 16 + 16)
                            for j in range(J):
                                dve.wait_ge(e_mul, t * J + (j + 1 + FREE * J))
                                link = Steps(dve, step, (t * J + j) * (E - 1))
                                for e in range(E):
                                    ins = dve.scalar_tensor_tensor(
                                        o[s][:, j, :], ps_e[j % 2][:, e // 4, (e % 4) * P:(e % 4 + 1) * P],
                                                    w1[s][:, j, e:e + 1], xr[s][:, j, :] if e == 0 else o[s][:, j, :],
                                        ALU.mult, ALU.add)
                                    if e < E - 1:
                                        link(ins)
                                ins.then_inc(e_used, 1)
                            dve.wait_ge(e_used, t * J + (J + FREE))
                            dve.sem_inc(o_ready, 1)

                @block.sync
                def _(sp):
                    with sp.Fori(0, NC // 2) as i:
                        for s in range(2):
                            t = 2 * i + s
                            sp.wait_ge(o_ready, t + (1 + FREE))
                            sp.dma_start(out[bass.ds(t * CH, CH), :].rearrange("(j p) c -> p j c", p=P),
                                         o[s][:, :, :]).then_inc(o_stored[s], 16)
                    for s in range(2):
                        sp.wait_ge(o_stored[s], 16 * (NC // 2) + 16)


def pack(parts):
    import numpy as np
    at, n = {}, 0
    for name, a in parts:
        at[name] = (n, a.shape[1])
        n += a.shape[1]
    return np.ascontiguousarray(np.concatenate([a for _, a in parts], axis=1)), at


def getter(tensor, at):
    def get(name, i=None, n=1):
        o, w = at[name]
        return tensor[:, o:o + w] if i is None else tensor[:, o + i:o + i + n]
    return get


def constants():
    import numpy as np
    f = np.float32
    i = np.arange(P)
    parts = [
        ("ident", np.eye(P, dtype=f)),
        ("gmat", ((i[:, None] // 4) == (i[None, :] // 4)).astype(f) / 4),
        ("ones128", np.full((P, P), 1 / 128, f)),
        ("ones256", np.full((P, P), 1 / 256, f)),
        ("heads", ((i[:, None] // 32) == (i[None, :] // 32)).astype(f)),
        ("later", (i[None, :] > i[:, None]).astype(f)),
        ("row8", ((i[:, None] % 8) == np.arange(8)[None, :]).astype(f)),
        ("rank8", np.broadcast_to(8 - np.arange(8, dtype=f), (P, 8))),
        ("eps", np.full((P, 1), 1e-5, f)),
        ("ones", np.ones((P, P), f)),
    ]
    return pack(parts)


def columns(**arrays):
    return list(arrays.items())


def layouts(a):
    import numpy as np

    def per_half(v):
        v = v.reshape(2, P, -1)
        return np.concatenate([v[0], v[1]], axis=1)

    def every(v):
        return np.broadcast_to(v.reshape(1, -1), (P, v.size))

    x_cm = np.ascontiguousarray(a["x"].reshape(N, P).T)
    xp = a["L0_conv_x_proj_w"]
    bc, dt = xp[:, 8:40], xp[:, 0:8]
    xproj = np.concatenate([bc, bc, bc, dt], axis=1)
    xproj = xproj.reshape(KD, 104, 2, P).transpose(3, 0, 2, 1)
    dtw = a["L0_conv_dt_w"].transpose(2, 0, 1).reshape(8, KD * 256)
    wa, wa_at = pack(columns(
        win=a["L0_conv_w_in"].T,
        conv_w=per_half(a["L0_conv_conv_w"].reshape(256, 9)),
        conv_b=per_half(a["L0_conv_conv_b"]),
        dt_b=a["L0_conv_dt_b"].reshape(KD * 2, P).T,
        a_log=a["L0_conv_A_logs"].reshape(KD * 2, P, NS).transpose(1, 0, 2).reshape(P, KD * 2 * NS),
        d_skip=a["L0_conv_Ds"].reshape(KD * 2, P).T,
        ln_w=per_half(a["L0_conv_ln_w"]), ln_b=per_half(a["L0_conv_ln_b"]),
        wout=per_half(a["L0_conv_w_out"].T),
    ))
    wb, wb_at = pack(columns(
        w_exp=a["L1_conv_W_exp"].T, b_exp=a["L1_conv_b_exp"].reshape(2, P).T,
        w_con=a["L1_conv_W_con"].T, b_con=a["L1_conv_b_con"].reshape(1, P).T,
    ))
    qkv = a["L2_attn_W_qkv"].T
    col = lambda v: v.reshape(1, P).T
    wc, wc_at = pack(columns(
        w_q=qkv[:, 0:P], w_k=qkv[:, P:2 * P], w_v=qkv[:, 2 * P:3 * P], w_o=a["L2_attn_W_out"].T,
        b_out=col(a["L2_attn_b_out"]), gn_w=col(a["L2_attn_gn_w"]), gn_b=col(a["L2_attn_gn_b"]),
    ))
    wd, wd_at = pack(columns(
        sigma=every(a["L2_ffn_sigma"]), logw=every(a["L2_ffn_log_weights"]), gumbel=every(a["L2_ffn_gumbel"]),
    ))
    w1, eight = a["L3_attn_W1"], 8
    we, we_at = pack(columns(
        w1f=np.repeat(w1[:P], eight, axis=1), w1g=np.repeat(w1[P:], eight, axis=1),
        b1=np.repeat(a["L3_attn_b1"], eight)[:, None], w2=np.repeat(a["L3_attn_w2"][:, 0], eight)[:, None],
        b2=every(a["L3_attn_b2"]),
    ))
    wf, wf_at = pack(columns(
        router=a["L3_ffn_router_w"], router_b=every(a["L3_ffn_router_b"]),
        expert_w=a["L3_ffn_expert_w"].transpose(1, 0, 2).reshape(P, 8 * P),
        expert_b=np.concatenate([a["L3_ffn_expert_b"], np.zeros((P - 8, P), np.float32)]),
    ))
    phi = np.zeros((16, 2, L // 2 + P + 1), np.float32)
    phi[:, :, P + 1:] = a["L2_ffn_phi"].reshape(L // 2, 2, 16).transpose(2, 1, 0)
    more = {"wc": wc, "wd": wd, "we": we, "wf": wf, "phi": phi.reshape(16, -1),
            "m_u": a["L2_ffn_M_u"].transpose(2, 0, 1, 3).reshape(P, -1),
            "m_plus": a["L2_ffn_M_phi_plus"].transpose(2, 0, 1, 3).reshape(P, -1),
            "m_minus": a["L2_ffn_M_phi_minus"].transpose(2, 0, 1, 3).reshape(P, -1)}
    sel = np.zeros((96, 32, P), np.float32)
    for n in range(32):
        sel[n::32, n, :] = 1
    cmn, cmn_at = constants()
    arrays = {"x_cm": x_cm, "common": cmn, "wa": wa, "wb": wb,
              "xproj": np.ascontiguousarray(xproj.reshape(P, -1)), "dtw": np.ascontiguousarray(dtw),
              "sel": sel.reshape(96, -1)}
    arrays.update({n: np.ascontiguousarray(v) for n, v in more.items()})
    return arrays, {"common": cmn_at, "wa": wa_at, "wb": wb_at, "wc": wc_at, "wd": wd_at, "we": we_at, "wf": wf_at}


def load(nc, pairs, name):
    with ExitStack() as ctx:
        p = Place(nc, ctx)
        loaded = p.sem(name + "_loaded")
        with nc.Block() as block:
            @block.sync
            def _(sp):
                for tile, array in pairs:
                    sp.dma_start(tile, array).then_inc(loaded, 16)
                sp.wait_ge(loaded, 16 * len(pairs))


def store_cm(nc, xt, dram, name):
    with ExitStack() as ctx:
        p = Place(nc, ctx)
        stored = p.sem(name + "_stored")
        with nc.Block() as block:
            @block.sync
            def _(sp):
                sp.dma_start(dram, xt[:, :]).then_inc(stored, 16)
                sp.wait_ge(stored, 16)


def scan_layer(nc, cm, d, at, gscale, gshift):
    with ExitStack() as ctx:
        p = Place(nc, ctx)
        wat = p.sb("wa_sb", list(d["wa"].shape))
        wa = getter(wat, at["wa"])
        y = p.sb("y", [P, 2, B, HH, WW])
        load(nc, [(wat[:, :], d["wa"])], "wa")
        with ExitStack() as inner:
            p2 = Place(nc, inner)
            xc = p2.sb("xc", [P, 2, B, HH, WW])
            xt = y[:, 0].rearrange("p b h w -> p (b h w)")
            wide_sel = y[0:96, 1, 0].rearrange("p h w -> p (h w)")
            load_residual(nc, xt, d["x_cm"], "l0")
            group_stats(nc, xt, cm, gscale, gshift, "gn0")
            conv_branch(nc, xt, cm, wa, gscale, gshift, xc)
            sel = p2.sb("sel_sb", [96, 2 * NS, P], BF16)
            xproj = p2.sb("xproj_sb", [P, KD, 2, 104])
            dtw = p2.sb("dtw_sb", [P, KD, 2 * P])
            sel_cast = p2.sem("sel_cast")
            load(nc, [(wide_sel, d["sel"]), (xproj[:, :, :, :].rearrange("p k f r -> p (k f r)"), d["xproj"]),
                      (dtw[96:104, :, :].rearrange("p k c -> p (k c)"), d["dtw"])], "scan_w")
            with nc.Block() as block:
                @block.vector
                def _(dve):
                    dve.tensor_copy(sel[:, :, :].rearrange("p n m -> p (n m)"), wide_sel).then_inc(sel_cast, 1)
            selective_scan(nc, cm, wa, sel, xproj, dtw, xc, y)
        z = p.sb("z", [P, 2, N])
        xt = p.sb("xt0", [P, N])
        load_residual(nc, xt, d["x_cm"], "l0b")
        gated_output(nc, xt, cm, wa, gscale, gshift, y, z)
        store_cm(nc, xt, d["spill"], "l0c")


def build(nc, d, at, out):
    with ExitStack() as top:
        p = Place(nc, top)
        cmt = p.sb("common_sb", list(d["common"].shape))
        cm = getter(cmt, at["common"])
        gscale = p.sb("gscale", [P, B])
        gshift = p.sb("gshift", [P, B])
        load(nc, [(cmt[:, :], d["common"])], "common")
        scan_layer(nc, cm, d, at, gscale, gshift)
        xt = p.sb("xt", [P, N])
        tiles = {name: p.sb(name + "_sb", list(d[name].shape)) for name in ("wb", "wc", "wd", "we", "wf")}
        w = {name: getter(tile, at[name]) for name, tile in tiles.items()}
        load_residual(nc, xt, d["spill"], "l1")
        load(nc, [(tile[:, :], d[name]) for name, tile in tiles.items()], "weights")
        group_stats(nc, xt, cm, gscale, gshift, "gn1")
        ema_gate(nc, xt, cm, w["wb"], gscale, gshift)
        u = p.sb("normed", [P, N])
        layer_norm(nc, xt, cm, u, "n2a")
        linear_attention(nc, xt, cm, w["wc"], u)
        layer_norm(nc, xt, cm, u, "n2f")
        spectral_ffn(nc, xt, cm, w["wd"], d, u)
        layer_norm(nc, xt, cm, u, "n3a")
        additive_attention(nc, xt, cm, w["we"], u)
        layer_norm(nc, xt, cm, u, "n3f")
        expert_ffn(nc, xt, cm, w["wf"], u, out)


def kernel(**inputs):
    import numpy as np
    import concourse.bacc as bacc
    from concourse.bass_utils import run_bass_kernel_spmd

    arrays, at = layouts({name: np.asarray(v) for name, v in inputs.items()})
    nc = bacc.Bacc("TRN2", target_bir_lowering=False, num_devices=1)
    d = {name: nc.dram_tensor(f"in_{name}_dram", v.shape, mybir.dt.from_np(v.dtype), kind="ExternalInput").ap()
         for name, v in arrays.items()}
    d["spill"] = nc.dram_tensor("residual_spill", [P, N], F32).ap()
    out = nc.dram_tensor("out_0_dram", [N, P], F32, kind="ExternalOutput").ap()
    build(nc, d, at, out)
    r = run_bass_kernel_spmd(nc, [{f"in_{name}_dram": v for name, v in arrays.items()}], core_ids=[0])
    return r.results[0]["out_0_dram"].reshape(B, HH, WW, P)
```

```python
from contextlib import ExitStack

import concourse.bass as bass
from concourse import mybir

F32 = mybir.dt.float32
BF16 = mybir.dt.bfloat16
ACT = mybir.ActivationFunctionType
ALU = mybir.AluOpType
AX_X = mybir.AxisListType.X

P = 128
B = 2
HH = WW = 64
L = HH * WW
N = B * L
CH = 512
NC = N // CH
CB = L // CH
ROWS = CH // WW
PAD = WW + 2
FREE = 2
LAST = 1
KD = 4
NS = 16
LN_SET = "natural_log_exp_and_others"


def halves(ap, n):
    a = [list(x) for x in ap.ap]
    return bass.AP(tensor=ap.tensor, offset=ap.offset, ap=[a[0], [0, n]] + a[1:])


def inside(ap, n):
    return bass.AP(tensor=ap.tensor, offset=ap.offset, ap=[list(x) for x in ap.ap] + [[0, n]])


class Place:

    def __init__(self, nc, ctx):
        self.nc, self.ctx, self.sems = nc, ctx, []
        ctx.callback(self.clear)

    def sb(self, name, shape, dt=F32):
        return self.ctx.enter_context(self.nc.sbuf_tensor(name, shape, dt))

    def ps(self, name, shape, dt=F32):
        return self.ctx.enter_context(self.nc.psum_tensor(name, shape, dt))

    def sem(self, name):
        self.sems.append(self.nc.alloc_semaphore(name))
        return self.sems[-1]

    def clear(self):
        if self.sems:
            with self.nc.Block() as block:
                @block.gpsimd
                def _(pool):
                    for s in self.sems:
                        pool.sem_clear(s)
            for s in self.sems:
                self.nc.release_semaphore(s)


class Steps:

    def __init__(self, eng, sem, base=0):
        self.eng, self.sem, self.base, self.n = eng, sem, base, 0

    def __call__(self, ins):
        self.n += 1
        ins.then_inc(self.sem, 1)
        self.eng.wait_ge(self.sem, self.base + self.n)


def load_residual(nc, xt, x_cm, name):
    with ExitStack() as ctx:
        p = Place(nc, ctx)
        x_loaded = p.sem(name + "_x_loaded")
        with nc.Block() as block:
            @block.sync
            def _(sp):
                for q in range(4):
                    w = N // 4
                    sp.dma_start(xt[:, q * w:(q + 1) * w], x_cm[:, q * w:(q + 1) * w]).then_inc(x_loaded, 16)
                sp.wait_ge(x_loaded, 64)


def group_stats(nc, xt, cm, gscale, gshift, name):
    with ExitStack() as ctx:
        p = Place(nc, ctx)
        stats = p.sb(name + "_stats", [P, NC, 6])
        mv = p.sb(name + "_mv", [P, B, 2])
        ex = p.sb(name + "_ex", [P, B, 2])
        g = p.sb(name + "_g", [P, B, 2])
        var = p.sb(name + "_var", [P, B])
        std = p.sb(name + "_std", [P, B])
        pg = p.ps(name + "_pg", [P, CH])
        stats_ready = p.sem(name + "_stats_ready")
        step = p.sem(name + "_step")
        moments_ready = p.sem(name + "_moments_ready")
        group_ready = p.sem(name + "_group_ready")
        var_ready = p.sem(name + "_var_ready")
        std_ready = p.sem(name + "_std_ready")
        with nc.Block() as block:
            @block.vector
            def _(dve):
                with dve.Fori(0, NC) as i:
                    dve.bn_stats(stats[:, bass.ds(i, 1), :].rearrange("p a s -> p (a s)"),
                                 xt[:, bass.ds(i * CH, CH)]).then_inc(stats_ready, 1)
                dve.wait_ge(stats_ready, NC)
                link = Steps(dve, step)
                for b in range(B):
                    link(dve.bn_aggr(mv[:, b, :], stats[:, b * CB:(b + 1) * CB, :].rearrange("p a s -> p (a s)")))
                link(dve.tensor_tensor(ex[:, :, 1], mv[:, :, 0], mv[:, :, 0], ALU.mult))
                link(dve.tensor_copy(ex[:, :, 0], mv[:, :, 0]))
                dve.tensor_tensor(ex[:, :, 1], ex[:, :, 1], mv[:, :, 1], ALU.add).then_inc(moments_ready, 1)
                dve.wait_ge(group_ready, 1)
                link(dve.tensor_copy(g[:, :, :].rearrange("p b s -> p (b s)"), pg[:, 0:2 * B]))
                link(dve.tensor_tensor(var[:, :], g[:, :, 0], g[:, :, 0], ALU.mult))
                dve.tensor_tensor(var[:, :], g[:, :, 1], var[:, :], ALU.subtract).then_inc(var_ready, 1)
                dve.wait_ge(std_ready, 1)
                link(dve.reciprocal(gscale[:, :], std[:, :]))
                link(dve.scalar_tensor_tensor(gshift[:, :], g[:, :, 0], -1.0, gscale[:, :], ALU.mult, ALU.mult))

            @block.tensor
            def _(pe):
                pe.wait_ge(moments_ready, 1)
                pe.matmul(pg[:, 0:2 * B], cm("gmat"), ex[:, :, :].rearrange("p b s -> p (b s)"),
                          start=True, stop=True).then_inc(group_ready, 1)

            @block.scalar
            def _(act):
                act.wait_ge(var_ready, 1)
                act.activation(std[:, :], var[:, :], ACT.Sqrt, bias=cm("eps")).then_inc(std_ready, 1)


def conv_branch(nc, xt, cm, wa, gscale, gshift, xc):
    with ExitStack() as ctx:
        p = Place(nc, ctx)
        pad = p.sb("xi_pad", [P, B, PAD, PAD])
        diag = p.sb("conv_diag", [P, 2, 9, P])
        psx = [p.ps(f"psx{s}", [P, CH]) for s in range(2)]
        psc = [p.ps(f"psc{s}", [P, CH]) for s in range(2)]
        pad_zeroed = p.sem("pad_zeroed")
        diag_ready = p.sem("diag_ready")
        xn_ready = p.sem("xn_ready")
        xi_ready = p.sem("xi_ready")
        xi_padded = p.sem("xi_padded")
        conv_ready = p.sem("conv_ready")
        xc_ready = p.sem("xc_ready")
        with nc.Block() as block:
            @block.gpsimd
            def _(pool):
                pool.memset(pad[:, :, :, :], 0.0).then_inc(pad_zeroed, 1)

            @block.vector
            def _(dve):
                for b in range(B):
                    with dve.Fori(0, CB) as c:
                        x = xt[:, bass.ds(c * CH + b * L, CH)]
                        dve.tensor_scalar(x, x, gscale[:, b:b + 1], gshift[:, b:b + 1],
                                          ALU.mult, ALU.add).then_inc(xn_ready, 1)
                for half in range(2):
                    for tap in range(9):
                        dve.tensor_scalar(diag[:, half, tap, :], cm("ident"), wa("conv_w", 9 * half + tap), None,
                                          ALU.mult).then_inc(diag_ready, 1)
                dve.wait_ge(pad_zeroed, 1)
                for half in range(2):
                    for b in range(B):
                        if half == 1:
                            dve.wait_ge(conv_ready, (b + 1) * CB)
                        with dve.Fori(0, CB // 2) as i:
                            for s in range(2):
                                c = 2 * i + s
                                dve.wait_ge(xi_ready, c + (half * NC + b * CB + 1))
                                dve.tensor_copy(pad[:, b, bass.ds(c * ROWS + 1, ROWS), 1:1 + WW],
                                                psx[s][:, :].rearrange("p (h w) -> p h w", w=WW)).then_inc(xi_padded, 1)

            @block.tensor
            def _(pe):
                pe.sem_inc(xi_padded, FREE)
                pe.sem_inc(xc_ready, FREE)
                for half in range(2):
                    with pe.Fori(0, NC // 2) as i:
                        for s in range(2):
                            t = 2 * i + s
                            if half == 0:
                                pe.wait_ge(xn_ready, t + 1)
                            pe.wait_ge(xi_padded, t + (half * NC + 1))
                            pe.matmul(psx[s][:, :], wa("win", half * P, P), xt[:, bass.ds(t * CH, CH)],
                                      start=True, stop=True).then_inc(xi_ready, 1)
                    pe.wait_ge(diag_ready, 18)
                    for b in range(B):
                        pe.wait_ge(xi_padded, FREE + half * NC + (b + 1) * CB)
                        with pe.Fori(0, CB // 2) as i:
                            for s in range(2):
                                c = 2 * i + s
                                pe.wait_ge(xc_ready, c + (half * NC + b * CB + 1))
                                for tap in range(9):
                                    dy, dx = divmod(tap, 3)
                                    mm = pe.matmul(psc[s][:, :], diag[:, half, tap, :],
                                                   pad[:, b, bass.ds(c * ROWS + dy, ROWS), dx:dx + WW],
                                                   start=(tap == 0), stop=(tap == 8))
                                mm.then_inc(conv_ready, 1)

            @block.scalar
            def _(act):
                act.preload_act_table(ACT.Silu)
                for half in range(2):
                    with act.Fori(0, NC // 2) as i:
                        for s in range(2):
                            t = 2 * i + s
                            act.wait_ge(conv_ready, t + (half * NC + 1))
                            act.activation(xc[:, half].rearrange("p b h w -> p (b h w)")[:, bass.ds(t * CH, CH)],
                                           psc[s][:, :], ACT.Silu, bias=wa("conv_b", half)).then_inc(xc_ready, 1)


def selective_scan(nc, cm, wa, sel, xproj, dtw, xc, y):
    with ExitStack() as ctx:
        p = Place(nc, ctx)
        neg_a = p.sb("neg_a", [P, KD, 2, NS])
        d_sum = p.sb("d_sum", [P, 2])
        sq_bias = p.sb("sq_bias", [P, 1])
        split = [p.sb(f"bc_split{s}", [96, CH], BF16) for s in range(2)]
        rest = p.sb("bc_rest", [P, CH])
        poly = p.sb("poly", [P, 2, CH])
        delta = [p.sb(f"delta{s}", [P, 2, CH]) for s in range(2)]
        u = [p.sb(f"u{s}", [P, 2, CH]) for s in range(2)]
        c_sb = [p.sb(f"c_sb{s}", [P, CH]) for s in range(2)]
        da = [p.sb(f"da{s}", [P, 2, CH]) for s in range(2)]
        dbx = [p.sb(f"dbx{s}", [P, 2, CH]) for s in range(3)]
        h = [p.sb(f"h{s}", [P, 2, CH]) for s in range(2)]
        state = p.sb("state", [P, 2, 2, NS])
        ps_xd = p.ps("ps_xd", [P, CH])
        ps_dt = p.ps("ps_dt", [P, 2, CH])
        ps_b = [p.ps(f"ps_b{s}", [P, CH]) for s in range(2)]
        ps_c = p.ps("ps_c", [P, CH])
        ps_y = p.ps("ps_y", [P, 2, CH])
        a_clamped = p.sem("a_clamped")
        d_ready = p.sem("d_ready")
        a_exp = p.sem("a_exp")
        a_ready = p.sem("a_ready")
        y_started = p.sem("y_started")
        xd_ready = p.sem("xd_ready")
        hi_ready = p.sem("hi_ready")
        dts_ready = p.sem("dts_ready")
        rest_ready = p.sem("rest_ready")
        mid_ready = p.sem("mid_ready")
        split_mid_ready = p.sem("split_mid_ready")
        split_low_ready = p.sem("split_low_ready")
        dt_ready = p.sem("dt_ready")
        abs_ready = p.sem("abs_ready")
        e_ready = p.sem("e_ready")
        ln_ready = p.sem("ln_ready")
        sq_ready = p.sem("sq_ready")
        far_ready = p.sem("far_ready")
        near_ready = p.sem("near_ready")
        log_ready = p.sem("log_ready")
        relu_ready = p.sem("relu_ready")
        delta_ready = p.sem("delta_ready")
        u_ready = p.sem("u_ready")
        b_ready = p.sem("b_ready")
        c_ready = p.sem("c_ready")
        c_copied = p.sem("c_copied")
        da_ready = p.sem("da_ready")
        dbx_ready = p.sem("dbx_ready")
        scanned = p.sem("scanned")
        state_reset = p.sem("state_reset")
        state_saved = p.sem("state_saved")
        hc_ready = p.sem("hc_ready")
        y_summed = p.sem("y_summed")
        y_added = p.sem("y_added")
        H2 = 2 * NS
        slot = [n % 3 for n in range(NS - 1)] + [1]
        ago = [min(m for m in range(1, NS) if slot[n - m] == slot[n]) for n in range(NS)]

        def piece(t_x, k, b, c, half=None):
            c = c if k < 2 else c * -1 + (CB - 1)
            some = bass.ds(c * ROWS, ROWS)
            if half is not None:
                v = t_x[:, half, b:b + 1, some, :] if k % 2 == 0 else t_x[:, half, b:b + 1, :, some]
                return v.rearrange("p o h w -> p (o h) w" if k % 2 == 0 else "p o h w -> p (o w) h")
            v = t_x[:, :, b:b + 1, some, :] if k % 2 == 0 else t_x[:, :, b:b + 1, :, some]
            return v.rearrange("p f o h w -> p f (o h) w" if k % 2 == 0 else "p f o h w -> p f (o w) h")

        def grid(ap):
            return ap.rearrange("p f (a b) -> p f a b", b=WW)

        def pieces(eng, prepare, work):
            G = KD * B

            def at(g, c):
                g, c = (g - 1, c + CB) if isinstance(c, int) and c < 0 else (g, c)
                g, c = (g + 1, c - CB) if isinstance(c, int) and c >= CB else (g, c)
                return (g // B, g % B, c, c + g * CB) if 0 <= g < G else None

            for n in range(NS):
                prepare(n, *at(0, 0), 0)
            for g in range(G):
                def one(c, s):
                    work(g, *at(g, c), s, at(g, c - 1), at(g, c + 1))
                one(0, 0)
                with eng.Fori(0, CB // 2 - 1) as i:
                    for s in range(2):
                        one(2 * i + (s + 1), (s + 1) % 2)
                one(CB - 1, 1)

        with nc.Block() as block:
            @block.tensor
            def _(pe):
                pe.sem_inc(rest_ready, LAST)
                pe.sem_inc(dts_ready, LAST)
                pe.sem_inc(relu_ready, LAST)
                pe.sem_inc(y_added, LAST)
                pe.sem_inc(c_copied, LAST)
                pe.sem_inc(dbx_ready, FREE)

                def prepare(n, k, b, c, t, s):
                    if n == 1:
                        pe.wait_ge(rest_ready, t + 1)
                        pe.wait_ge(dts_ready, t + 1)
                        for half in range(2):
                            mm = pe.matmul(ps_xd[0:104, :], xproj[:, k, half, :], piece(xc, k, b, c, half),
                                           start=(half == 0), stop=(half == 1))
                        mm.then_inc(xd_ready, 1)
                    if n == 3:
                        pe.wait_ge(dts_ready, t + (1 + LAST))
                        pe.wait_ge(relu_ready, t + 1)
                        for half in range(2):
                            mm = pe.matmul(ps_dt[:, half, :], dtw[96:104, k, half * P:(half + 1) * P],
                                           rest[96:104, :], start=True, stop=True)
                        mm.then_inc(dt_ready, 1)

                def spread_b(n, t, s):
                    if n == 0:
                        pe.wait_ge(split_mid_ready, t + 1)
                        pe.wait_ge(split_low_ready, t + 1)
                    pe.wait_ge(dbx_ready, t * NS + (n + 1))
                    pe.matmul(ps_b[n % 2][:, :], sel[:, n, :], split[s][:, :], start=True, stop=True).then_inc(b_ready, 1)

                def add_y(n, t):
                    for half in range(2):
                        pe.wait_ge(hc_ready, t * H2 + (2 * n + half + 1 + 2 * FREE))
                        if n == 0:
                            pe.wait_ge(y_added, t + 1)
                        pe.matmul(ps_y[:, half, :], cm("ident"), h[n % 2][:, half, :],
                                  start=(n == 0), stop=(n == NS - 1)).then_inc(y_summed, 1)

                def work(g, k, b, c, t, s, before, after):
                    if not before:
                        spread_b(0, t, s)
                    for n in range(NS):
                        if n + 1 < NS:
                            spread_b(n + 1, t, s)
                        elif after:
                            spread_b(0, after[3], 1 - s)
                        pe.wait_ge(c_copied, t * NS + (n + 1))
                        pe.matmul(ps_c[:, :], sel[:, NS + n, :], split[s][:, :], start=True, stop=True).then_inc(c_ready, 1)
                        if n >= 2:
                            add_y(n - 2, t)
                        elif before:
                            add_y(n - 2 + NS, before[3])
                        if after:
                            prepare(n, *after, 1 - s)
                    if not after:
                        add_y(NS - 2, t)
                        add_y(NS - 1, t)

                pieces(pe, prepare, work)

            @block.scalar
            def _(act):
                act.preload_act_table_set(LN_SET)
                act.wait_ge(a_clamped, 1)
                act.activation(neg_a[:, :, :, :], neg_a[:, :, :, :], ACT.Exp).then_inc(a_exp, 1)
                act.sem_inc(scanned, 2 * FREE)
                act.sem_inc(hc_ready, 2 * FREE)
                act.sem_inc(delta_ready, LAST)

                def prepare(n, k, b, c, t, s):
                    if n == 2:
                        act.wait_ge(xd_ready, t + 1)
                        act.activation(split[s][:, :], ps_xd[0:96, :], ACT.Copy).then_inc(hi_ready, 1)
                        act.activation(rest[96:104, :], ps_xd[96:104, :], ACT.Copy).then_inc(dts_ready, 1)
                    if n == 4:
                        act.wait_ge(rest_ready, t + (1 + LAST))
                        act.activation(split[s][32:64, :], rest[32:64, :], ACT.Copy).then_inc(split_mid_ready, 1)
                        act.activation(split[s][64:96, :], rest[64:96, :], ACT.Copy).then_inc(mid_ready, 1)
                    if n == 5:
                        act.wait_ge(dt_ready, t + 1)
                        if not isinstance(t, int) or t >= 2:
                            act.wait_ge(dbx_ready, t * NS + (FREE - NS))
                        for half in range(2):
                            ins = act.activation(u[s][:, half, :], ps_dt[:, half, :], ACT.Abs,
                                                 bias=wa("dt_b", 2 * k + half))
                        ins.then_inc(abs_ready, 1)
                    if n == 6:
                        act.wait_ge(abs_ready, t + 1)
                        act.activation(u[s][:, :, :], u[s][:, :, :], ACT.Exp, scale=-1.0).then_inc(e_ready, 1)
                    if n == 7:
                        act.wait_ge(e_ready, t + 1)
                        act.activation(delta[s][:, :, :], u[s][:, :, :], ACT.Ln, bias=1.0).then_inc(ln_ready, 1)
                    if n == 7:
                        act.wait_ge(delta_ready, t + 1)
                        act.activation(poly[:, :, :], u[s][:, :, :], ACT.Square, scale=3.0 ** -0.5,
                                       bias=sq_bias[:, :]).then_inc(sq_ready, 1)
                    if n == 9:
                        act.wait_ge(far_ready, t + 1)
                        act.wait_ge(near_ready, t + 1)
                        for half in range(2):
                            ins = act.activation(u[s][:, half, :], ps_dt[:, half, :], ACT.Relu,
                                                 bias=wa("dt_b", 2 * k + half))
                        ins.then_inc(relu_ready, 1)

                def save(n, g, k, t):
                    last = CH - 1 if k < 2 else 0
                    for half in range(2):
                        act.wait_ge(scanned, t * H2 + (2 * n + half + 1 + 2 * FREE))
                        act.activation(state[:, g % 2, half, n:n + 1], h[n % 2][:, half, last:last + 1],
                                       ACT.Copy).then_inc(state_saved, 1)

                def work(g, k, b, c, t, s, before, after):
                    act.wait_ge(delta_ready, t + (1 + LAST))
                    for n in range(NS):
                        for half in range(2):
                            act.wait_ge(scanned, t * H2 + (2 * n + half + 1))
                            act.activation(da[n % 2][:, half, :], delta[s][:, half, :], ACT.Exp,
                                           scale=neg_a[:, k, half, n:n + 1]).then_inc(da_ready, 1)
                        if n:
                            save(n - 1, g, k, t)
                        elif before:
                            save(NS - 1, before[0] * B + before[1], before[0], before[3])
                        act.wait_ge(c_ready, t * NS + (n + 1))
                        act.wait_ge(hc_ready, t * H2 + (2 * n + 2))
                        act.activation(c_sb[n % 2][:, :], ps_c[:, :], ACT.Copy).then_inc(c_copied, 1)
                        if after:
                            prepare(n, *after, 1 - s)
                    if not after:
                        save(NS - 1, g, k, t)

                act.wait_ge(a_ready, 2)
                pieces(act, prepare, work)

            @block.vector
            def _(dve):
                dve.tensor_scalar(neg_a[:, :, :, :].rearrange("p k f n -> p (k f n)"), wa("a_log", 0, KD * 2 * NS),
                                  83.0, None, ALU.min).then_inc(a_clamped, 1)
                dve.wait_ge(a_exp, 1)
                dve.tensor_scalar(neg_a[:, :, :, :], neg_a[:, :, :, :], -1.0, None, ALU.mult).then_inc(a_ready, 1)
                dve.memset(sq_bias[:, :], -(3.0 ** 0.5) / 4.0).then_inc(a_ready, 1)
                dve.tensor_reduce(d_sum[:, :], wa("d_skip", 0, KD * 2).rearrange("p (k f) -> p f k", f=2), AX_X,
                                  ALU.add).then_inc(d_ready, 1)
                dve.wait_ge(d_ready, 1)
                for half in range(2):
                    dve.tensor_scalar(y[:, half], xc[:, half], d_sum[:, half:half + 1], None,
                                      ALU.mult).then_inc(y_started, 1)
                dve.wait_ge(y_started, 2)
                dve.sem_inc(y_summed, 2 * FREE)
                dve.sem_inc(state_saved, H2)

                def prepare(n, k, b, c, t, s):
                    if n == 3:
                        dve.wait_ge(hi_ready, t + 1)
                        dve.tensor_tensor(rest[0:96, :], ps_xd[0:96, :], split[s][:, :], ALU.subtract).then_inc(rest_ready, 1)
                    if n == 5:
                        dve.wait_ge(mid_ready, t + 1)
                        dve.tensor_tensor(split[s][64:96, :], rest[64:96, :], split[s][64:96, :],
                                          ALU.subtract).then_inc(split_low_ready, 1)
                    if n == 8:
                        dve.wait_ge(ln_ready, t + 1)
                        dve.scalar_tensor_tensor(delta[s][:, :, :], u[s][:, :, :], 0.02, delta[s][:, :, :],
                                                 ALU.is_lt, ALU.add).then_inc(far_ready, 1)
                    if n == 8:
                        dve.wait_ge(sq_ready, t + 1)
                        dve.scalar_tensor_tensor(poly[:, :, :], poly[:, :, :], 13.0 / 16.0, u[s][:, :, :],
                                                 ALU.add, ALU.mult).then_inc(near_ready, 1)
                    if n == 9:
                        dve.wait_ge(far_ready, t + 1)
                        dve.wait_ge(near_ready, t + 1)
                        dve.tensor_tensor(poly[:, :, :], poly[:, :, :], delta[s][:, :, :],
                                          ALU.min).then_inc(log_ready, 1)
                    if n == 12:
                        dve.wait_ge(delta_ready, t + (1 + LAST))
                        dve.tensor_tensor(grid(u[s][:, :, :]), grid(delta[s][:, :, :]), piece(xc, k, b, c),
                                           ALU.mult).then_inc(u_ready, 1)

                def y_add(k, b, c, t):
                    part = piece(y, k, b, c)
                    dve.wait_ge(y_summed, t * H2 + (H2 + 2 * FREE))
                    dve.wait_ge(y_added, t + 1)
                    dve.tensor_tensor(part, part, grid(ps_y[:, :, :]), ALU.add).then_inc(y_added, 1)

                def scale_b(n, t, s):
                    if not (isinstance(t, int) and t == 0 and n < ago[n]):
                        dve.wait_ge(scanned, t * H2 + (2 * (n - ago[n] + 1) + 2 * FREE))
                    dve.wait_ge(b_ready, t * NS + (n + 1))
                    dve.tensor_tensor(dbx[slot[n]][:, :, :], u[s][:, :, :], halves(ps_b[n % 2][:, :], 2),
                                      ALU.mult).then_inc(dbx_ready, 1)

                def work(g, k, b, c, t, s, before, after):
                    if isinstance(c, int) and c == 0:
                        dve.wait_ge(state_reset, max(g, 1))
                    if not before:
                        dve.wait_ge(u_ready, t + 1)
                        scale_b(0, t, s)
                    order = slice(None) if k < 2 else slice(None, None, -1)
                    for n in range(NS):
                        r = n % 2
                        if n + 1 < NS:
                            scale_b(n + 1, t, s)
                        elif after:
                            dve.wait_ge(u_ready, after[3] + 1)
                            scale_b(0, after[3], 1 - s)
                        if n == 1 and before:
                            y_add(*before)
                        dve.wait_ge(dbx_ready, t * NS + (n + 1 + FREE))
                        for half in range(2):
                            dve.wait_ge(da_ready, t * H2 + (2 * n + half + 1))
                            dve.wait_ge(y_summed, t * H2 + (2 * n + half + 1))
                            dve.wait_ge(state_saved, t * H2 + (2 * n + half + 1))
                            dve.tensor_tensor_scan(h[r][:, half, order], da[r][:, half, order], dbx[slot[n]][:, half, order],
                                                   state[:, g % 2, half, n:n + 1], ALU.mult, ALU.add).then_inc(scanned, 1)
                        if after:
                            prepare(n, *after, 1 - s)
                    if not after:
                        y_add(k, b, c, t)

                pieces(dve, prepare, work)

            @block.gpsimd
            def _(pool):
                pool.memset(state[:, :, :, :], 0.0).then_inc(state_reset, 1)

                def prepare(n, k, b, c, t, s):
                    if n == 10:
                        pool.wait_ge(log_ready, t + 1)
                        pool.wait_ge(relu_ready, t + (1 + LAST))
                        pool.tensor_tensor(delta[s][:, :, :], poly[:, :, :], u[s][:, :, :], ALU.add).then_inc(delta_ready, 1)

                def work(g, k, b, c, t, s, before, after):
                    if g > 0 and isinstance(c, int) and c == 0:
                        pool.memset(state[:, (g + 1) % 2, :, :], 0.0).then_inc(state_reset, 1)
                    for n in range(NS):
                        for half in range(2):
                            part = h[n % 2][:, half, :]
                            pool.wait_ge(c_copied, t * NS + (n + 1 + LAST))
                            pool.wait_ge(state_saved, t * H2 + (2 * n + half + 1 + H2))
                            pool.tensor_tensor(part, part, c_sb[n % 2][:, :], ALU.mult).then_inc(hc_ready, 1)
                        if after:
                            prepare(n, *after, 1 - s)

                pieces(pool, prepare, work)


def gated_output(nc, xt, cm, wa, gscale, gshift, y, z):
    with ExitStack() as ctx:
        p = Place(nc, ctx)
        xn = [p.sb(f"xn{s}", [P, CH]) for s in range(2)]
        psz = [p.ps(f"psz{s}", [P, 2, CH]) for s in range(2)]
        xn_ready = p.sem("z_xn_ready")
        z_mul = p.sem("z_mul")
        z_ready = p.sem("z_ready")
        with nc.Block() as block:
            @block.vector
            def _(dve):
                dve.sem_inc(z_mul, FREE)
                for b in range(B):
                    with dve.Fori(0, CB // 2) as i:
                        for s in range(2):
                            t = 2 * i + (s + b * CB)
                            dve.wait_ge(z_mul, t + 1)
                            dve.tensor_scalar(xn[s][:, :], xt[:, bass.ds(t * CH, CH)], gscale[:, b:b + 1],
                                              gshift[:, b:b + 1], ALU.mult, ALU.add).then_inc(xn_ready, 1)

            @block.tensor
            def _(pe):
                pe.sem_inc(z_ready, FREE)
                with pe.Fori(0, NC // 2) as i:
                    for s in range(2):
                        t = 2 * i + s
                        pe.wait_ge(xn_ready, t + 1)
                        pe.wait_ge(z_ready, t + 1)
                        for half in range(2):
                            mm = pe.matmul(psz[s][:, half, :], wa("win", (2 + half) * P, P), xn[s][:, :],
                                           start=True, stop=True)
                        mm.then_inc(z_mul, 1)

            @block.scalar
            def _(act):
                act.preload_act_table(ACT.Silu)
                with act.Fori(0, NC // 2) as i:
                    for s in range(2):
                        t = 2 * i + s
                        act.wait_ge(z_mul, t + (1 + FREE))
                        act.activation(z[:, :, bass.ds(t * CH, CH)], psz[s][:, :, :], ACT.Silu).then_inc(z_ready, 1)
    with ExitStack() as ctx:
        p = Place(nc, ctx)
        d = [p.sb(f"d{s}", [P, 2, CH]) for s in range(2)]
        sq = [p.sb(f"sq{s}", [P, 2, CH]) for s in range(2)]
        lv = [p.sb(f"lv{s}", [P, CH]) for s in range(2)]
        psm = [p.ps(f"psm{s}", [P, CH]) for s in range(2)]
        psv = [p.ps(f"psv{s}", [P, CH]) for s in range(2)]
        pso = [p.ps(f"pso{s}", [P, CH]) for s in range(2)]
        mean_ready = p.sem("mean_ready")
        d_ready = p.sem("d_ready")
        sq_ready = p.sem("sq_ready")
        var_ready = p.sem("lvar_ready")
        ln_ready = p.sem("lln_ready")
        rstd_ready = p.sem("rstd_ready")
        norm_step = p.sem("norm_step")
        gated = p.sem("gated")
        out_ready = p.sem("out_ready")
        x_added = p.sem("x_added")
        y_flat = y[:, :].rearrange("p f b h w -> p f (b h w)")
        with nc.Block() as block:
            @block.tensor
            def _(pe):
                with pe.Fori(0, NC // 2) as i:
                    for s in range(2):
                        t = 2 * i + s
                        for half in range(2):
                            mm = pe.matmul(psm[s][:, :], cm("ones256"), y_flat[:, half, bass.ds(t * CH, CH)],
                                           start=(half == 0), stop=(half == 1))
                        mm.then_inc(mean_ready, 1)
                    for s in range(2):
                        t = 2 * i + s
                        pe.wait_ge(sq_ready, t + 1)
                        for half in range(2):
                            mm = pe.matmul(psv[s][:, :], cm("ones256"), sq[s][:, half, :],
                                           start=(half == 0), stop=(half == 1))
                        mm.then_inc(var_ready, 1)
                    for s in range(2):
                        t = 2 * i + s
                        pe.wait_ge(gated, t + 1)
                        for half in range(2):
                            mm = pe.matmul(pso[s][:, :], wa("wout", half * P, P), d[s][:, half, :],
                                           start=(half == 0), stop=(half == 1))
                        mm.then_inc(out_ready, 1)

            @block.scalar
            def _(act):
                act.preload_act_table_set(LN_SET)
                with act.Fori(0, NC // 2) as i:
                    for s in range(2):
                        t = 2 * i + s
                        act.wait_ge(d_ready, t + 1)
                        act.activation(sq[s][:, :, :], d[s][:, :, :], ACT.Square).then_inc(sq_ready, 1)
                    for s in range(2):
                        t = 2 * i + s
                        act.wait_ge(var_ready, t + 1)
                        act.activation(lv[s][:, :], psv[s][:, :], ACT.Ln, bias=cm("eps")).then_inc(ln_ready, 1)
                        act.wait_ge(ln_ready, t + 1)
                        act.activation(lv[s][:, :], lv[s][:, :], ACT.Exp, scale=-0.5).then_inc(rstd_ready, 1)

            @block.vector
            def _(dve):
                with dve.Fori(0, NC // 2) as i:
                    for s in range(2):
                        t = 2 * i + s
                        dve.wait_ge(mean_ready, t + 1)
                        dve.tensor_tensor(d[s][:, :, :], y_flat[:, :, bass.ds(t * CH, CH)], halves(psm[s][:, :], 2),
                                          ALU.subtract).then_inc(d_ready, 1)
                    for s in range(2):
                        t = 2 * i + s
                        dve.wait_ge(rstd_ready, t + 1)
                        link = Steps(dve, norm_step, t * 2)
                        for half in range(2):
                            link(dve.scalar_tensor_tensor(d[s][:, half, :], d[s][:, half, :], wa("ln_w", half),
                                                          lv[s][:, :], ALU.mult, ALU.mult))
                        for half in range(2):
                            ins = dve.scalar_tensor_tensor(d[s][:, half, :], d[s][:, half, :], wa("ln_b", half),
                                                           z[:, half, bass.ds(t * CH, CH)], ALU.add, ALU.mult)
                        ins.then_inc(gated, 1)
                    for s in range(2):
                        t = 2 * i + s
                        dve.wait_ge(out_ready, t + 1)
                        dve.tensor_tensor(y_flat[:, 0, bass.ds(t * CH, CH)], xt[:, bass.ds(t * CH, CH)], pso[s][:, :],
                                          ALU.add).then_inc(x_added, 1)


def ema_gate(nc, xt, cm, wb, gscale, gshift):
    with ExitStack() as ctx:
        p = Place(nc, ctx)
        prim = p.sb("prim", [P, N])
        gate = p.sb("gate", [P, B, WW, HH])
        decay = p.sb("decay", [P, WW, HH])
        b01 = p.sb("b01", [P, 1])
        xn = [p.sb(f"exn{s}", [P, CH]) for s in range(2)]
        prod = [p.sb(f"prod{s}", [P, CH]) for s in range(2)]
        psg = [p.ps(f"psg{s}", [P, CH]) for s in range(2)]
        psp = [p.ps(f"psp{s}", [P, CH]) for s in range(2)]
        pso = [p.ps(f"epso{s}", [P, CH]) for s in range(2)]
        const_step = p.sem("ema_const")
        xn_ready = p.sem("e_xn_ready")
        expanded = p.sem("expanded")
        gate_ready = p.sem("gate_ready")
        prim_ready = p.sem("prim_ready")
        averaged = p.sem("averaged")
        sig_ready = p.sem("sig_ready")
        prod_ready = p.sem("prod_ready")
        out_ready = p.sem("e_out_ready")
        x_added = p.sem("e_x_added")
        with nc.Block() as block:
            @block.vector
            def _(dve):
                link = Steps(dve, const_step)
                link(dve.tensor_scalar(b01[:, :], wb("b_exp", 1), 0.1, None, ALU.mult))
                link(dve.memset(decay[:, :, :], 0.9))
                link(dve.memset(decay[:, :, 0:1], 0.0))
                dve.sem_inc(expanded, FREE)
                for b in range(B):
                    with dve.Fori(0, CB // 2) as i:
                        for s in range(2):
                            t = 2 * i + (s + b * CB)
                            dve.wait_ge(expanded, t + 1)
                            dve.tensor_scalar(xn[s][:, :], xt[:, bass.ds(t * CH, CH)], gscale[:, b:b + 1],
                                              gshift[:, b:b + 1], ALU.mult, ALU.add).then_inc(xn_ready, 1)
                        for s in range(2):
                            t = 2 * i + (s + b * CB)
                            dve.wait_ge(expanded, t + (1 + FREE))
                            dve.tensor_scalar(prim[:, bass.ds(t * CH, CH)], psp[s][:, :], wb("b_exp", 0), None,
                                              ALU.add).then_inc(prim_ready, 1)
                for b in range(B):
                    dve.wait_ge(gate_ready, FREE + (b + 1) * CB)
                    row = gate[:, b].rearrange("p w h -> p (w h)")
                    dve.tensor_tensor_scan(row, decay[:, :, :].rearrange("p w h -> p (w h)"), row, 0.0,
                                           ALU.mult, ALU.add).then_inc(averaged, 1)
                dve.sem_inc(out_ready, FREE)
                for b in range(B):
                    dve.wait_ge(sig_ready, (b + 1) * CB)
                    dve.wait_ge(prim_ready, FREE + (b + 1) * CB)
                    with dve.Fori(0, CB // 2) as i:
                        for s in range(2):
                            c = 2 * i + s
                            t = 2 * i + (s + b * CB)
                            dve.wait_ge(out_ready, t + 1)
                            dve.tensor_tensor(prod[s][:, :].rearrange("p (h w) -> p h w", w=WW),
                                              prim[:, bass.ds(t * CH, CH)].rearrange("p (h w) -> p h w", w=WW),
                                              gate[:, b, :, bass.ds(c * ROWS, ROWS)].rearrange("p w h -> p h w"),
                                              ALU.mult).then_inc(prod_ready, 1)
                        for s in range(2):
                            t = 2 * i + (s + b * CB)
                            dve.wait_ge(out_ready, t + (1 + FREE))
                            x = xt[:, bass.ds(t * CH, CH)]
                            dve.scalar_tensor_tensor(x, pso[s][:, :], wb("b_con", 0), x,
                                                     ALU.add, ALU.add).then_inc(x_added, 1)

            @block.tensor
            def _(pe):
                pe.sem_inc(gate_ready, FREE)
                pe.sem_inc(prim_ready, FREE)
                with pe.Fori(0, NC // 2) as i:
                    for s in range(2):
                        t = 2 * i + s
                        pe.wait_ge(xn_ready, t + 1)
                        pe.wait_ge(gate_ready, t + 1)
                        pe.wait_ge(prim_ready, t + 1)
                        pe.matmul(psg[s][:, :], wb("w_exp", P, P), xn[s][:, :], start=True, stop=True)
                        pe.matmul(psp[s][:, :], wb("w_exp", 0, P), xn[s][:, :], start=True, stop=True)\
                            .then_inc(expanded, 1)
                pe.sem_inc(x_added, FREE)
                with pe.Fori(0, NC // 2) as i:
                    for s in range(2):
                        t = 2 * i + s
                        pe.wait_ge(prod_ready, t + 1)
                        pe.wait_ge(x_added, t + 1)
                        pe.matmul(pso[s][:, :], wb("w_con", 0, P), prod[s][:, :], start=True, stop=True)\
                            .then_inc(out_ready, 1)

            @block.scalar
            def _(act):
                act.wait_ge(const_step, 1)
                for b in range(B):
                    with act.Fori(0, CB // 2) as i:
                        for s in range(2):
                            c = 2 * i + s
                            act.wait_ge(expanded, c + (b * CB + 1 + FREE))
                            act.activation(gate[:, b, :, bass.ds(c * ROWS, ROWS)].rearrange("p w h -> p h w"),
                                           psg[s][:, :].rearrange("p (h w) -> p h w", w=WW), ACT.Identity,
                                           bias=b01[:, :], scale=0.1).then_inc(gate_ready, 1)
                act.preload_act_table(ACT.Sigmoid)
                for b in range(B):
                    act.wait_ge(averaged, b + 1)
                    row = gate[:, b].rearrange("p w h -> p (w h)")
                    with act.Fori(0, CB) as c:
                        part = row[:, bass.ds(c * CH, CH)]
                        act.activation(part, part, ACT.Sigmoid).then_inc(sig_ready, 1)


def layer_norm(nc, xt, cm, u, name):
    G = 4
    with ExitStack() as ctx:
        p = Place(nc, ctx)
        d = [p.sb(f"{name}_d{s}", [P, CH]) for s in range(G)]
        sq = [p.sb(f"{name}_sq{s}", [P, CH]) for s in range(G)]
        lv = [p.sb(f"{name}_lv{s}", [P, CH]) for s in range(G)]
        psm = [p.ps(f"{name}_psm{s}", [P, CH]) for s in range(G)]
        psv = [p.ps(f"{name}_psv{s}", [P, CH]) for s in range(G)]
        mean_ready = p.sem(name + "_mean_ready")
        d_ready = p.sem(name + "_d_ready")
        sq_ready = p.sem(name + "_sq_ready")
        var_ready = p.sem(name + "_var_ready")
        ln_ready = p.sem(name + "_ln_ready")
        rstd_ready = p.sem(name + "_rstd_ready")
        u_ready = p.sem(name + "_u_ready")
        with nc.Block() as block:
            @block.tensor
            def _(pe):
                with pe.Fori(0, NC // G) as i:
                    for s in range(G):
                        t = i * G + s
                        pe.matmul(psm[s][:, :], cm("ones128"), xt[:, bass.ds(t * CH, CH)],
                                  start=True, stop=True).then_inc(mean_ready, 1)
                    for s in range(G):
                        t = i * G + s
                        pe.wait_ge(sq_ready, t + 1)
                        pe.matmul(psv[s][:, :], cm("ones128"), sq[s][:, :],
                                  start=True, stop=True).then_inc(var_ready, 1)

            @block.scalar
            def _(act):
                act.preload_act_table_set(LN_SET)
                with act.Fori(0, NC // G) as i:
                    for s in range(G):
                        t = i * G + s
                        act.wait_ge(d_ready, t + 1)
                        act.activation(sq[s][:, :], d[s][:, :], ACT.Square).then_inc(sq_ready, 1)
                    for s in range(G):
                        t = i * G + s
                        act.wait_ge(var_ready, t + 1)
                        act.activation(lv[s][:, :], psv[s][:, :], ACT.Ln, bias=cm("eps")).then_inc(ln_ready, 1)
                        act.wait_ge(ln_ready, t + 1)
                        act.activation(lv[s][:, :], lv[s][:, :], ACT.Exp, scale=-0.5).then_inc(rstd_ready, 1)

            @block.vector
            def _(dve):
                dve.sem_inc(u_ready, LAST)
                with dve.Fori(0, NC // G) as i:
                    dve.wait_ge(u_ready, i * G + LAST)
                    for s in range(G):
                        t = i * G + s
                        dve.wait_ge(mean_ready, t + 1)
                        dve.tensor_tensor(d[s][:, :], xt[:, bass.ds(t * CH, CH)], psm[s][:, :],
                                          ALU.subtract).then_inc(d_ready, 1)
                    for s in range(G):
                        t = i * G + s
                        dve.wait_ge(rstd_ready, t + 1)
                        dve.tensor_tensor(u[:, bass.ds(t * CH, CH)], d[s][:, :], lv[s][:, :],
                                          ALU.mult).then_inc(u_ready, 1)


def linear_attention(nc, xt, cm, wc, u):
    H, DH = 4, 32
    J = CH // P
    with ExitStack() as ctx:
        p = Place(nc, ctx)
        k = p.sb("k", [P, B, L])
        q_t = p.sb("q_t", [P, B, L])
        kmax = p.sb("kmax", [P, B, CB])
        nmax = p.sb("nmax", [P, B])
        ctxs = p.sb("ctxs", [P, B, P + 1])
        m_out = p.sb("m_out", [P, B, P])
        stats = p.sb("a_stats", [P, NC, 6])
        with ExitStack() as inner:
            p2 = Place(nc, inner)
            psk = [p2.ps(f"psk{s}", [P, CH]) for s in range(2)]
            ke = [p2.sb(f"ke{s}", [P, CH]) for s in range(2)]
            uf = [p2.sb(f"uf{s}", [P, CH]) for s in range(2)]
            kt = p2.sb("kt", [P, J, P])
            vt = p2.sb("vt", [P, J, P + 1])
            q1 = p2.sb("q1", [P, J * H, DH])
            qm = p2.sb("qm", [P, J * H])
            qs = p2.sb("qs", [P, J * H])
            ps_kt = p2.ps("ps_kt", [P, J, P])
            ps_v = p2.ps("ps_v", [P, J, P])
            ps_q = p2.ps("ps_q", [P, J * H, DH])
            ps_qt = p2.ps("ps_qt", [P, CH])
            ps_ctx = p2.ps("ps_ctx", [P, CH])
            k_mul = p2.sem("k_mul")
            k_copied = p2.sem("k_copied")
            kmax_ready = p2.sem("kmax_ready")
            nmax_step = p2.sem("nmax_step")
            nmax_ready = p2.sem("nmax_ready")
            ones_set = p2.sem("ones_set")
            uf_ready = p2.sem("uf_ready")
            ke_ready = p2.sem("ke_ready")
            kt_mul = p2.sem("kt_mul")
            vq_mul = p2.sem("vq_mul")
            kt_ready = p2.sem("kt_ready")
            vt_ready = p2.sem("vt_ready")
            ctx_mul = p2.sem("ctx_mul")
            ctx_added = p2.sem("ctx_added")
            q_step = p2.sem("q_step")
            q_shifted = p2.sem("q_shifted")
            q_exp = p2.sem("q_exp")
            q_norm = p2.sem("q_norm")
            qt_mul = p2.sem("qt_mul")
            qt_ready = p2.sem("qt_ready")

            def over_head(ap):
                a = [list(x) for x in ap.ap]
                return bass.AP(tensor=ap.tensor, offset=ap.offset, ap=a + [[0, DH]])

            with nc.Block() as block:
                @block.tensor
                def _(pe):
                    pe.sem_inc(k_copied, FREE)
                    pe.sem_inc(vt_ready, LAST)
                    pe.sem_inc(q_shifted, LAST)
                    pe.sem_inc(kt_ready, LAST)
                    pe.sem_inc(ctx_added, LAST)
                    pe.sem_inc(qt_ready, LAST)
                    with pe.Fori(0, NC // 2) as i:
                        for s in range(2):
                            t = 2 * i + s
                            pe.wait_ge(k_copied, t + 1)
                            pe.matmul(psk[s][:, :], wc("w_k", 0, P), u[:, bass.ds(t * CH, CH)],
                                      start=True, stop=True).then_inc(k_mul, 1)
                    with pe.Fori(0, NC // 2) as i:
                        for s in range(2):
                            t = 2 * i + s
                            pe.wait_ge(uf_ready, t + 1)
                            pe.wait_ge(vt_ready, t + 1)
                            pe.wait_ge(q_shifted, t + 1)
                            for j in range(J):
                                pe.matmul(ps_v[:, j, :], uf[s][:, j * P:(j + 1) * P], wc("w_v", 0, P),
                                          start=True, stop=True)
                                mm = pe.matmul(ps_q[:, j * H:(j + 1) * H, :], uf[s][:, j * P:(j + 1) * P],
                                               wc("w_q", 0, P), start=True, stop=True)
                            mm.then_inc(vq_mul, 1)
                            pe.wait_ge(ke_ready, t + 1)
                            pe.wait_ge(kt_ready, t + 1)
                            for j in range(J):
                                mm = pe.transpose(ps_kt[:, j, :], ke[s][:, j * P:(j + 1) * P], cm("ident"))
                            mm.then_inc(kt_mul, 1)
                            pe.wait_ge(kt_ready, t + (1 + LAST))
                            pe.wait_ge(vt_ready, t + (1 + LAST))
                            pe.wait_ge(ctx_added, t + 1)
                            for j in range(J):
                                mm = pe.matmul(ps_ctx[:, 0:P + 1], kt[:, j, :], vt[:, j, :],
                                               start=(j == 0), stop=(j == J - 1))
                            mm.then_inc(ctx_mul, 1)
                            pe.wait_ge(q_norm, t + 1)
                            pe.wait_ge(qt_ready, t + 1)
                            for j in range(J):
                                mm = pe.transpose(ps_qt[:, j * P:(j + 1) * P],
                                                  q1[:, j * H:(j + 1) * H, :].rearrange("p h d -> p (h d)"), cm("ident"))
                            mm.then_inc(qt_mul, 1)

                @block.scalar
                def _(act):
                    act.preload_act_table(ACT.Exp)
                    k_flat = k[:, :, :].rearrange("p b l -> p (b l)")
                    q_flat = q_t[:, :, :].rearrange("p b l -> p (b l)")
                    with act.Fori(0, NC // 2) as i:
                        for s in range(2):
                            t = 2 * i + s
                            act.wait_ge(k_mul, t + 1)
                            act.activation(k_flat[:, bass.ds(t * CH, CH)], psk[s][:, :], ACT.Copy).then_inc(k_copied, 1)
                    act.wait_ge(nmax_ready, 1)
                    act.wait_ge(k_copied, NC + FREE)
                    for b in range(B):
                        with act.Fori(0, CB // 2) as i:
                            for s in range(2):
                                t = 2 * i + (s + b * CB)
                                act.activation(ke[s][:, :], k_flat[:, bass.ds(t * CH, CH)], ACT.Exp,
                                               bias=nmax[:, b:b + 1]).then_inc(ke_ready, 1)
                                act.wait_ge(q_shifted, t + (1 + LAST))
                                act.activation(q1[:, :, :], q1[:, :, :], ACT.Exp).then_inc(q_exp, 1)
                                act.wait_ge(kt_mul, t + 1)
                                act.activation(kt[:, :, :], ps_kt[:, :, :], ACT.Copy).then_inc(kt_ready, 1)
                                act.wait_ge(qt_mul, t + (1 + LAST))
                                act.activation(q_flat[:, bass.ds(t * CH, CH)], ps_qt[:, :], ACT.Copy,
                                               scale=DH ** -0.5).then_inc(qt_ready, 1)

                @block.vector
                def _(dve):
                    dve.memset(vt[:, :, P:P + 1], 1.0).then_inc(ones_set, 1)
                    dve.memset(ctxs[:, :, :], 0.0).then_inc(ones_set, 1)
                    kmax_flat = kmax[:, :, :].rearrange("p b c -> p (b c)")
                    k_flat = k[:, :, :].rearrange("p b l -> p (b l)")
                    with dve.Fori(0, NC // 2) as i:
                        for s in range(2):
                            t = 2 * i + s
                            dve.wait_ge(k_copied, t + (1 + FREE))
                            dve.tensor_reduce(kmax_flat[:, bass.ds(t, 1)], k_flat[:, bass.ds(t * CH, CH)], AX_X,
                                              ALU.max).then_inc(kmax_ready, 1)
                    dve.wait_ge(kmax_ready, NC)
                    dve.tensor_reduce(nmax[:, :], kmax[:, :, :], AX_X, ALU.max).then_inc(nmax_step, 1)
                    dve.wait_ge(nmax_step, 1)
                    dve.tensor_scalar(nmax[:, :], nmax[:, :], -1.0, None, ALU.mult).then_inc(nmax_ready, 1)
                    dve.wait_ge(ones_set, 2)
                    dve.sem_inc(vq_mul, FREE)
                    dve.sem_inc(qt_mul, LAST)
                    dve.sem_inc(ctx_mul, LAST)
                    for b in range(B):
                        with dve.Fori(0, CB // 2) as i:
                            for s in range(2):
                                t = 2 * i + (s + b * CB)
                                dve.wait_ge(vq_mul, t + 1)
                                dve.tensor_copy(uf[s][:, :], u[:, bass.ds(t * CH, CH)]).then_inc(uf_ready, 1)
                                dve.wait_ge(vq_mul, t + (1 + FREE))
                                link = Steps(dve, q_step, t * 3)
                                link(dve.tensor_reduce(qm[:, :], ps_q[:, :, :], AX_X, ALU.max))
                                dve.wait_ge(qt_mul, t + 1)
                                dve.tensor_tensor(q1[:, :, :], ps_q[:, :, :], over_head(qm[:, :]),
                                                  ALU.subtract).then_inc(q_shifted, 1)
                                dve.wait_ge(ctx_mul, t + 1)
                                dve.tensor_copy(vt[:, :, 0:P], ps_v[:, :, :]).then_inc(vt_ready, 1)
                                dve.wait_ge(q_exp, t + 1)
                                link(dve.tensor_reduce(qs[:, :], q1[:, :, :], AX_X, ALU.add))
                                link(dve.reciprocal(qs[:, :], qs[:, :]))
                                dve.tensor_tensor(q1[:, :, :], q1[:, :, :], over_head(qs[:, :]),
                                                  ALU.mult).then_inc(q_norm, 1)
                                dve.wait_ge(ctx_mul, t + (1 + LAST))
                                dve.wait_ge(ctx_added, t + 1)
                                dve.tensor_tensor(ctxs[:, b, :], ctxs[:, b, :], ps_ctx[:, 0:P + 1],
                                                  ALU.add).then_inc(ctx_added, 1)
        with ExitStack() as inner:
            p2 = Place(nc, inner)
            mv = p2.sb("a_mv", [P, B, 2])
            ex = p2.sb("a_ex", [P, B, 2])
            g = p2.sb("a_g", [P, B, 2])
            var = p2.sb("a_var", [P, B])
            std = p2.sb("a_std", [P, B])
            sc = p2.sb("a_sc", [P, B])
            sh = p2.sb("a_sh", [P, B])
            kinv = p2.sb("kinv", [P, B])
            ps_m = p2.ps("ps_m", [P, B, P])
            ps_g = p2.ps("ps_g", [P, CH])
            ps_o = [p2.ps(f"ps_o{s}", [P, CH]) for s in range(2)]
            step = p2.sem("m_step")
            ctx_ready = p2.sem("ctx_ready")
            m_mul = p2.sem("m_mul")
            m_ready = p2.sem("m_ready")
            o_mul = p2.sem("o_mul")
            o_ready = p2.sem("o_ready")
            stats_ready = p2.sem("o_stats_ready")
            moments_ready = p2.sem("o_moments_ready")
            group_ready = p2.sem("o_group_ready")
            var_ready = p2.sem("o_var_ready")
            std_ready = p2.sem("o_std_ready")
            scale_ready = p2.sem("scale_ready")
            o_scaled = p2.sem("o_scaled")
            x_added = p2.sem("o_x_added")
            with nc.Block() as block:
                @block.vector
                def _(dve):
                    link = Steps(dve, step)
                    link(dve.reciprocal(kinv[:, :], ctxs[:, :, P]))
                    for b in range(B):
                        ins = dve.scalar_tensor_tensor(ctxs[:, b, 0:P], ctxs[:, b, 0:P], kinv[:, b:b + 1], cm("heads"),
                                                       ALU.mult, ALU.mult)
                    ins.then_inc(ctx_ready, 1)
                    dve.wait_ge(m_mul, 1)
                    dve.tensor_copy(m_out[:, :, :], ps_m[:, :, :]).then_inc(m_ready, 1)
                    with dve.Fori(0, NC) as t:
                        dve.wait_ge(o_ready, t + (1 + FREE))
                        dve.bn_stats(stats[:, bass.ds(t, 1), :].rearrange("p a s -> p (a s)"),
                                     u[:, bass.ds(t * CH, CH)]).then_inc(stats_ready, 1)
                    dve.wait_ge(stats_ready, NC)
                    for b in range(B):
                        link(dve.bn_aggr(mv[:, b, :], stats[:, b * CB:(b + 1) * CB, :].rearrange("p a s -> p (a s)")))
                    link(dve.tensor_tensor(ex[:, :, 1], mv[:, :, 0], mv[:, :, 0], ALU.mult))
                    link(dve.tensor_copy(ex[:, :, 0], mv[:, :, 0]))
                    dve.tensor_tensor(ex[:, :, 1], ex[:, :, 1], mv[:, :, 1], ALU.add).then_inc(moments_ready, 1)
                    dve.wait_ge(group_ready, 1)
                    link(dve.tensor_copy(g[:, :, :].rearrange("p b s -> p (b s)"), ps_g[:, 0:2 * B]))
                    link(dve.tensor_tensor(var[:, :], g[:, :, 0], g[:, :, 0], ALU.mult))
                    dve.tensor_tensor(var[:, :], g[:, :, 1], var[:, :], ALU.subtract).then_inc(var_ready, 1)
                    dve.wait_ge(std_ready, 1)
                    link(dve.reciprocal(std[:, :], std[:, :]))
                    link(dve.tensor_scalar(sc[:, :], std[:, :], wc("gn_w", 0), None, ALU.mult))
                    link(dve.tensor_tensor(sh[:, :], g[:, :, 0], sc[:, :], ALU.mult))
                    dve.tensor_scalar(sh[:, :], sh[:, :], -1.0, wc("gn_b", 0), ALU.mult, ALU.add).then_inc(scale_ready, 1)
                    with dve.Fori(0, NC) as t:
                        dve.wait_ge(o_scaled, t + 1)
                        x = xt[:, bass.ds(t * CH, CH)]
                        dve.tensor_tensor(x, x, u[:, bass.ds(t * CH, CH)], ALU.add).then_inc(x_added, 1)

                @block.tensor
                def _(pe):
                    pe.wait_ge(ctx_ready, 1)
                    for b in range(B):
                        mm = pe.matmul(ps_m[:, b, :], ctxs[:, b, 0:P], wc("w_o", 0, P), start=True, stop=True)
                    mm.then_inc(m_mul, 1)
                    pe.wait_ge(m_ready, 1)
                    pe.sem_inc(o_ready, FREE)
                    for b in range(B):
                        with pe.Fori(0, CB // 2) as i:
                            for s in range(2):
                                t = 2 * i + (s + b * CB)
                                pe.wait_ge(o_ready, t + 1)
                                pe.matmul(ps_o[s][:, :], m_out[:, b, :],
                                          q_t[:, :, :].rearrange("p b l -> p (b l)")[:, bass.ds(t * CH, CH)],
                                          start=True, stop=True).then_inc(o_mul, 1)
                    pe.wait_ge(moments_ready, 1)
                    pe.matmul(ps_g[:, 0:2 * B], cm("ones128"), ex[:, :, :].rearrange("p b s -> p (b s)"),
                              start=True, stop=True).then_inc(group_ready, 1)

                @block.scalar
                def _(act):
                    with act.Fori(0, NC // 2) as i:
                        for s in range(2):
                            t = 2 * i + s
                            act.wait_ge(o_mul, t + 1)
                            act.activation(u[:, bass.ds(t * CH, CH)], ps_o[s][:, :], ACT.Identity,
                                           bias=wc("b_out", 0)).then_inc(o_ready, 1)
                    act.wait_ge(var_ready, 1)
                    act.activation(std[:, :], var[:, :], ACT.Sqrt, bias=cm("eps")).then_inc(std_ready, 1)
                    act.wait_ge(scale_ready, 1)
                    for b in range(B):
                        with act.Fori(0, CB) as c:
                            part = u[:, bass.ds(c * CH + b * L, CH)]
                            act.activation(part, part, ACT.Identity, scale=sc[:, b:b + 1],
                                           bias=sh[:, b:b + 1]).then_inc(o_scaled, 1)


def split_exactly(link, dve, x, scratch, high, low, scaled=None):
    if scaled is None:
        scaled = high
        link(dve.tensor_scalar(scaled, x, 4097.0, None, ALU.mult))
    link(dve.tensor_tensor(scratch, scaled, x, ALU.subtract))
    link(dve.tensor_tensor(high, scaled, scratch, ALU.subtract))
    link(dve.tensor_tensor(low, x, high, ALU.subtract))


def spectral_ffn(nc, xt, cm, wd, d, u):
    S4, K, T2 = 4, 16, L // 2
    TB = T2 // P
    AR = 3
    ALLM = K * P
    PW = T2 + 2 * P + 4
    F = 2 * K * PW // P
    parts = nc.dram_tensor("phi_parts", [2, 2 * K * PW], F32).ap()
    mixing = nc.dram_tensor("mixing", [P, K * 2 * P], F32).ap()
    with ExitStack() as ctx:
        p = Place(nc, ctx)
        mu = p.sb("mu", [P, AR, P])
        reach = p.sb("reach", [P, CB])
        gain = p.sb("gain", [P, CB])
        with ExitStack() as inner:
            p2 = Place(nc, inner)
            mp = [p2.sb(f"mp{i}", [P, ALLM]) for i in range(2)]
            mm_ = [p2.sb(f"mm{i}", [P, ALLM]) for i in range(2)]
            mus = p2.sb("mus", [P, S4, AR * P])
            acc_p = p2.sb("acc_p", [P, ALLM])
            acc_m = p2.sb("acc_m", [P, ALLM])
            small = p2.sb("small", [P, 8, S4])
            sig = p2.sb("sig", [P, K])
            msel = p2.sb("msel", [P, K, 2, P])
            phi_sb = p2.sb("phi_sb", [P, F])
            scaled = p2.sb("phi_scaled", [P, F])
            part = [p2.sb(f"phi_part{i}", [P, F]) for i in range(2)]
            phi_loaded = p2.sem("phi_loaded")
            phi_step = p2.sem("phi_step")
            stored = p2.sem("w_stored")
            m_loaded = [p2.sem(f"m_loaded{i}") for i in range(2)]
            mu_loaded = p2.sem("mu_loaded")
            step = p2.sem("w_step")
            shifted = p2.sem("w_shifted")
            expd = p2.sem("w_exp")
            root = p2.sem("sig_root")
            MIXED = 14
            CHOSEN = MIXED + 3 * S4 + 4
            with nc.Block() as block:
                @block.sync
                def _(sp):
                    sp.dma_start(mus[:, :, :].rearrange("p i n -> p (i n)"), d["m_u"]).then_inc(mu_loaded, 16)
                    for i in range(S4):
                        if i >= 2:
                            sp.wait_ge(step, MIXED + 2 * (i - 1))
                        sp.dma_start(mp[i % 2][:, :], d["m_plus"][:, i * ALLM:(i + 1) * ALLM]).then_inc(m_loaded[i % 2], 16)
                        sp.dma_start(mm_[i % 2][:, :], d["m_minus"][:, i * ALLM:(i + 1) * ALLM]).then_inc(m_loaded[i % 2], 16)

                    sp.dma_start(phi_sb[:, :], d["phi"]).then_inc(phi_loaded, 16)
                    sp.wait_ge(phi_step, 4)
                    for i in range(2):
                        sp.dma_start(parts[i, :].rearrange("(p f) -> p f", f=F), part[i][:, :]).then_inc(stored, 16)
                    sp.wait_ge(step, CHOSEN)
                    sp.dma_start(mixing, msel[:, :, :, :].rearrange("p k o e -> p (k o e)")).then_inc(stored, 16)
                    sp.wait_ge(stored, 48)

                @block.scalar
                def _(act):
                    act.activation(sig[:, :], wd("sigma", 0, K), ACT.Sqrt).then_inc(root, 1)
                    act.wait_ge(root, 1)
                    act.activation(sig[:, :], sig[:, :], ACT.Sqrt).then_inc(root, 1)
                    act.wait_ge(shifted, 1)
                    act.activation(small[:, 1, :], small[:, 0, :], ACT.Exp).then_inc(expd, 1)

                @block.vector
                def _(dve):
                    link = Steps(dve, step)
                    lg, ex, pr, hot, w, one = (small[:, i, :] for i in (0, 1, 2, 3, 4, 5))
                    scal = small[:, 7, :]
                    link(dve.tensor_tensor(lg, wd("logw", 0, S4), wd("gumbel", 0, S4), ALU.add))
                    link(dve.tensor_reduce(scal[:, 0:1], lg, AX_X, ALU.max))
                    dve.tensor_scalar(lg, lg, scal[:, 0:1], None, ALU.subtract).then_inc(shifted, 1)
                    dve.wait_ge(expd, 1)
                    link(dve.tensor_reduce(scal[:, 1:2], ex, AX_X, ALU.add))
                    link(dve.reciprocal(scal[:, 1:2], scal[:, 1:2]))
                    link(dve.tensor_scalar(pr, ex, scal[:, 1:2], None, ALU.mult))
                    link(dve.tensor_reduce(scal[:, 2:3], pr, AX_X, ALU.max))
                    link(dve.tensor_scalar(hot, pr, scal[:, 2:3], None, ALU.is_ge))
                    link(dve.tensor_tensor(one, hot, cm("rank8")[:, 0:S4], ALU.mult))
                    link(dve.tensor_reduce(scal[:, 3:4], one, AX_X, ALU.max))
                    link(dve.tensor_scalar(hot, one, scal[:, 3:4], None, ALU.is_equal))
                    link(dve.tensor_tensor(w, hot, pr, ALU.subtract))
                    link(dve.tensor_tensor(w, w, pr, ALU.add))
                    for src, dst in ((hot, reach), (w, gain)):
                        dve.tensor_scalar(dst[:, :], cm("ones")[:, 0:CB], src[:, 0:1], None, ALU.mult).then_inc(shifted, 1)
                    dve.wait_ge(shifted, 3)
                    n_shift = 3
                    for i in range(1, S4):
                        for src, dst in ((hot, reach), (w, gain)):
                            dve.tensor_scalar(dst[:, 0:CB >> i], dst[:, 0:CB >> i], src[:, i:i + 1], None,
                                              ALU.add).then_inc(shifted, 1)
                            n_shift += 1
                        dve.wait_ge(shifted, n_shift)
                    link(dve.memset(acc_p[:, :], 0.0))
                    link(dve.memset(acc_m[:, :], 0.0))
                    assert link.n == MIXED
                    for i in range(S4):
                        dve.wait_ge(m_loaded[i % 2], 32 * (i // 2 + 1))
                        for src, acc in ((mp, acc_p), (mm_, acc_m)):
                            link(dve.scalar_tensor_tensor(acc[:, :], src[i % 2][:, :], hot[:, i:i + 1], acc[:, :],
                                                          ALU.mult, ALU.add))
                    dve.wait_ge(mu_loaded, 16)
                    flat = mu[:, :, :].rearrange("p i n -> p (i n)")
                    link(dve.tensor_scalar(flat, mus[:, 0, :], hot[:, 0:1], None, ALU.mult))
                    for i in range(1, S4):
                        link(dve.scalar_tensor_tensor(flat, mus[:, i, :], hot[:, i:i + 1], flat, ALU.mult, ALU.add))
                    a3, b3 = (a[:, :].rearrange("p (k n) -> p k n", k=K) for a in (acc_p, acc_m))
                    link(dve.tensor_tensor(msel[:, :, 0, :], a3, b3, ALU.add))
                    link(dve.tensor_tensor(msel[:, :, 1, :], a3, b3, ALU.subtract))
                    dve.wait_ge(root, 2)
                    sa = [list(x) for x in sig[:, :].ap]
                    every = bass.AP(tensor=sig[:, :].tensor, offset=sig[:, :].offset, ap=sa + [[0, P]])
                    for par in range(2):
                        link(dve.tensor_tensor(msel[:, :, par, :], msel[:, :, par, :], every, ALU.mult))
                    assert link.n == CHOSEN
                    dve.wait_ge(phi_loaded, 16)
                    split_exactly(Steps(dve, phi_step), dve, phi_sb[:, :], scaled[:, :], part[0][:, :], part[1][:, :])
        acc = u
        utok = [p.sb(f"utok{i}", [P, B, 2, TB, P]) for i in range(2)]
        with ExitStack() as inner:
            p2 = Place(nc, inner)
            upad = p2.sb("upad", [P, B, 4 + L])
            uf = [p2.sb(f"suf{s}", [P, CH]) for s in range(2)]
            tx = [p2.sb(f"tx{s}", [P, 2, 2, P]) for s in range(2)]
            tx_scaled = [p2.sb(f"tx_scaled{s}", [P, 2, 2, P]) for s in range(2)]
            tx_diff = p2.sb("tx_diff", [P, 2, 2, P])
            tx_split = p2.sem("tx_split")
            ps_t = [p2.ps(f"ps_t{s}", [P, 2, 2, P]) for s in range(2)]
            ps_a = [p2.ps(f"ps_a{s}", [P, CH]) for s in range(2)]
            padded = p2.sem("u_padded")
            uf_ready = p2.sem("s_uf_ready")
            up_ready = p2.sem("s_up_ready")
            t_mul = p2.sem("s_t_mul")
            t_copied = p2.sem("s_t_copied")
            a_mul = p2.sem("s_a_mul")
            a_copied = p2.sem("s_a_copied")

            with nc.Block() as block:
                @block.vector
                def _(dve):
                    dve.memset(upad[:, :, 0:4], 0.0).then_inc(padded, 1)
                    dve.sem_inc(t_mul, FREE)
                    for b in range(B):
                        with dve.Fori(0, CB // 2) as i:
                            for s in range(2):
                                c = 2 * i + s
                                t = 2 * i + (s + b * CB)
                                dve.wait_ge(t_mul, t + 1)
                                dve.tensor_scalar(uf[s][:, ::-1], u[:, bass.ds(t * CH, CH)], reach[:, bass.ds(c, 1)], None,
                                                  ALU.mult).then_inc(uf_ready, 1)
                                dve.wait_ge(uf_ready, t + 1)
                                dve.tensor_scalar(upad[:, b, bass.ds(c * CH + 4, CH)], uf[s][:, ::-1], 1.0, None, ALU.mult).then_inc(up_ready, 1)
                                dve.wait_ge(a_mul, t + 1)
                                dve.tensor_scalar(acc[:, bass.ds(t * CH, CH)], ps_a[s][:, :], 1.0, None, ALU.mult).then_inc(a_copied, 1)
                                dve.wait_ge(t_copied, 2 * t + (2 + 2 * FREE))
                                split_exactly(Steps(dve, tx_split, t * 3 + 3 * FREE), dve, tx[s][:, :, :, :],
                                              tx_diff[:, :, :, :], utok[0][:, b, :, bass.ds(c * 2, 2), :],
                                              utok[1][:, b, :, bass.ds(c * 2, 2), :], tx_scaled[s][:, :, :, :])

                @block.tensor
                def _(pe):
                    pe.wait_ge(padded, 1)
                    pe.sem_inc(t_copied, 2 * FREE)
                    pe.sem_inc(a_copied, FREE)
                    for b in range(B):
                        with pe.Fori(0, CB // 2) as i:
                            for s in range(2):
                                c = 2 * i + s
                                t = 2 * i + (s + b * CB)
                                pe.wait_ge(uf_ready, t + 1)
                                pe.wait_ge(t_copied, 2 * t + 2)
                                for par in range(2):
                                    for j in range(2):
                                        mm = pe.transpose(ps_t[s][:, par, j, :],
                                                          uf[s][:, (2 * P + 1) - 2 * P * j - par:(4 * P) - 2 * P * j - par:2], cm("ident"))
                                mm.then_inc(t_mul, 1)
                                pe.wait_ge(up_ready, t + 1)
                                pe.wait_ge(a_copied, t + 1)
                                for a in range(AR):
                                    mm = pe.matmul(ps_a[s][:, :], mu[:, a, :], upad[:, b, bass.ds(c * CH + (4 - a), CH)],
                                                   start=(a == 0), stop=(a == AR - 1))
                                mm.then_inc(a_mul, 1)

                @block.scalar
                def _(act):
                    act.sem_inc(tx_split, 3 * FREE)
                    for b in range(B):
                        with act.Fori(0, CB // 2) as i:
                            for s in range(2):
                                t = 2 * i + (s + b * CB)
                                act.wait_ge(t_mul, t + (1 + FREE))
                                act.wait_ge(tx_split, 3 * t + 3)
                                act.activation(tx[s][:, :, :, :], ps_t[s][:, :, :, :], ACT.Copy).then_inc(t_copied, 1)
                                act.activation(tx_scaled[s][:, :, :, :], ps_t[s][:, :, :, :], ACT.Copy,
                                               scale=4097.0).then_inc(t_copied, 1)
        with ExitStack() as inner:
            p2 = Place(nc, inner)
            HALF, OVER = T2 // 2, T2 // 2 - (CH - P)
            near = [p2.sb(f"near{s}", [P, 2, 2, P + HALF + 1]) for s in range(2)]
            far = p2.sb("far", [P, 2, 2, T2 + 1 - OVER])
            mk = [p2.sb(f"mk{s}", [P, 2, P]) for s in range(2)]
            yk = [p2.sb(f"yk{s}", [P, 2, CH]) for s in range(2)]
            ps_y = [p2.ps(f"sps_y{s}", [P, 2, CH]) for s in range(2)]
            ps_o = [p2.ps(f"sps_o{s}", [P, CH]) for s in range(2)]
            near_loaded = [p2.sem(f"near_loaded{s}") for s in range(2)]
            far_loaded = p2.sem("far_loaded")
            mk_loaded = [p2.sem(f"mk_loaded{s}") for s in range(2)]
            k_done = p2.sem("k_done")
            y_mul = p2.sem("s_y_mul")
            ye_copied = p2.sem("s_ye_copied")
            yo_copied = p2.sem("s_yo_copied")
            o_mul = p2.sem("s_o_mul")
            o_added = p2.sem("s_o_added")
            x_added = p2.sem("s_x_added")
            units = [(b, par, c) for c in range(T2 // CH) for b in range(B) for par in range(2)]
            UN = len(units)
            R32 = mybir.dt.float32r
            with nc.Block() as block:
                @block.sync
                def _(sp):
                    sp.sem_inc(k_done, FREE)
                    sp.sem_inc(o_mul, FREE * UN)

                    def strips(k, part, x, w):
                        row = parts[part:part + 1, bass.ds(k * (2 * PW) + (P + 2 + x), w)]
                        return bass.AP(tensor=row.tensor, offset=row.offset, ap=[[1, P], [PW - 1, 2], [1, w]])

                    with sp.Fori(0, K // 2) as i:
                        for s in range(2):
                            k = 2 * i + s
                            sp.wait_ge(k_done, k + 1)
                            for part in range(2):
                                sp.dma_start(near[s][:, part, :, :],
                                             strips(k, part, -P, P + HALF + 1)).then_inc(near_loaded[s], 16)
                            sp.wait_ge(o_mul, k * UN + UN)
                            sp.dma_start(mk[s][:, :, :].rearrange("p o e -> p (o e)"),
                                         mixing[:, bass.ds(k * (2 * P), 2 * P)]).then_inc(mk_loaded[s], 16)
                            sp.wait_ge(k_done, k + (LAST + 1))
                            for part in range(2):
                                sp.dma_start(far[:, part, :, :],
                                             strips(k, part, OVER, T2 + 1 - OVER)).then_inc(far_loaded, 16)

                @block.tensor
                def _(pe):
                    pe.sem_inc(ye_copied, FREE)
                    pe.sem_inc(yo_copied, FREE)
                    pe.sem_inc(o_added, FREE)
                    with pe.Fori(0, K // 2) as i:
                        for s in range(2):
                            k = 2 * i + s

                            def mix(n):
                                pe.wait_ge(ye_copied, k * UN + (n + 1 + FREE))
                                pe.wait_ge(yo_copied, k * UN + (n + 1 + FREE))
                                pe.wait_ge(o_added, k * UN + (n + 1))
                                if n == 0:
                                    pe.wait_ge(mk_loaded[s], i * 16 + 16)
                                for par in range(2):
                                    mm = pe.matmul(ps_o[n % 2][:, :], mk[s][:, par, :], yk[n % 2][:, par, :],
                                                   start=(par == 0), stop=(par == 1))
                                mm.then_inc(o_mul, 1)

                            pe.wait_ge(near_loaded[s], i * 32 + 32)
                            for n, (b, par, c) in enumerate(units):
                                if c == HALF // CH and units[n - 1][2] < c:
                                    pe.wait_ge(far_loaded, k * 32 + 32)
                                pe.wait_ge(ye_copied, k * UN + (n + 1))
                                pe.wait_ge(yo_copied, k * UN + (n + 1))
                                tiles = 4 * c + 4
                                for tap in range(2):
                                    for j in range(tiles):
                                        lo = min(max(0, (j - 4 * c) * P), CH - 2 * P)
                                        x = c * CH - j * P + lo + (par if tap else 0)
                                        w = CH - lo
                                        strip, x = (near[s], x + P) if x + w <= HALF + 1 else (far, x - OVER)
                                        out = ps_y[n % 2][:, tap, lo:CH]
                                        tok = [utok[i][:, b, par if tap == 0 else 1 - par, j, :].bitcast(R32)
                                               for i in range(2)]
                                        hi, low = (strip[:, i, tap, x:x + w].bitcast(R32) for i in range(2))
                                        pe.matmul(out, tok[0], hi, start=(j == 0), stop=False)
                                        pe.matmul(out, tok[0], low, start=False, stop=False)
                                        mm = pe.matmul(out, tok[1], hi, start=False, stop=(j == tiles - 1))
                                mm.then_inc(y_mul, 1)
                                if n:
                                    mix(n - 1)
                            mix(UN - 1)

                @block.scalar
                def _(act):
                    with act.Fori(0, K // 2) as i:
                        for s in range(2):
                            k = 2 * i + s
                            for n in range(UN):
                                act.wait_ge(y_mul, k * UN + (n + 1))
                                act.activation(yk[n % 2][:, 0, :], ps_y[n % 2][:, 0, :], ACT.Copy).then_inc(ye_copied, 1)

                @block.vector
                def _(dve):
                    with dve.Fori(0, K // 2) as i:
                        for s in range(2):
                            k = 2 * i + s

                            def add(n):
                                dve.wait_ge(o_mul, k * UN + (n + 1 + FREE * UN))
                                b, par, c = units[n]
                                at = b * L + 2 * c * CH + par
                                part = acc[:, at:at + 2 * CH - par:2]
                                dve.tensor_tensor(part, part, ps_o[n % 2][:, :], ALU.add).then_inc(o_added, 1)

                            for n in range(UN):
                                dve.wait_ge(y_mul, k * UN + (n + 1))
                                if n == UN - 1:
                                    dve.sem_inc(k_done, 1)
                                dve.tensor_copy(yk[n % 2][:, 1, :], ps_y[n % 2][:, 1, :]).then_inc(yo_copied, 1)
                                if n:
                                    add(n - 1)
                            add(UN - 1)
                    dve.wait_ge(o_added, K * UN + FREE)
                    with dve.Fori(0, CB) as c:
                        for b in range(B):
                            x = xt[:, bass.ds(c * CH + b * L, CH)]
                            dve.scalar_tensor_tensor(x, acc[:, bass.ds(c * CH + b * L, CH)], gain[:, bass.ds(c, 1)], x,
                                                     ALU.mult, ALU.add).then_inc(x_added, 1)


def additive_attention(nc, xt, cm, we, u):
    A, R = 16, 8
    QB = P // R
    TI = L // P
    SEG = 8
    ST = TI // SEG
    QG = 4
    with ExitStack() as ctx:
        p = Place(nc, ctx)
        g_rep = p.sb("g_rep", [P, B, L])
        f_bias = p.sb("f_bias", [P, B, L // R])
        xtok = p.sb("xtok", [P, B * TI, P + 1])
        w2 = p.sb("w2", [P, QG, QG * R])
        with ExitStack() as inner:
            p2 = Place(nc, inner)
            uf = [p2.sb(f"auf{s}", [P, CH]) for s in range(2)]
            fm = [p2.sb(f"fm{s}", [P, CH // R, R]) for s in range(2)]
            ps_g = [p2.ps(f"aps_g{s}", [P, CH]) for s in range(2)]
            ps_f = [p2.ps(f"aps_f{s}", [P, CH]) for s in range(2)]
            ps_t = [p2.ps(f"aps_t{s}", [P, CH]) for s in range(2)]
            const_ready = p2.sem("a3_const")
            uf_ready = p2.sem("a_uf_ready")
            mul_ready = p2.sem("a_mul_ready")
            t_copied = p2.sem("a_t_copied")
            fm_ready = p2.sem("fm_ready")
            f_summed = p2.sem("f_summed")
            f_ready = p2.sem("f_ready")
            f_flat = f_bias[:, :, :].rearrange("p b n -> p (b n)")
            g_flat = g_rep[:, :, :].rearrange("p b n -> p (b n)")
            with nc.Block() as block:
                @block.vector
                def _(dve):
                    dve.memset(xtok[:, :, P:P + 1], 1.0).then_inc(const_ready, 1)
                    dve.memset(w2[:, :, :], 0.0).then_inc(const_ready, 1)
                    dve.wait_ge(const_ready, 2)
                    for m in range(QG):
                        dve.tensor_scalar(w2[:, m, m * R:(m + 1) * R], cm("row8"), we("w2", 0), None,
                                          ALU.mult).then_inc(const_ready, 1)
                    dve.sem_inc(mul_ready, FREE)
                    row = [list(x) for x in cm("row8").ap]
                    pick = bass.AP(tensor=cm("row8").tensor, offset=cm("row8").offset,
                                   ap=[row[0], [0, CH // R], row[1]])
                    with dve.Fori(0, NC // 2) as i:
                        for s in range(2):
                            t = 2 * i + s
                            dve.wait_ge(mul_ready, t + 1)
                            dve.tensor_copy(uf[s][:, :], u[:, bass.ds(t * CH, CH)]).then_inc(uf_ready, 1)
                        for s in range(2):
                            t = 2 * i + s
                            dve.wait_ge(mul_ready, t + (1 + FREE))
                            dve.tensor_tensor(fm[s][:, :, :], ps_f[s][:, :].rearrange("p (n r) -> p n r", r=R), pick,
                                              ALU.mult).then_inc(fm_ready, 1)
                        for s in range(2):
                            t = 2 * i + s
                            dve.wait_ge(fm_ready, t + 1)
                            dve.tensor_reduce(f_flat[:, bass.ds(t * (CH // R), CH // R)], fm[s][:, :, :], AX_X,
                                              ALU.add).then_inc(f_summed, 1)
                    dve.wait_ge(f_summed, NC)
                    dve.tensor_scalar(f_flat, f_flat, we("b1", 0), None, ALU.add).then_inc(f_ready, 1)

                @block.tensor
                def _(pe):
                    pe.sem_inc(t_copied, FREE)
                    with pe.Fori(0, NC // 2) as i:
                        for s in range(2):
                            t = 2 * i + s
                            pe.wait_ge(uf_ready, t + 1)
                            pe.wait_ge(t_copied, t + 1)
                            for j in range(CH // P):
                                pe.transpose(ps_t[s][:, j * P:(j + 1) * P], uf[s][:, j * P:(j + 1) * P], cm("ident"))
                            pe.matmul(ps_g[s][:, :], we("w1g", 0, P), uf[s][:, :], start=True, stop=True)
                            pe.matmul(ps_f[s][:, :], we("w1f", 0, P), uf[s][:, :], start=True, stop=True)\
                                .then_inc(mul_ready, 1)

                @block.scalar
                def _(act):
                    with act.Fori(0, NC // 2) as i:
                        for s in range(2):
                            t = 2 * i + s
                            act.wait_ge(mul_ready, t + (1 + FREE))
                            act.activation(g_flat[:, bass.ds(t * CH, CH)], ps_g[s][:, :], ACT.Copy)
                            act.activation(xtok[:, bass.ds(t * 4, 4), 0:P],
                                           ps_t[s][:, :].rearrange("p (j c) -> p j c", c=P), ACT.Copy)\
                                .then_inc(t_copied, 1)
        acc = p.sb("a_acc", [P, B * TI, P + 1])
        with ExitStack() as inner:
            p2 = Place(nc, inner)
            TH = 3
            th_own = p2.sb("th_own", [P, QG, SEG * P])
            th_u = u[:, :].rearrange("p (s j n) -> p s j n", s=TH - 1, j=QG)
            th = [th_u[:, 0], th_u[:, 1], th_own[:, :, :]]
            ago = [2] * (QG * SEG % TH) + [TH] * (QG * SEG - QG * SEG % TH)
            assert QG * SEG % TH == 2
            z_ready = p2.sem("z_sum_ready")
            e = [p2.sb(f"ae{s}", [P, SEG * P]) for s in range(2)]
            et = [p2.sb(f"et{s}", [P, SEG, P]) for s in range(2)]
            ps_s = [p2.ps(f"ps_s{s}", [P, SEG * P]) for s in range(2)]
            ps_e = p2.ps("ps_e", [P, SEG, P])
            ps_o = [p2.ps(f"aps_o{s}", [P, CH]) for s in range(2)]
            tanh_ready = p2.sem("tanh_ready")
            scored = p2.sem("scored")
            e_ready = p2.sem("ae_ready")
            e_turned = p2.sem("ae_turned")
            et_ready = p2.sem("et_ready")
            o_mul = p2.sem("ao_mul")
            o_added = p2.sem("ao_added")

            def runs(eng, run, finish):
                def on_diagonal(g):
                    return g * SEG, g * SEG, g * SEG, True

                run(on_diagonal(0), None)
                with eng.Fori(0, B * ST - 1) as i:
                    run(on_diagonal(i + 1), on_diagonal(i))
                last = on_diagonal(B * ST - 1)
                x0 = B * TI
                for seg in range(ST - 1):
                    n = ST - seg - 1
                    for b in range(B):
                        def full(i):
                            return i * SEG + x0, i * SEG + (b * TI + SEG * (seg + 1)), b * TI + seg * SEG, False

                        run(full(0), last)
                        if n == 2:
                            run(full(1), full(0))
                        elif n > 2:
                            with eng.Fori(0, n - 1) as i:
                                run(full(i + 1), full(i))
                        last = full(n - 1)
                        x0 += n * SEG
                finish(last)

            def unit(this, before, k):
                x0, tile0, key0, diagonal = this if k >= 0 else before
                kk = k % SEG
                return x0 + kk, tile0 + kk, key0, kk + 1 if diagonal else SEG, diagonal

            with nc.Block() as block:
                @block.scalar
                def _(act):
                    act.preload_act_table(ACT.Tanh)
                    act.sem_inc(e_turned, FREE)

                    def exp(this, before, k):
                        x, _, _, m, _ = unit(this, before, k)
                        act.wait_ge(scored, x * QG + (QG + TH))
                        act.wait_ge(e_turned, x + 1)
                        act.activation(e[k % 2][:, 0:m * P], ps_s[k % 2][:, 0:m * P], ACT.Exp,
                                       bias=we("b2", 0)).then_inc(e_ready, 1)

                    def run(this, before):
                        for k in range(SEG):
                            x, _, _, m, _ = unit(this, before, k)
                            for g in range(QG):
                                some = th[(k * QG + g) % TH][:, :, 0:m * P]
                                act.wait_ge(z_ready, x * QG + (g + 1))
                                act.activation(some, some, ACT.Tanh).then_inc(tanh_ready, 1)
                                if g == 0 and (k > 0 or before):
                                    exp(this, before, k - 1)

                    runs(act, run, lambda last: exp(None, last, -1))

                @block.tensor
                def _(pe):
                    pe.sem_inc(e_ready, FREE)
                    pe.sem_inc(et_ready, LAST)
                    pe.sem_inc(o_added, FREE)

                    def turn(this, before, k):
                        x, _, _, m, _ = unit(this, before, k)
                        pe.wait_ge(e_ready, x + (1 + FREE))
                        pe.wait_ge(et_ready, x + 1)
                        for j in range(m):
                            mm = pe.transpose(ps_e[:, j, :], e[k % 2][:, j * P:(j + 1) * P], cm("ident"))
                        mm.then_inc(e_turned, 1)

                    def weigh(this, before, k):
                        x, _, key0, m, _ = unit(this, before, k)
                        pe.wait_ge(et_ready, x + (1 + LAST))
                        pe.wait_ge(o_added, x + 1)
                        for j in range(m):
                            mm = pe.matmul(ps_o[k % 2][:, 0:P + 1], et[k % 2][:, j, :],
                                           xtok[:, bass.ds(key0 + j, 1), :].rearrange("p a c -> p (a c)"),
                                           start=(j == 0), stop=(j == m - 1))
                        mm.then_inc(o_mul, 1)

                    def run(this, before):
                        for k in range(SEG):
                            x, _, _, m, _ = unit(this, before, k)
                            pe.wait_ge(e_ready, x + 1)
                            for g in range(QG):
                                pe.wait_ge(tanh_ready, x * QG + (g + 1))
                                for h in range(0, m * P, CH):
                                    c = min(CH, m * P - h)
                                    for j in range(QG):
                                        mm = pe.matmul(ps_s[k % 2][32 * j:32 * (j + 1), h:h + c], w2[:, g, :],
                                                       th[(k * QG + g) % TH][:, j, h:h + c],
                                                       start=(g == 0), stop=(g == QG - 1))
                                mm.then_inc(scored, 1)
                                if g == 1 and (k > 0 or before):
                                    turn(this, before, k - 1)
                                if g == 2 and (k > 0 or before):
                                    weigh(this, before, k - 1)

                    def finish(last):
                        turn(None, last, -1)
                        weigh(None, last, -1)

                    runs(pe, run, finish)

                @block.vector
                def _(dve):
                    dve.sem_inc(o_mul, FREE)
                    dve.sem_inc(scored, TH)
                    f_flat = f_bias[:, :, :].rearrange("p b n -> p (b n)")
                    g_flat = g_rep[:, :, :].rearrange("p b n -> p (b n)")

                    def add(this, k, g):
                        x, tile, key0, m, _ = unit(this, None, k)
                        i = k * QG + g
                        dve.wait_ge(scored, x * QG + (g - ago[i] + TH + 1))
                        for j in range(QG):
                            ins = dve.tensor_scalar(th[i % TH][:, j, 0:m * P], g_flat[:, bass.ds(key0 * P, m * P)],
                                                    f_flat[:, bass.ds(tile * QB + (QG * j + g), 1)], None, ALU.add)
                        ins.then_inc(z_ready, 1)

                    def take(this, before, k):
                        x, _, _, m, diagonal = unit(this, before, k)
                        dve.wait_ge(e_turned, x + (1 + FREE))
                        dve.wait_ge(o_mul, x + 1)
                        whole = m - 1 if diagonal else m
                        if whole > 0:
                            ins = dve.tensor_copy(et[k % 2][:, 0:whole, :], ps_e[:, 0:whole, :])
                        if diagonal:
                            ins = dve.tensor_tensor(et[k % 2][:, whole, :], ps_e[:, whole, :], cm("later"), ALU.mult)
                        ins.then_inc(et_ready, 1)

                    def collect(this, before, k):
                        x, tile, _, _, diagonal = unit(this, before, k)
                        part = acc[:, bass.ds(tile, 1), :].rearrange("p a c -> p (a c)")
                        dve.wait_ge(o_mul, x + (1 + FREE))
                        if diagonal:
                            dve.tensor_copy(part, ps_o[k % 2][:, 0:P + 1]).then_inc(o_added, 1)
                        else:
                            dve.wait_ge(o_added, x + FREE)
                            dve.tensor_tensor(part, part, ps_o[k % 2][:, 0:P + 1], ALU.add).then_inc(o_added, 1)

                    def run(this, before):
                        for k in range(SEG):
                            for g in range(QG):
                                add(this, k, g)
                                if g == 0 and (k > 1 or before):
                                    take(this, before, k - 2)
                                if g == 1 and (k > 1 or before):
                                    collect(this, before, k - 2)

                    def finish(last):
                        take(None, last, -2)
                        collect(None, last, -2)
                        take(None, last, -1)
                        collect(None, last, -1)

                    runs(dve, run, finish)
        with ExitStack() as inner:
            p2 = Place(nc, inner)
            rden = p2.sb("rden", [P, B * TI])
            wn = [p2.sb(f"wn{s}", [P, CH // P, P]) for s in range(2)]
            ps_x = [p2.ps(f"aps_x{s}", [P, CH]) for s in range(2)]
            den_step = p2.sem("den_step")
            wn_ready = p2.sem("wn_ready")
            x_mul = p2.sem("ax_mul")
            x_added = p2.sem("ax_added")
            with nc.Block() as block:
                @block.vector
                def _(dve):
                    link = Steps(dve, den_step)
                    link(dve.tensor_scalar(rden[:, :], acc[:, :, P], 1e-10, None, ALU.add))
                    link(dve.reciprocal(rden[:, :], rden[:, :]))
                    with dve.Fori(0, NC // 2) as i:
                        for s in range(2):
                            t = 2 * i + s
                            part = rden[:, bass.ds(t * 4, 4)]
                            dve.tensor_tensor(wn[s][:, :, :], acc[:, bass.ds(t * 4, 4), 0:P], inside(part, P),
                                              ALU.mult).then_inc(wn_ready, 1)
                        for s in range(2):
                            t = 2 * i + s
                            dve.wait_ge(x_mul, t + 1)
                            x = xt[:, bass.ds(t * CH, CH)]
                            dve.tensor_tensor(x, x, ps_x[s][:, :], ALU.add).then_inc(x_added, 1)

                @block.tensor
                def _(pe):
                    with pe.Fori(0, NC // 2) as i:
                        for s in range(2):
                            t = 2 * i + s
                            pe.wait_ge(wn_ready, t + 1)
                            for j in range(CH // P):
                                mm = pe.transpose(ps_x[s][:, j * P:(j + 1) * P], wn[s][:, j, :], cm("ident"))
                            mm.then_inc(x_mul, 1)


def expert_ffn(nc, xt, cm, wf, u, out):
    E, J, T = 8, CH // P, N // P
    with ExitStack() as ctx:
        p = Place(nc, ctx)
        lg = p.sb("lg", [P, T, E])
        wt = p.sb("wt", [P, T, E])
        with ExitStack() as inner:
            p2 = Place(nc, inner)
            hot = p2.sb("f_hot", [P, T, E])
            hot2 = p2.sb("f_hot2", [P, T, E])
            sc = p2.sb("f_sc", [P, T, E])
            m1 = p2.sb("f_m1", [P, T])
            m2 = p2.sb("f_m2", [P, T])
            mx = p2.sb("f_mx", [P, T])
            uf = [p2.sb(f"fuf{s}", [P, CH]) for s in range(2)]
            ps_l = [p2.ps(f"ps_l{s}", [P, J, E]) for s in range(2)]
            uf_ready = p2.sem("f_uf_ready")
            l_mul = p2.sem("l_mul")
            l_ready = p2.sem("l_ready")
            step = p2.sem("f_step")
            shifted = p2.sem("f_shifted")
            expd = p2.sem("f_expd")
            rb = wf("router_b", 0, E)
            with nc.Block() as block:
                @block.scalar
                def _(act):
                    act.wait_ge(shifted, 1)
                    act.activation(lg[:, :, :], lg[:, :, :], ACT.Exp).then_inc(expd, 1)

                @block.tensor
                def _(pe):
                    with pe.Fori(0, NC // 2) as i:
                        for s in range(2):
                            t = 2 * i + s
                            pe.wait_ge(uf_ready, t + 1)
                            for j in range(J):
                                mm = pe.matmul(ps_l[s][:, j, :], uf[s][:, j * P:(j + 1) * P], wf("router", 0, E),
                                               start=True, stop=True)
                            mm.then_inc(l_mul, 1)

                @block.vector
                def _(dve):
                    with dve.Fori(0, NC // 2) as i:
                        for s in range(2):
                            t = 2 * i + s
                            dve.tensor_copy(uf[s][:, :], u[:, bass.ds(t * CH, CH)]).then_inc(uf_ready, 1)
                        for s in range(2):
                            t = 2 * i + s
                            dve.wait_ge(l_mul, t + 1)
                            dve.tensor_tensor(lg[:, bass.ds(t * J, J), :], ps_l[s][:, :, :], halves(rb, J),
                                              ALU.add).then_inc(l_ready, 1)
                    dve.wait_ge(l_ready, NC)
                    link = Steps(dve, step)
                    link(dve.tensor_reduce(mx[:, :], lg[:, :, :], AX_X, ALU.max))
                    dve.tensor_tensor(lg[:, :, :], lg[:, :, :], inside(mx[:, :], E), ALU.subtract).then_inc(shifted, 1)
                    dve.wait_ge(expd, 1)
                    link(dve.tensor_reduce(mx[:, :], lg[:, :, :], AX_X, ALU.add))
                    link(dve.reciprocal(mx[:, :], mx[:, :]))
                    link(dve.tensor_tensor(lg[:, :, :], lg[:, :, :], inside(mx[:, :], E), ALU.mult))
                    link(dve.tensor_copy(wt[:, :, :], lg[:, :, :]))
                    for m, one in ((m1, hot), (m2, hot2)):
                        link(dve.tensor_reduce(m[:, :], wt[:, :, :], AX_X, ALU.max))
                        link(dve.tensor_tensor(sc[:, :, :], wt[:, :, :], inside(m[:, :], E), ALU.is_ge))
                        link(dve.tensor_tensor(sc[:, :, :], sc[:, :, :], halves(cm("rank8"), T), ALU.mult))
                        link(dve.tensor_reduce(mx[:, :], sc[:, :, :], AX_X, ALU.max))
                        link(dve.tensor_tensor(one[:, :, :], sc[:, :, :], inside(mx[:, :], E), ALU.is_equal))
                        if m is m1:
                            link(dve.scalar_tensor_tensor(wt[:, :, :], one[:, :, :], -2.0, wt[:, :, :],
                                                          ALU.mult, ALU.add))
                    link(dve.tensor_tensor(mx[:, :], m1[:, :], m2[:, :], ALU.add))
                    link(dve.reciprocal(mx[:, :], mx[:, :]))
                    link(dve.tensor_tensor(hot[:, :, :], hot[:, :, :], hot2[:, :, :], ALU.add))
                    link(dve.tensor_tensor(wt[:, :, :], hot[:, :, :], lg[:, :, :], ALU.mult))
                    link(dve.tensor_tensor(wt[:, :, :], wt[:, :, :], inside(mx[:, :], E), ALU.mult))
        with ExitStack() as inner:
            p2 = Place(nc, inner)
            uf = [p2.sb(f"guf{s}", [P, CH]) for s in range(2)]
            xf = [p2.sb(f"gxf{s}", [P, CH]) for s in range(2)]
            w1 = [p2.sb(f"gw{s}", [P, J, E]) for s in range(2)]
            wts = [p2.sb(f"gwt{s}", [E, CH]) for s in range(2)]
            xr = [p2.sb(f"gxr{s}", [P, J, P]) for s in range(2)]
            o = [p2.sb(f"go{s}", [P, J, P]) for s in range(2)]
            ps_e = [p2.ps(f"ps_e{s}", [P, 2, CH]) for s in range(2)]
            ps_w = p2.ps("ps_w", [E, CH])
            ps_r = [p2.ps(f"ps_r{s}", [P, J, P]) for s in range(2)]
            fixed = p2.sem("g_fixed")
            w_mul = p2.sem("gw_mul")
            w_copied = p2.sem("gw_copied")
            r_mul = p2.sem("gr_mul")
            r_copied = p2.sem("gr_copied")
            e_mul = p2.sem("ge_mul")
            e_used = p2.sem("ge_used")
            step = p2.sem("g_step")
            o_stored = [p2.sem(f"go_stored{s}") for s in range(2)]
            o_ready = p2.sem("go_ready")
            with nc.Block() as block:
                @block.tensor
                def _(pe):
                    pe.sem_inc(e_used, FREE)
                    pe.sem_inc(w_copied, LAST)
                    with pe.Fori(0, NC // 2) as i:
                        for s in range(2):
                            t = 2 * i + s
                            pe.wait_ge(fixed, 3 * t + 3)
                            pe.wait_ge(w_copied, t + 1)
                            for j in range(J):
                                mm = pe.transpose(ps_w[:, j * P:(j + 1) * P], w1[s][:, j, :], cm("ident"))
                            mm.then_inc(w_mul, 1)
                            pe.wait_ge(w_copied, t + (1 + LAST))
                            for j in range(J):
                                some = slice(j * P, (j + 1) * P)
                                pe.matmul(ps_r[s][:, j, :], xf[s][:, some], cm("ident"), start=True, stop=False)
                                mm = pe.matmul(ps_r[s][:, j, :], wts[s][:, some], wf("expert_b", 0, P)[0:E, :],
                                               start=False, stop=True)
                            mm.then_inc(r_mul, 1)
                            for j in range(J):
                                pe.wait_ge(e_used, t * J + (j + 1))
                                for h in range(2):
                                    mm = pe.matmul(ps_e[j % 2][:, h, :], uf[s][:, j * P:(j + 1) * P],
                                                   wf("expert_w", h * CH, CH), start=True, stop=True)
                                mm.then_inc(e_mul, 1)

                @block.scalar
                def _(act):
                    act.sem_inc(e_mul, FREE * J)
                    act.sem_inc(r_mul, FREE)
                    with act.Fori(0, NC // 2) as i:
                        for s in range(2):
                            t = 2 * i + s
                            act.wait_ge(e_mul, t * J + J)
                            act.wait_ge(r_mul, t + 1)
                            act.activation(uf[s][:, :], u[:, bass.ds(t * CH, CH)], ACT.Copy).then_inc(fixed, 1)
                            act.activation(xf[s][:, :], xt[:, bass.ds(t * CH, CH)], ACT.Copy).then_inc(fixed, 1)
                            act.wait_ge(o_ready, t + 1)
                            act.activation(w1[s][:, :, :], wt[:, bass.ds(t * J, J), :], ACT.Copy).then_inc(fixed, 1)
                            act.wait_ge(w_mul, t + 1)
                            act.activation(wts[s][:, :], ps_w[:, :], ACT.Copy).then_inc(w_copied, 1)
                            act.wait_ge(r_mul, t + (1 + FREE))
                            act.activation(xr[s][:, :, :], ps_r[s][:, :, :], ACT.Copy).then_inc(r_copied, 1)

                @block.vector
                def _(dve):
                    dve.sem_inc(o_ready, FREE)
                    for s in range(2):
                        dve.sem_inc(o_stored[s], 16)
                    with dve.Fori(0, NC // 2) as i:
                        for s in range(2):
                            t = 2 * i + s
                            dve.wait_ge(r_copied, t + 1)
                            dve.wait_ge(o_stored[s], i * 16 + 16)
                            for j in range(J):
                                dve.wait_ge(e_mul, t * J + (j + 1 + FREE * J))
                                link = Steps(dve, step, (t * J + j) * (E - 1))
                                for e in range(E):
                                    ins = dve.scalar_tensor_tensor(
                                        o[s][:, j, :], ps_e[j % 2][:, e // 4, (e % 4) * P:(e % 4 + 1) * P],
                                                    w1[s][:, j, e:e + 1], xr[s][:, j, :] if e == 0 else o[s][:, j, :],
                                        ALU.mult, ALU.add)
                                    if e < E - 1:
                                        link(ins)
                                ins.then_inc(e_used, 1)
                            dve.wait_ge(e_used, t * J + (J + FREE))
                            dve.sem_inc(o_ready, 1)

                @block.sync
                def _(sp):
                    with sp.Fori(0, NC // 2) as i:
                        for s in range(2):
                            t = 2 * i + s
                            sp.wait_ge(o_ready, t + (1 + FREE))
                            sp.dma_start(out[bass.ds(t * CH, CH), :].rearrange("(j p) c -> p j c", p=P),
                                         o[s][:, :, :]).then_inc(o_stored[s], 16)
                    for s in range(2):
                        sp.wait_ge(o_stored[s], 16 * (NC // 2) + 16)


def pack(parts):
    import numpy as np
    at, n = {}, 0
    for name, a in parts:
        at[name] = (n, a.shape[1])
        n += a.shape[1]
    return np.ascontiguousarray(np.concatenate([a for _, a in parts], axis=1)), at


def getter(tensor, at):
    def get(name, i=None, n=1):
        o, w = at[name]
        return tensor[:, o:o + w] if i is None else tensor[:, o + i:o + i + n]
    return get


def constants():
    import numpy as np
    f = np.float32
    i = np.arange(P)
    parts = [
        ("ident", np.eye(P, dtype=f)),
        ("gmat", ((i[:, None] // 4) == (i[None, :] // 4)).astype(f) / 4),
        ("ones128", np.full((P, P), 1 / 128, f)),
        ("ones256", np.full((P, P), 1 / 256, f)),
        ("heads", ((i[:, None] // 32) == (i[None, :] // 32)).astype(f)),
        ("later", (i[None, :] > i[:, None]).astype(f)),
        ("row8", ((i[:, None] % 8) == np.arange(8)[None, :]).astype(f)),
        ("rank8", np.broadcast_to(8 - np.arange(8, dtype=f), (P, 8))),
        ("eps", np.full((P, 1), 1e-5, f)),
        ("ones", np.ones((P, P), f)),
    ]
    return pack(parts)


def columns(**arrays):
    return list(arrays.items())


def layouts(a):
    import numpy as np

    def per_half(v):
        v = v.reshape(2, P, -1)
        return np.concatenate([v[0], v[1]], axis=1)

    def every(v):
        return np.broadcast_to(v.reshape(1, -1), (P, v.size))

    x_cm = np.ascontiguousarray(a["x"].reshape(N, P).T)
    xp = a["L0_conv_x_proj_w"]
    bc, dt = xp[:, 8:40], xp[:, 0:8]
    xproj = np.concatenate([bc, bc, bc, dt], axis=1)
    xproj = xproj.reshape(KD, 104, 2, P).transpose(3, 0, 2, 1)
    dtw = a["L0_conv_dt_w"].transpose(2, 0, 1).reshape(8, KD * 256)
    wa, wa_at = pack(columns(
        win=a["L0_conv_w_in"].T,
        conv_w=per_half(a["L0_conv_conv_w"].reshape(256, 9)),
        conv_b=per_half(a["L0_conv_conv_b"]),
        dt_b=a["L0_conv_dt_b"].reshape(KD * 2, P).T,
        a_log=a["L0_conv_A_logs"].reshape(KD * 2, P, NS).transpose(1, 0, 2).reshape(P, KD * 2 * NS),
        d_skip=a["L0_conv_Ds"].reshape(KD * 2, P).T,
        ln_w=per_half(a["L0_conv_ln_w"]), ln_b=per_half(a["L0_conv_ln_b"]),
        wout=per_half(a["L0_conv_w_out"].T),
    ))
    wb, wb_at = pack(columns(
        w_exp=a["L1_conv_W_exp"].T, b_exp=a["L1_conv_b_exp"].reshape(2, P).T,
        w_con=a["L1_conv_W_con"].T, b_con=a["L1_conv_b_con"].reshape(1, P).T,
    ))
    qkv = a["L2_attn_W_qkv"].T
    col = lambda v: v.reshape(1, P).T
    wc, wc_at = pack(columns(
        w_q=qkv[:, 0:P], w_k=qkv[:, P:2 * P], w_v=qkv[:, 2 * P:3 * P], w_o=a["L2_attn_W_out"].T,
        b_out=col(a["L2_attn_b_out"]), gn_w=col(a["L2_attn_gn_w"]), gn_b=col(a["L2_attn_gn_b"]),
    ))
    wd, wd_at = pack(columns(
        sigma=every(a["L2_ffn_sigma"]), logw=every(a["L2_ffn_log_weights"]), gumbel=every(a["L2_ffn_gumbel"]),
    ))
    w1, eight = a["L3_attn_W1"], 8
    we, we_at = pack(columns(
        w1f=np.repeat(w1[:P], eight, axis=1), w1g=np.repeat(w1[P:], eight, axis=1),
        b1=np.repeat(a["L3_attn_b1"], eight)[:, None], w2=np.repeat(a["L3_attn_w2"][:, 0], eight)[:, None],
        b2=every(a["L3_attn_b2"]),
    ))
    wf, wf_at = pack(columns(
        router=a["L3_ffn_router_w"], router_b=every(a["L3_ffn_router_b"]),
        expert_w=a["L3_ffn_expert_w"].transpose(1, 0, 2).reshape(P, 8 * P),
        expert_b=np.concatenate([a["L3_ffn_expert_b"], np.zeros((P - 8, P), np.float32)]),
    ))
    phi = np.zeros((16, 2, L // 2 + 2 * P + 4), np.float32)
    phi[:, :, 2 * P + 1:-3] = a["L2_ffn_phi"].reshape(L // 2, 2, 16).transpose(2, 1, 0)
    more = {"wc": wc, "wd": wd, "we": we, "wf": wf, "phi": phi.reshape(P, -1),
            "m_u": a["L2_ffn_M_u"].transpose(2, 0, 1, 3).reshape(P, -1),
            "m_plus": a["L2_ffn_M_phi_plus"].transpose(2, 0, 1, 3).reshape(P, -1),
            "m_minus": a["L2_ffn_M_phi_minus"].transpose(2, 0, 1, 3).reshape(P, -1)}
    sel = np.zeros((96, 32, P), np.float32)
    for n in range(32):
        sel[n::32, n, :] = 1
    cmn, cmn_at = constants()
    arrays = {"x_cm": x_cm, "common": cmn, "wa": wa, "wb": wb,
              "xproj": np.ascontiguousarray(xproj.reshape(P, -1)), "dtw": np.ascontiguousarray(dtw),
              "sel": sel.reshape(96, -1)}
    arrays.update({n: np.ascontiguousarray(v) for n, v in more.items()})
    return arrays, {"common": cmn_at, "wa": wa_at, "wb": wb_at, "wc": wc_at, "wd": wd_at, "we": we_at, "wf": wf_at}


def load(nc, pairs, name):
    with ExitStack() as ctx:
        p = Place(nc, ctx)
        loaded = p.sem(name + "_loaded")
        with nc.Block() as block:
            @block.sync
            def _(sp):
                for tile, array in pairs:
                    sp.dma_start(tile, array).then_inc(loaded, 16)
                sp.wait_ge(loaded, 16 * len(pairs))


def scan_layer(nc, cm, d, at, gscale, gshift, y):
    with ExitStack() as ctx:
        p = Place(nc, ctx)
        wat = p.sb("wa_sb", list(d["wa"].shape))
        wa = getter(wat, at["wa"])
        load(nc, [(wat[:, :], d["wa"])], "wa")
        with ExitStack() as inner:
            p2 = Place(nc, inner)
            xc = p2.sb("xc", [P, 2, B, HH, WW])
            xt = y[:, 0].rearrange("p b h w -> p (b h w)")
            wide_sel = y[0:96, 1, 0].rearrange("p h w -> p (h w)")
            load_residual(nc, xt, d["x_cm"], "l0")
            group_stats(nc, xt, cm, gscale, gshift, "gn0")
            conv_branch(nc, xt, cm, wa, gscale, gshift, xc)
            sel = p2.sb("sel_sb", [96, 2 * NS, P], BF16)
            xproj = p2.sb("xproj_sb", [P, KD, 2, 104])
            dtw = p2.sb("dtw_sb", [P, KD, 2 * P])
            sel_cast = p2.sem("sel_cast")
            load(nc, [(wide_sel, d["sel"]), (xproj[:, :, :, :].rearrange("p k f r -> p (k f r)"), d["xproj"]),
                      (dtw[96:104, :, :].rearrange("p k c -> p (k c)"), d["dtw"])], "scan_w")
            with nc.Block() as block:
                @block.vector
                def _(dve):
                    dve.tensor_copy(sel[:, :, :].rearrange("p n m -> p (n m)"), wide_sel).then_inc(sel_cast, 1)
            selective_scan(nc, cm, wa, sel, xproj, dtw, xc, y)
        z = p.sb("z", [P, 2, N])
        xt = p.sb("xt0", [P, N])
        load_residual(nc, xt, d["x_cm"], "l0b")
        gated_output(nc, xt, cm, wa, gscale, gshift, y, z)


def build(nc, d, at, out):
    with ExitStack() as top:
        p = Place(nc, top)
        cmt = p.sb("common_sb", list(d["common"].shape))
        cm = getter(cmt, at["common"])
        gscale = p.sb("gscale", [P, B])
        gshift = p.sb("gshift", [P, B])
        load(nc, [(cmt[:, :], d["common"])], "common")
        both = p.sb("both", [P, 2, B, HH, WW])
        xt, u = (both[:, half].rearrange("p b h w -> p (b h w)") for half in range(2))
        scan_layer(nc, cm, d, at, gscale, gshift, both)
        def weights(place, names):
            tiles = {name: place.sb(name + "_sb", list(d[name].shape)) for name in names}
            load(nc, [(tile[:, :], d[name]) for name, tile in tiles.items()], "_".join(names))
            return {name: getter(tile, at[name]) for name, tile in tiles.items()}

        with ExitStack() as stage:
            w = weights(Place(nc, stage), ("wb", "wc"))
            group_stats(nc, xt, cm, gscale, gshift, "gn1")
            ema_gate(nc, xt, cm, w["wb"], gscale, gshift)
            layer_norm(nc, xt, cm, u, "n2a")
            linear_attention(nc, xt, cm, w["wc"], u)
        with ExitStack() as stage:
            w = weights(Place(nc, stage), ("wd",))
            layer_norm(nc, xt, cm, u, "n2f")
            spectral_ffn(nc, xt, cm, w["wd"], d, u)
        with ExitStack() as stage:
            w = weights(Place(nc, stage), ("we", "wf"))
            layer_norm(nc, xt, cm, u, "n3a")
            additive_attention(nc, xt, cm, w["we"], u)
            layer_norm(nc, xt, cm, u, "n3f")
            expert_ffn(nc, xt, cm, w["wf"], u, out)


def kernel(**inputs):
    import numpy as np
    import concourse.bacc as bacc
    from concourse.bass_utils import run_bass_kernel_spmd

    arrays, at = layouts({name: np.asarray(v) for name, v in inputs.items()})
    nc = bacc.Bacc("TRN2", target_bir_lowering=False, num_devices=1)
    d = {name: nc.dram_tensor(f"in_{name}_dram", v.shape, mybir.dt.from_np(v.dtype), kind="ExternalInput").ap()
         for name, v in arrays.items()}
    out = nc.dram_tensor("out_0_dram", [N, P], F32, kind="ExternalOutput").ap()
    build(nc, d, at, out)
    r = run_bass_kernel_spmd(nc, [{f"in_{name}_dram": v for name, v in arrays.items()}], core_ids=[0])
    return r.results[0]["out_0_dram"].reshape(B, HH, WW, P)
```
